# Optimizing a Trainium2 kernel written in Bass

```python
import numpy as np
import jax
import jax.numpy as jnp

def _softmax(x, axis=-1):
    return jax.nn.softmax(x, axis=axis)

def _gelu(x):
    return jax.nn.gelu(x, approximate=True)

def _silu(x):
    return jax.nn.silu(x)

def _sigmoid(x):
    return jax.nn.sigmoid(x)

def _layernorm(x, axis=-1, eps=1e-05):
    m = jnp.mean(x, axis=axis, keepdims=True)
    v = jnp.var(x, axis=axis, keepdims=True)
    return (x - m) / jnp.sqrt(v + eps)

def _scatter_add(tgt, idx, src, axis=0):
    return tgt.at[idx].add(src)

def _segment_sum(src, seg, n):
    return jax.ops.segment_sum(src, seg, n)
kernel_name = 'mk_metaformer_d1_conv_nchw256_r4_a9059a'

def setup_inputs(seed: int=0):
    np.random.seed(seed)
    _w = jnp.asarray

    def _rec_inputs():
        import jax
        import jax.numpy as jnp
        _gk = jax.random.key(seed)
        x = -0.5108 + 73.9 * jax.random.normal(jax.random.fold_in(_gk, 1), (32, 64, 16, 16), jnp.float32)
        return x
    x = _rec_inputs()

    def _L0_conv_setup():
        import jax, jax.numpy as jnp
        import numpy as np
        INT32_MIN = -2147483648.0
        INT32_MAX = 2147483647.0

        def _ste_trunc(x):
            return x + jax.lax.stop_gradient(jnp.trunc(x) - x)

        def _ste_wrap16(x):
            return x + jax.lax.stop_gradient((x + 32768.0) % 65536.0 - 32768.0 - x)
        key = jax.random.key(seed)
        k1, k2, k3, k4, k5 = jax.random.split(key, 5)
        B, C, H, W = (32, 64, 16, 16)
        x = jax.random.randint(k1, (B, C, H, W), -32, 32).astype(jnp.float32)
        weight = jax.random.randint(k2, (C, 1, 3, 3), -127, 32).astype(jnp.float32)
        bias = jax.random.randint(k3, (C,), -8192, 8192).astype(jnp.float32)
        scl_in = jax.random.randint(k4, (C,), 1, 15000).astype(jnp.float32)
        srarh_shift = jax.random.randint(k5, (C,), 0, 16).astype(jnp.float32)
        return {'x': x, 'weight': weight, 'bias': bias, 'scl_in': scl_in, 'srarh_shift': srarh_shift, 'zp': 32, 'upper': 255, 'pad_fill': 0.0}
    _L0_conv_all = _L0_conv_setup()
    _L0_conv_in = {k: v for k, v in _L0_conv_all.items() if k in ('weight', 'bias', 'scl_in', 'srarh_shift', 'pad_fill')}
    del _L0_conv_all

    def _L0_ffn_setup():
        import jax, jax.numpy as jnp
        import numpy as np
        B, N, D = (16, 1024, 64)
        NUM_EXPERTS, TOP_K, HEADS = (4, 2, 4)
        N_EDGES = 262144
        LN_EPS = 1e-05

        def _layernorm(x, g, b):
            mu = x.mean(-1, keepdims=True)
            var = ((x - mu) ** 2).mean(-1, keepdims=True)
            return (x - mu) * jax.lax.rsqrt(var + LN_EPS) * g + b

        def _forward(x, edge_index, W_gat, att_src, att_dst, b_gat, ln_gamma, ln_beta, W1, b1, W2, b2):
            Bc, Nc, Dc = x.shape
            M = Bc * Nc
            x_flat = x.reshape(M, Dc)
            h = (x_flat @ W_gat).reshape(M, HEADS, NUM_EXPERTS)
            loops = jnp.arange(M, dtype=edge_index.dtype)
            src = jnp.concatenate([edge_index[0], loops])
            dst = jnp.concatenate([edge_index[1], loops])
            a_src = (h * att_src).sum(-1)
            a_dst = (h * att_dst).sum(-1)
            e = jax.nn.leaky_relu(a_src[src] + a_dst[dst], negative_slope=0.2)
            e_max = jax.ops.segment_max(e, dst, num_segments=M)
            ee = jnp.exp(e - e_max[dst])
            denom = jax.ops.segment_sum(ee, dst, num_segments=M)
            alpha = ee / (denom[dst] + 1e-16)
            msg = h[src] * alpha[:, :, None]
            agg = jax.ops.segment_sum(msg, dst, num_segments=M).reshape(M, HEADS * NUM_EXPERTS) + b_gat
            scores = _layernorm(agg, ln_gamma, ln_beta).reshape(M, HEADS, NUM_EXPERTS).mean(1)
            scores = scores.reshape(Bc, Nc, NUM_EXPERTS)
            topk_s, topk_i = jax.lax.top_k(scores, TOP_K)
            w = jax.nn.softmax(topk_s, axis=-1)
            out = jnp.zeros_like(x)
            for ei in range(NUM_EXPERTS):
                g = jnp.where(topk_i == ei, w, 0.0).sum(-1)
                hh = jax.nn.gelu(x @ W1[ei] + b1[ei], approximate=False)
                out = out + g[..., None] * (hh @ W2[ei] + b2[ei])
            return out
        key = jax.random.key(seed)
        ks = jax.random.split(key, 8)
        s = 0.05
        return {'x': jax.random.normal(ks[0], (B, N, D), jnp.float32), 'W_gat': jax.random.normal(ks[1], (D, HEADS * NUM_EXPERTS), jnp.float32) * s, 'att_src': jax.random.normal(ks[2], (HEADS, NUM_EXPERTS), jnp.float32) * s, 'att_dst': jax.random.normal(ks[3], (HEADS, NUM_EXPERTS), jnp.float32) * s, 'b_gat': jnp.zeros((HEADS * NUM_EXPERTS,), jnp.float32), 'ln_gamma': jnp.ones((HEADS * NUM_EXPERTS,), jnp.float32), 'ln_beta': jnp.zeros((HEADS * NUM_EXPERTS,), jnp.float32), 'W1': jax.random.normal(ks[4], (NUM_EXPERTS, D, 2 * D), jnp.float32) * s, 'b1': jnp.zeros((NUM_EXPERTS, 2 * D), jnp.float32), 'W2': jax.random.normal(ks[5], (NUM_EXPERTS, 2 * D, D), jnp.float32) * s, 'b2': jnp.zeros((NUM_EXPERTS, D), jnp.float32), 'edge_index': jax.random.randint(ks[6], (2, N_EDGES), 0, B * N, jnp.int32)}
    _L0_ffn_all = _L0_ffn_setup()
    _L0_ffn_in = {k: v for k, v in _L0_ffn_all.items() if k in ('W_gat', 'att_src', 'att_dst', 'b_gat', 'ln_gamma', 'ln_beta', 'W1', 'b1', 'W2', 'b2', 'edge_index')}
    del _L0_ffn_all
    return {'x': x, 'L0_conv_weight': _L0_conv_in['weight'], 'L0_conv_bias': _L0_conv_in['bias'], 'L0_conv_scl_in': _L0_conv_in['scl_in'], 'L0_conv_srarh_shift': _L0_conv_in['srarh_shift'], 'L0_conv_pad_fill': _L0_conv_in['pad_fill'], 'L0_ffn_W_gat': _L0_ffn_in['W_gat'], 'L0_ffn_att_src': _L0_ffn_in['att_src'], 'L0_ffn_att_dst': _L0_ffn_in['att_dst'], 'L0_ffn_b_gat': _L0_ffn_in['b_gat'], 'L0_ffn_ln_gamma': _L0_ffn_in['ln_gamma'], 'L0_ffn_ln_beta': _L0_ffn_in['ln_beta'], 'L0_ffn_W1': _L0_ffn_in['W1'], 'L0_ffn_b1': _L0_ffn_in['b1'], 'L0_ffn_W2': _L0_ffn_in['W2'], 'L0_ffn_b2': _L0_ffn_in['b2'], 'L0_ffn_edge_index': _L0_ffn_in['edge_index']}

def reference(x, L0_conv_weight, L0_conv_bias, L0_conv_scl_in, L0_conv_srarh_shift, L0_conv_pad_fill, L0_ffn_W_gat, L0_ffn_att_src, L0_ffn_att_dst, L0_ffn_b_gat, L0_ffn_ln_gamma, L0_ffn_ln_beta, L0_ffn_W1, L0_ffn_b1, L0_ffn_W2, L0_ffn_b2, L0_ffn_edge_index):
    import jax
    import jax.numpy as jnp

    def _L0_conv_ref(x, weight, bias, scl_in, srarh_shift, zp, upper, pad_fill):
        import jax, jax.numpy as jnp
        import numpy as np
        INT32_MIN = -2147483648.0
        INT32_MAX = 2147483647.0

        def _ste_trunc(x):
            return x + jax.lax.stop_gradient(jnp.trunc(x) - x)

        def _ste_wrap16(x):
            return x + jax.lax.stop_gradient((x + 32768.0) % 65536.0 - 32768.0 - x)
        C = weight.shape[0]
        xp = jnp.pad(x, ((0, 0), (0, 0), (1, 1), (1, 1)), constant_values=pad_fill)
        acc = jax.lax.conv_general_dilated(xp, weight, window_strides=(1, 1), padding='VALID', dimension_numbers=('NCHW', 'OIHW', 'NCHW'), feature_group_count=C)
        acc = acc + bias[None, :, None, None]
        acc = _ste_wrap16(acc)
        prod = acc * scl_in[None, :, None, None]
        shifted = jnp.clip(prod * 2.0, INT32_MIN, INT32_MAX)
        mq = _ste_trunc(shifted / 65536.0)
        sh = srarh_shift[None, :, None, None]
        half = jnp.where(sh > 0, 2.0 ** (sh - 1.0), 0.0)
        rounded = _ste_trunc((mq + half) / 2.0 ** sh)
        return jnp.clip(rounded, 0.0, float(upper)) - zp

    def _L0_ffn_ref(x, W_gat, att_src, att_dst, b_gat, ln_gamma, ln_beta, W1, b1, W2, b2, edge_index):
        import jax, jax.numpy as jnp
        import numpy as np
        B, N, D = (16, 1024, 64)
        NUM_EXPERTS, TOP_K, HEADS = (4, 2, 4)
        N_EDGES = 262144
        LN_EPS = 1e-05

        def _layernorm(x, g, b):
            mu = x.mean(-1, keepdims=True)
            var = ((x - mu) ** 2).mean(-1, keepdims=True)
            return (x - mu) * jax.lax.rsqrt(var + LN_EPS) * g + b

        def _forward(x, edge_index, W_gat, att_src, att_dst, b_gat, ln_gamma, ln_beta, W1, b1, W2, b2):
            Bc, Nc, Dc = x.shape
            M = Bc * Nc
            x_flat = x.reshape(M, Dc)
            h = (x_flat @ W_gat).reshape(M, HEADS, NUM_EXPERTS)
            loops = jnp.arange(M, dtype=edge_index.dtype)
            src = jnp.concatenate([edge_index[0], loops])
            dst = jnp.concatenate([edge_index[1], loops])
            a_src = (h * att_src).sum(-1)
            a_dst = (h * att_dst).sum(-1)
            e = jax.nn.leaky_relu(a_src[src] + a_dst[dst], negative_slope=0.2)
            e_max = jax.ops.segment_max(e, dst, num_segments=M)
            ee = jnp.exp(e - e_max[dst])
            denom = jax.ops.segment_sum(ee, dst, num_segments=M)
            alpha = ee / (denom[dst] + 1e-16)
            msg = h[src] * alpha[:, :, None]
            agg = jax.ops.segment_sum(msg, dst, num_segments=M).reshape(M, HEADS * NUM_EXPERTS) + b_gat
            scores = _layernorm(agg, ln_gamma, ln_beta).reshape(M, HEADS, NUM_EXPERTS).mean(1)
            scores = scores.reshape(Bc, Nc, NUM_EXPERTS)
            topk_s, topk_i = jax.lax.top_k(scores, TOP_K)
            w = jax.nn.softmax(topk_s, axis=-1)
            out = jnp.zeros_like(x)
            for ei in range(NUM_EXPERTS):
                g = jnp.where(topk_i == ei, w, 0.0).sum(-1)
                hh = jax.nn.gelu(x @ W1[ei] + b1[ei], approximate=False)
                out = out + g[..., None] * (hh @ W2[ei] + b2[ei])
            return out
        return _forward(x, edge_index, W_gat, att_src, att_dst, b_gat, ln_gamma, ln_beta, W1, b1, W2, b2)

    def _gn(v, G=32, eps=1e-05):
        B_, C_, H_, W_ = v.shape
        g = v.reshape(B_, G, C_ // G, H_, W_)
        m = jnp.mean(g, axis=(2, 3, 4), keepdims=True)
        s = jnp.var(g, axis=(2, 3, 4), keepdims=True)
        return ((g - m) / jnp.sqrt(s + eps)).reshape(v.shape)

    def _ln_c(v, eps=1e-06):
        m = jnp.mean(v, axis=1, keepdims=True)
        s = jnp.var(v, axis=1, keepdims=True)
        return (v - m) / jnp.sqrt(s + eps)

    def _ln_t(v, eps=1e-05):
        m = jnp.mean(v, axis=-1, keepdims=True)
        s = jnp.var(v, axis=-1, keepdims=True)
        return (v - m) / jnp.sqrt(s + eps)

    def _to_tokens(v):
        B_, C_, H_, W_ = v.shape
        return v.reshape(B_, C_, H_ * W_).transpose(0, 2, 1)

    def _from_tokens(t, like):
        B_, C_, H_, W_ = like.shape
        return t.transpose(0, 2, 1).reshape(B_, C_, H_, W_)
    x = x + _L0_conv_ref(_ln_c(x), L0_conv_weight, L0_conv_bias, L0_conv_scl_in, L0_conv_srarh_shift, 32, 255, L0_conv_pad_fill)
    t = _to_tokens(x)
    t = t + _L0_ffn_ref(_ln_t(t), L0_ffn_W_gat, L0_ffn_att_src, L0_ffn_att_dst, L0_ffn_b_gat, L0_ffn_ln_gamma, L0_ffn_ln_beta, L0_ffn_W1, L0_ffn_b1, L0_ffn_W2, L0_ffn_b2, L0_ffn_edge_index)
    x = _from_tokens(t, x)
    return x

_drawn_inputs = setup_inputs


def setup_inputs(seed=0):
    import zlib

    import numpy as np

    out = dict(_drawn_inputs(seed))
    spreads = {'L0_ffn_b_gat': (0.0, 2.0),
     'L0_ffn_ln_gamma': (1.0, 0.6),
     'L0_ffn_ln_beta': (0.0, 0.8),
     'L0_ffn_b1': (0.0, 2.0),
     'L0_ffn_b2': (0.0, 2.0)}
    factors = {'L0_ffn_W_gat': 8.0,
     'L0_ffn_att_src': 8.0,
     'L0_ffn_att_dst': 8.0,
     'L0_ffn_W1': 8.0,
     'L0_ffn_W2': 8.0}
    for name, (base, spread) in spreads.items():
        noise = np.random.default_rng([zlib.crc32(name.encode()), seed]).standard_normal(out[name].shape)
        drawn = base * np.exp(spread * noise) if base else spread * noise
        out[name] = jnp.asarray(drawn.astype(out[name].dtype))
    for name, factor in factors.items():
        out[name] = (out[name] * factor).astype(out[name].dtype)
    return out
```

```python
import concourse.bass as bass
from concourse import mybir
from contextlib import ExitStack

F32 = mybir.dt.float32
I32 = mybir.dt.int32
ALU = mybir.AluOpType
ACT = mybir.ActivationFunctionType
AX = mybir.AxisListType

P = 128
B, C, S = 32, 64, 256
SIDE = 16
NODES = B * S
EDGES = 262144
COLS = EDGES // P
TILES = NODES // P
HALF = B // 2
TOK = HALF * S
CH = 512
NCH = TOK // CH
PAIRS = TOK // P
HEADS, EXP = 4, 4
HE = HEADS * EXP
HID = 2 * C
SRC_BITS = 13
KEY_ONE = 0x20000000
ROW = HE + HEADS
ST = HEADS + HEADS + HE
TC = 64
NCHUNK = COLS // TC
SAMPLE = 128
NSAMP = EDGES // SAMPLE
SROUND = 33
BIG = 1.0e30
MAGIC = 12582912.0
FAR = 1 << 20
LN1_EPS, LN2_EPS, LN3_EPS = 1e-6, 1e-5, 1e-5
SLOPE = 0.2
LOG_COLS = 11
LOG_EDGES = 18


def build(nc, A, out):
    ctx = ExitStack()
    with ctx:
        def sb(name, shape, dt=F32):
            return ctx.enter_context(nc.sbuf_tensor(name, shape, dt))

        def sem(name):
            return ctx.enter_context(nc.semaphore(name))

        def dram(name, shape, dt=F32):
            return nc.dram_tensor(name, shape, dt).ap()

        keys_d = dram("keys_d", [P, COLS], I32)
        samples_d = dram("samples_d", [P, COLS // SAMPLE], I32)
        rows_d = dram("rows_d", [NODES, ROW])
        adst_d = dram("adst_d", [NODES, HEADS])
        heads_d = dram("heads_d", [EDGES, HEADS])
        state_d = dram("state_d", [EDGES, ST])
        carry_d = dram("carry_d", [NODES, ST])

        x_sb = sb("x_sb", [P, TOK])
        ln2 = sb("ln2", [P, TOK])
        experts = sb("experts", [P, PAIRS, EXP, P])
        ex_flat = experts[:, :, :, :].rearrange("p a e c -> p (a e c)")
        centred = ex_flat[:, 0:TOK]
        std1 = ex_flat[:, TOK:2 * TOK]
        tmp = [ex_flat[:, 2 * TOK + n * CH:2 * TOK + (n + 1) * CH] for n in range(8)]
        square = tmp[0]
        rstd, qa, qb, qc, qd = tmp[1:6]
        centred2 = [tmp[6], tmp[7]]
        std2 = [ex_flat[:, 2 * TOK + (8 + n) * CH:2 * TOK + (9 + n) * CH] for n in range(2)]
        square2 = ex_flat[:, 2 * TOK + 10 * CH:2 * TOK + 11 * CH]
        SP_ = SIDE + 2
        pad0, padn = 2 * TOK + 11 * CH, 2 * SP_ * SP_
        padded = [ex_flat[:, pad0 + n * padn:pad0 + (n + 1) * padn]
                  .rearrange("p (b r c) -> p b r c", b=2, r=SP_) for n in range(2)]

        keys = [sb("keys0", [P, COLS]), sb("keys1", [P, COLS])]
        sources = sb("sources", [P, COLS + 2 * TC], I32)
        same = sb("same", [P, COLS])
        work = sb("work", [P, 4096])
        samples_b = work[:, 0:NSAMP]
        found = sb("found", [P, SROUND, SAMPLE])
        index = [sb("index0", [P, TC], I32), sb("index1", [P, TC], I32)]
        gathered = [sb("gath0", [P, TC, ROW]), sb("gath1", [P, TC, ROW])]
        state = [sb("state0", [P, TC, ST]), sb("state1", [P, TC, ST])]
        headrow = [sb("headrow0", [P, TC, HEADS]), sb("headrow1", [P, TC, HEADS])]
        o = 0
        adst_e, top_e = [], []
        for n in range(2):
            adst_e.append(work[:, o:o + HEADS * TC].rearrange("p (h t) -> p h t", h=HEADS)); o += HEADS * TC
        for n in range(2):
            top_e.append(work[:, o:o + HEADS * (TC + 1)].rearrange("p (h t) -> p h t", h=HEADS)); o += HEADS * (TC + 1)
        fresh = work[:, o:o + TC]; o += TC
        raw = work[:, o:o + 2 * HEADS * TC].rearrange("p (a h t) -> p a h t", a=2, h=HEADS); o += 2 * HEADS * TC
        diff = work[:, o:o + 2 * HEADS * TC].rearrange("p (a h t) -> p a h t", a=2, h=HEADS); o += 2 * HEADS * TC
        weight = work[:, o:o + 2 * HEADS * TC].rearrange("p (a h t) -> p a h t", a=2, h=HEADS); o += 2 * HEADS * TC
        part = work[:, o:o + HE * TC].rearrange("p (h e t) -> p h e t", h=HEADS, e=EXP)
        assert o + HE * TC <= 4096

        table = sb("table", [P, TILES, ROW])
        adst = sb("adst", [P, TILES, HEADS])
        samples = sb("samples", [P, COLS // SAMPLE], I32)
        targets = sb("targets", [P, TILES + 1], I32)
        count = sb("count", [P, TILES + 1])
        block_f = sb("block_f", [P, TILES + 1])
        block_i = sb("block_i", [P, TILES + 1], I32)
        first = sb("first", [P, TILES + 1])
        empty = sb("empty", [P, TILES])
        scat_f = sb("scat_f", [P, 2, TILES])
        scat_i = sb("scat_i", [P, 2, TILES], I32)
        ends = sb("ends", [P, 4], I32)
        ends_i = sb("ends_i", [P, 4], I32)
        ends_f = sb("ends_f", [P, 4])
        flags = sb("flags", [P, 4])
        dfirst_i = sb("dfirst_i", [P, 1], I32)
        cidx_f = sb("cidx_f", [P, 1])
        cidx_i = sb("cidx_i", [P, 1], I32)
        dfirst = sb("dfirst", [P, HEADS])
        hidden = [state[0][:, :, :].rearrange("p t s -> p (t s)")[:, n * CH:(n + 1) * CH] for n in range(2)]

        ident = sb("ident", [P, P])
        blockmean = sb("blockmean", [P, P])
        centring = sb("centring", [P, P])
        taps = sb("taps", [P, 9, P])
        shift1 = sb("shift1", [P, P])
        shift2 = sb("shift2", [P, P])
        onesrow = sb("onesrow", [1, P])
        w3 = sb("w3", [P, 9])
        chan = sb("chan", [P, 3])
        half_s = sb("half_s", [P, 4])
        pow_i = sb("pow_i", [P, 2], I32)
        pad_i = sb("pad_i", [P, 2], I32)
        pad_t = sb("pad_t", [P, 6], I32)
        pad_f = sb("pad_f", [P, 2])
        signs_i = sb("signs_i", [P, 8], I32)
        signs = sb("signs", [P, 7])
        wgat = sb("wgat", [P, 2, HE])
        w1 = work[:, 3072:4096].rearrange("p (h e n) -> p h e n", h=2, e=EXP)
        b1 = sb("b1", [P, EXP])
        w2 = sb("w2", [P, EXP, C])
        b2 = sb("b2", [1, EXP * C])
        rowc = sb("rowc", [P, 5, HE])
        eps = sb("eps", [P, 3])

        psum = [ctx.enter_context(nc.psum_tensor(f"ps{n}", [P, 512], F32)) for n in range(8)]
        tr_ps = psum[0:4]
        ps_centre, ps_var, ps_conv, ps_h = psum[4:8]

        rn_flat = sources[:, 0:TILES * ST].bitcast(F32)
        last_rows = rn_flat.rearrange("p (t s) -> p t s", s=ST)
        carried = keys[0][:, 0:TILES * ST].rearrange("p (t s) -> p t s", s=ST)
        neutral = found[:, 0:12, :].rearrange("p a b -> p (a b)")
        zeros = same
        NH4 = TILES * HEADS
        nt = [keys[1][:, n * NH4:(n + 1) * NH4].rearrange("p (t h) -> p t h", h=HEADS) for n in range(8)]
        n16 = [ln2[:, n * TILES * HE:(n + 1) * TILES * HE].rearrange("p (t h e) -> p t h e", h=HEADS, e=EXP)
               for n in range(4)]
        gates = found[:, 0:2, :].rearrange("p a b -> p (a b)").rearrange("p (e a h) -> p e a h", e=EXP, a=PAIRS)
        nsm = [found[:, 2 + n:3 + n, 0:TILES].rearrange("p a b -> p (a b)") for n in range(12)]
        tri = found[:, 16:22, :].rearrange("p a b -> p (a b)").rearrange("p (a t h) -> p a t h", a=3, h=HEADS)
        tri2 = found[:, 22:28, :].rearrange("p a b -> p (a b)").rearrange("p (a t h) -> p a t h", a=3, h=HEADS)
        CHN = HEADS * (1 + EXP)
        cx = sb("cx", [P, 4, CHN])
        ct = found[0:CHN, 0:12, :]
        cback = sb("cback", [P, ST])

        names = ("edges_in x_in conv_in chan_in pad_in gat_in rows_in w1_in b1_in w2_in b2_in consts pool made "
                 "taps_made dve signs_ready keys_out keys_moved banks_moved ln1_centred ln1_squared ln1_var "
                 "ln1_std refill_begun padded_ready conv_done x1_ready ln2_centred ln2_squared ln2_var ln2_std ln2_ready h_done "
                 "h_used table_ready rows_out adst_out samples_ready samples_out keysort_out samples_in neigh_in sorted_ready "
                 "block_ready found0 found1 found_used dfirst_in places_ready first_ready ends_ps idx_ready "
                 "zeros_ready zeros_out heads_out neutral_ready neutral_out gath0 gath1 head_in0 head_in1 "
                 "diffs_ready weights_ready state_ready state_out0 state_out1 "
                 "carry_x carry_t carry_diff carry_w carry_c carry_b carry_row carry_out carry_in carry_idx last_in "
                 "hid_ps hid_ready ex_ps ex_ready node_diff node_w node_var node_std top_ready top_exp "
                 "gated out_ps final out_done").split()
        s = {n: sem(n) for n in names}

        block = ctx.enter_context(nc.Block())

        LEVELS_T = list(range(LOG_COLS + 1, LOG_EDGES + 1))
        PASSES = 2 * len(LEVELS_T)
        MOVES, at = [], LOG_COLS * (LOG_COLS + 1) // 2 % 2
        for level in LEVELS_T:
            MOVES.append((at, 1 - at, None))
            at = (1 - at + level - LOG_COLS) % 2
            MOVES.append((at, 1 - at, level - LOG_COLS if level < LOG_EDGES else None))
            at = (1 - at + LOG_COLS) % 2
        SORTED = at

        @block.sync
        def _(sp):
            for n in range(2):
                sp.dma_start(keys[n][:, :].bitcast(I32), A["edge_index"][n].rearrange("(p t) -> p t", p=P)) \
                  .then_inc(s["edges_in"], 16)
            for h in range(2):
                sp.dma_start(x_sb[h * C:(h + 1) * C, :].rearrange("p (b s) -> p b s", b=HALF),
                             A["x"][h * HALF:(h + 1) * HALF].rearrange("b c i j -> c b (i j)")) \
                  .then_inc(s["x_in"], 16)
            for h in range(2):
                rows = slice(h * C, (h + 1) * C)
                sp.dma_start(w3[rows, :], A["weight"].rearrange("c a i j -> c (a i j)")).then_inc(s["conv_in"], 16)
                for n, name in enumerate(("bias", "scl_in", "srarh_shift")):
                    sp.dma_start(chan[rows, n:n + 1], A[name].rearrange("(c a) -> c a", a=1)).then_inc(s["chan_in"], 16)
            sp.dma_start(pad_i[:, :], A["pad"].bitcast(I32).rearrange("(a n) -> a n", a=1).broadcast_to([P, 2])) \
              .then_inc(s["pad_in"], 16)
            sp.wait_ge(s["consts"], 1)
            for h in range(2):
                rows = slice(h * C, (h + 1) * C)
                sp.dma_start(wgat[rows, h, :], A["W_gat"]).then_inc(s["gat_in"], 16)
                sp.dma_start(w1[rows, h, :, :], A["W1"].rearrange("e c n -> c e n")).then_inc(s["w1_in"], 16)
            for n, name in enumerate(("att_src", "att_dst")):
                sp.dma_start(rowc[:, n, :], A[name].rearrange("(a h) e -> a (h e)", a=1).broadcast_to([P, HE])) \
                  .then_inc(s["rows_in"], 16)
            for n, name in enumerate(("b_gat", "ln_gamma", "ln_beta")):
                sp.dma_start(rowc[:, 2 + n, :], A[name].rearrange("(a n) -> a n", a=1).broadcast_to([P, HE])) \
                  .then_inc(s["rows_in"], 16)
            with nc.allow_non_contiguous_dma(reason="small weights"):
                sp.dma_start(b1[:, :], A["b1"].rearrange("e n -> n e")).then_inc(s["b1_in"], 16)
            sp.dma_start(w2[:, :, :], A["W2"].rearrange("e n c -> n e c")).then_inc(s["w2_in"], 16)
            sp.dma_start(b2[:, :], A["b2"].rearrange("(a e) c -> a (e c)", a=1)).then_inc(s["b2_in"], 16)
            sp.wait_ge(s["zeros_ready"], 1)
            for h in range(HEADS):
                sp.dma_start(heads_d.rearrange("(p t) h -> p (t h)", p=P)[:, h * COLS:(h + 1) * COLS], zeros[:, :]) \
                  .then_inc(s["zeros_out"], 16)
            sp.wait_ge(s["neutral_ready"], 1)
            sp.dma_start(carry_d.rearrange("(p t) s -> p (t s)", p=P), neutral).then_inc(s["neutral_out"], 16)
            sp.wait_ge(s["table_ready"], 1)
            sp.dma_start(rows_d.rearrange("(t p) r -> p t r", p=P), table[:, :, :]).then_inc(s["rows_out"], 16)
            sp.dma_start(adst_d.rearrange("(t p) r -> p t r", p=P), adst[:, :, :]).then_inc(s["adst_out"], 16)
            sp.wait_ge(s["sorted_ready"], 1)
            sp.dma_start(keys_d, keys[SORTED][:, :].bitcast(I32)).then_inc(s["keysort_out"], 16)
            sp.wait_ge(s["samples_ready"], 1)
            sp.dma_start(samples_d, samples[:, :]).then_inc(s["samples_out"], 16)
            sp.wait_ge(s["samples_out"], 16)
            sp.dma_start(samples_b.bitcast(I32),
                         samples_d.rearrange("(a p) t -> a (p t)", a=1).broadcast_to([P, NSAMP])) \
              .then_inc(s["samples_in"], 16)
            sp.wait_ge(s["keysort_out"], 16)
            sp.dma_start(ends[1:P, 2:3], keys_d[0:P - 1, COLS - 1:COLS], allow_slow_non_contiguous=True).then_inc(s["neigh_in"], 16)
            sp.dma_start(ends[0:P - 1, 3:4], keys_d[1:P, 0:1], allow_slow_non_contiguous=True).then_inc(s["neigh_in"], 16)
            sp.wait_ge(s["heads_out"], 16 * TILES)
            heads_v = heads_d.rearrange("(p t) h -> p t h", p=P)
            state_v = state_d.rearrange("(p t) s -> p t s", p=P)
            for u in range(2):
                sp.dma_start(headrow[u][:, :, :], heads_v[:, u * TC:(u + 1) * TC, :]).then_inc(s[f"head_in{u}"], 16)
            with sp.Fori(0, NCHUNK // 2 - 1) as i:
                for u in range(2):
                    sp.wait_ge(s["state_ready"], i * 2 + (u + 1))
                    sp.dma_start(state_v[:, bass.ds(i * (2 * TC) + u * TC, TC), :], state[u][:, :, :]) \
                      .then_inc(s[f"state_out{u}"], 16)
                    sp.dma_start(headrow[u][:, :, :], heads_v[:, bass.ds(i * (2 * TC) + (u + 2) * TC, TC), :]) \
                      .then_inc(s[f"head_in{u}"], 16)
            for u in range(2):
                sp.wait_ge(s["state_ready"], NCHUNK - 2 + u + 1)
                sp.dma_start(state_v[:, COLS - (2 - u) * TC:COLS - (1 - u) * TC, :], state[u][:, :, :]) \
                  .then_inc(s[f"state_out{u}"], 16)
            sp.wait_ge(s["carry_out"], 16)
            sp.dma_start(carried, carry_d.rearrange("(t p) s -> p t s", p=P)).then_inc(s["carry_in"], 16)
            for c in range(NCH):
                sp.wait_ge(s["final"], c + 1)
                for h in range(2):
                    sp.dma_start(out[h * HALF + 2 * c:h * HALF + 2 * c + 2].rearrange("b c i j -> c b (i j)"),
                                 x_sb[h * C:(h + 1) * C, c * CH:(c + 1) * CH].rearrange("p (b s) -> p b s", b=2)) \
                      .then_inc(s["out_done"], 16)
            sp.wait_ge(s["out_done"], 16 * 2 * NCH)

        @block.gpsimd
        def _(pool):
            steps = [0]

            def settle(ins):
                steps[0] += 1
                ins.then_inc(s["pool"], 1)
                pool.wait_ge(s["pool"], steps[0])

            settle(pool.memset(wgat[:, :, :], 0.0))
            settle(pool.memset(w1, 0.0))
            settle(pool.iota(signs_i[:, 7:8], [[0, 1]], base=0, channel_multiplier=1))
            pool.iota(targets[:, :], [[P, TILES + 1]], base=0, channel_multiplier=1).then_inc(s["consts"], 1)
            pool.wait_ge(s["consts"], 1)
            for tile in (ident, shift1, shift2, blockmean):
                settle(pool.memset(tile[:, :], 0.0))
            settle(pool.memset(onesrow[:, :], 1.0))
            settle(pool.memset(blockmean[0:C, 0:C], 1.0 / C))
            settle(pool.memset(blockmean[C:P, C:P], 1.0 / C))
            settle(pool.memset(shift2[0:1, P - 1:P], 1.0))
            settle(pool.affine_select(out=ident[:, :], in_=ident[:, :], compare_op=ALU.not_equal, fill=1.0, base=0,
                                      pattern=[[-1, P]], channel_multiplier=1))
            settle(pool.affine_select(out=shift1[:, :], in_=shift1[:, :], compare_op=ALU.not_equal, fill=1.0, base=-1,
                                      pattern=[[-1, P]], channel_multiplier=1))
            pool.tensor_tensor(centring[:, :], ident[:, :], blockmean[:, :], ALU.subtract).then_inc(s["made"], 1)
            pool.wait_ge(s["conv_in"], 32)
            pool.wait_ge(s["made"], 1)
            for k in range(9):
                pool.tensor_scalar(taps[:, k, :], ident[:, :], w3[:, k:k + 1], None, ALU.mult).then_inc(s["taps_made"], 1)
                pool.wait_ge(s["taps_made"], k + 1)
            settle(pool.memset(neutral, 0.0))
            pool.memset(neutral.rearrange("p (t s) -> p t s", s=ST)[:, :, 0:HEADS], -BIG).then_inc(s["neutral_ready"], 1)
            pool.wait_ge(s["neutral_ready"], 1)

            node_bound, edge_bound, sample_bound = (pool.to_reg(n - 1) for n in (NODES, EDGES, NSAMP))

            def gather_rows(u):
                for t in range(TC):
                    pool.indirect_dma_start(out=gathered[u][:, t, :], out_offset=None, in_=rows_d,
                                            in_offset=bass.IndirectOffsetOnAxis(ap=index[u][:, t:t + 1], axis=0),
                                            bounds_check=node_bound, oob_is_err=False).then_inc(s[f"gath{u}"], 16)

            pool.wait_ge(s["rows_out"], 16)
            pool.wait_ge(s["adst_out"], 16)
            pool.wait_ge(s["idx_ready"], 1)
            pool.indirect_dma_start(out=dfirst[:, :], out_offset=None, in_=adst_d,
                                    in_offset=bass.IndirectOffsetOnAxis(ap=dfirst_i[:, :], axis=0),
                                    bounds_check=node_bound, oob_is_err=False).then_inc(s["dfirst_in"], 16)
            gather_rows(0)
            gather_rows(1)
            key_blocks = keys_d.rearrange("p (a b) -> (p a) b", b=SAMPLE)
            pool.wait_ge(s["keysort_out"], 16)
            pool.wait_ge(s["block_ready"], 1)
            pool.wait_ge(s["neutral_out"], 16)
            for t in range(TILES + 1):
                if t >= SROUND:
                    pool.wait_ge(s["found_used"], t - SROUND + 1)
                pool.indirect_dma_start(out=found[:, t % SROUND, :].bitcast(I32), out_offset=None, in_=key_blocks,
                                        in_offset=bass.IndirectOffsetOnAxis(ap=block_i[:, t:t + 1], axis=0),
                                        bounds_check=sample_bound, oob_is_err=False) \
                    .then_inc(s["found0" if t < SROUND else "found1"], 16)
            pool.wait_ge(s["zeros_out"], 16 * HEADS)
            pool.wait_ge(s["places_ready"], 1)
            for t in range(TILES):
                pool.indirect_dma_start(out=heads_d, in_=adst[:, t, :], in_offset=None,
                                        out_offset=bass.IndirectOffsetOnAxis(ap=scat_i[:, 0, t:t + 1], axis=0),
                                        bounds_check=edge_bound, oob_is_err=False).then_inc(s["heads_out"], 16)
            with pool.Fori(0, NCHUNK // 2 - 1) as i:
                for u in range(2):
                    pool.wait_ge(s["state_ready"], i * 2 + (u + 1))
                    pool.sem_inc(s["refill_begun"], 1)
                    gather_rows(u)
            pool.wait_ge(s["neutral_out"], 16)
            pool.wait_ge(s["carry_row"], 1)
            pool.indirect_dma_start(out=carry_d, in_=cback[:, :], in_offset=None,
                                    out_offset=bass.IndirectOffsetOnAxis(ap=cidx_i[:, :], axis=0),
                                    bounds_check=node_bound, oob_is_err=False).then_inc(s["carry_out"], 16)
            for u in range(2):
                pool.wait_ge(s[f"state_out{u}"], 16 * (NCHUNK // 2))
            for t in range(TILES):
                pool.indirect_dma_start(out=last_rows[:, t, :], out_offset=None, in_=state_d,
                                        in_offset=bass.IndirectOffsetOnAxis(ap=scat_i[:, 1, t:t + 1], axis=0),
                                        bounds_check=edge_bound, oob_is_err=False).then_inc(s["last_in"], 16)

        @block.tensor
        def _(pe):
            T = nc.tensor
            def expert_out(g, e):
                k = g * EXP + e
                pe.wait_ge(s["hid_ready"], k + 1)
                for j in range(4):
                    last = T.matmul(psum[2 + j // 2][:, (j % 2) * EXP * C + e * C:(j % 2) * EXP * C + (e + 1) * C],
                                    hidden[k % 2][:, j * P:(j + 1) * P], w2[:, e, :], start=False,
                                    stop=(e == EXP - 1), skip_group_check=True)
                last.then_inc(s["ex_ps"], 1)

            pe.wait_ge(s["made"], 1)
            pe.wait_ge(s["x_in"], 32)
            with pe.Fori(0, NCH) as i:
                pe.wait_ge(s["ln1_squared"], i)
                T.matmul(ps_centre[:, :], centring[:, :], x_sb[:, bass.ds(i * CH, CH)], start=True, stop=True) \
                    .then_inc(s["ln1_centred"], 1)
                pe.wait_ge(s["ln1_squared"], i + 1)
                pe.wait_ge(s["ln1_std"], i)
                T.matmul(ps_var[:, :], blockmean[:, :], square, start=True, stop=True).then_inc(s["ln1_var"], 1)
            pe.wait_ge(s["taps_made"], 9)
            pe.wait_ge(s["gat_in"], 32)
            wg = wgat[:, :, :].rearrange("p a n -> p (a n)")

            def conv(c):
                pe.wait_ge(s["padded_ready"], c + 1)
                if c >= 1:
                    pe.wait_ge(s["x1_ready"], c)
                for k in range(9):
                    last = T.matmul(ps_conv[:, :], taps[:, k, :],
                                    padded[c % 2][:, :, k // 3:k // 3 + SIDE, k % 3:k % 3 + SIDE],
                                    start=(k == 0), stop=(k == 8))
                last.then_inc(s["conv_done"], 1)

            def norm2(c):
                pe.wait_ge(s["x1_ready"], c + 1)
                if c == 0:
                    pe.wait_ge(s["ln1_std"], NCH)
                T.matmul(ps_centre[:, :], centring[:, :], x_sb[:, c * CH:(c + 1) * CH], start=True, stop=True) \
                    .then_inc(s["ln2_centred"], 1)
                pe.wait_ge(s["ln2_squared"], c + 1)
                T.matmul(ps_var[:, :], blockmean[:, :], square2, start=True, stop=True).then_inc(s["ln2_var"], 1)

            def project(c):
                pe.wait_ge(s["ln2_ready"], c + 1)
                if c >= 1:
                    pe.wait_ge(s["h_used"], c)
                for j in range(CH // P):
                    last = T.matmul(ps_h[:, j * 2 * HE:(j + 1) * 2 * HE], ln2[:, c * CH + j * P:c * CH + (j + 1) * P],
                                    wg, start=True, stop=True)
                last.then_inc(s["h_done"], 1)

            for n in range(PASSES):
                pe.wait_ge(s["keys_out"], n + 1)
                src = keys[MOVES[n][0]]
                for b in range(4):
                    for j in range(4):
                        cs = (b * 4 + j) * P
                        last = T.transpose(tr_ps[b][:, j * P:(j + 1) * P], src[:, cs:cs + P], ident[:, :])
                    last.then_inc(s["keys_moved"], 1)
                if n < NCH:
                    conv(n)
                if 1 <= n < NCH + 1:
                    norm2(n - 1)
                if 2 <= n < NCH + 2:
                    project(n - 2)

            pe.wait_ge(s["banks_moved"], 4 * PASSES)
            pe.wait_ge(s["w1_in"], 32)
            pe.wait_ge(s["w2_in"], 16)
            pe.wait_ge(s["b2_in"], 16)
            for g in range(2 * NCH):
                c, h = g // 2, g % 2
                if g >= 1:
                    pe.wait_ge(s["ex_ready"], 2 * g)
                for bank in range(2):
                    T.matmul(psum[2 + bank][:, :].rearrange("p (a n) -> p a n", a=2), onesrow[:, :],
                             b2[:, :].rearrange("p (a n) -> p a n", a=1).broadcast_to([1, 2, EXP * C]),
                             start=True, stop=False, skip_group_check=True)
                for e in range(EXP):
                    k = g * EXP + e
                    if k >= 2:
                        pe.wait_ge(s["hid_ready"], k - 1)
                    T.matmul(psum[k % 2][:, :], w1[:, h, e, :], ln2[:, c * CH:(c + 1) * CH], start=True, stop=True) \
                        .then_inc(s["hid_ps"], 1)
                    if e >= 1:
                        expert_out(g, e - 1)
                expert_out(g, EXP - 1)

            pe.wait_ge(s["first_ready"], 1)
            T.matmul(ps_h[:, 0:TILES], shift1[:, :], first[:, 0:TILES], start=True, stop=False)
            T.matmul(ps_h[:, 0:TILES], shift2[:, :], first[:, 1:TILES + 1], start=False, stop=True) \
                .then_inc(s["ends_ps"], 1)

            pe.wait_ge(s["carry_x"], 1)
            for n in range(4):
                last = T.transpose(ps_centre[0:CHN, n * P:(n + 1) * P], cx[:, n, :], ident[:, :])
            last.then_inc(s["carry_t"], 1)
            pe.wait_ge(s["carry_c"], 1)
            for n in range(2):
                last = T.transpose(ps_var[:, n * 32:n * 32 + CHN], ct[:, 10 + n, :], ident[0:CHN, 0:CHN])
            last.then_inc(s["carry_b"], 1)

            for c in range(NCH):
                pe.wait_ge(s["gated"], c + 1)
                if c >= 2:
                    pe.wait_ge(s["final"], c - 1)
                for j in range(CH // P):
                    for e in range(EXP):
                        last = T.matmul(psum[c % 2][:, j * P:(j + 1) * P], experts[:, c * 4 + j, e, :], ident[:, :],
                                        start=(e == 0), stop=(e == EXP - 1))
                last.then_inc(s["out_ps"], 1)

        @block.scalar
        def _(act):
            N = nc.scalar
            act.wait_ge(s["signs_ready"], 1)
            with act.Fori(0, NCH) as i:
                act.wait_ge(s["ln1_centred"], i + 1)
                N.activation(centred[:, bass.ds(i * CH, CH)], ps_centre[:, :], ACT.Copy)
                N.activation(square, ps_centre[:, :], ACT.Square).then_inc(s["ln1_squared"], 1)
                act.wait_ge(s["ln1_var"], i + 1)
                N.activation(std1[:, bass.ds(i * CH, CH)], ps_var[:, :], ACT.Sqrt, bias=eps[:, 0:1]) \
                 .then_inc(s["ln1_std"], 1)
            for n in range(PASSES):
                dst = keys[MOVES[n][1]]
                for b in range(4):
                    act.wait_ge(s["keys_moved"], 4 * n + b + 1)
                    sign = 1.0 if MOVES[n][2] is None else signs[:, MOVES[n][2]:MOVES[n][2] + 1]
                    N.activation(dst[:, b * 512:(b + 1) * 512], tr_ps[b][:, :], ACT.Copy, scale=sign) \
                     .then_inc(s["banks_moved"], 1)
                if 1 <= n < NCH + 1:
                    c = n - 1
                    act.wait_ge(s["ln2_centred"], c + 1)
                    if c >= 2:
                        act.wait_ge(s["ln2_ready"], c - 1)
                    N.activation(centred2[c % 2], ps_centre[:, :], ACT.Copy)
                    N.activation(square2, ps_centre[:, :], ACT.Square).then_inc(s["ln2_squared"], 1)
                    act.wait_ge(s["ln2_var"], c + 1)
                    N.activation(std2[c % 2], ps_var[:, :], ACT.Sqrt, bias=eps[:, 1:2]).then_inc(s["ln2_std"], 1)
            act.wait_ge(s["b1_in"], 16)
            act.wait_ge(s["table_ready"], 1)
            for g in range(2 * NCH):
                c, h = g // 2, g % 2
                for e in range(EXP):
                    k = g * EXP + e
                    act.wait_ge(s["hid_ps"], k + 1)
                    if k >= 2:
                        act.wait_ge(s["ex_ps"], k - 1)
                    N.activation(hidden[k % 2], psum[k % 2][:, :], ACT.Gelu, bias=b1[:, e:e + 1]) \
                     .then_inc(s["hid_ready"], 1)
                act.wait_ge(s["ex_ps"], (g + 1) * EXP)
                for bank in range(2):
                    pair = 4 * c + 2 * bank
                    N.activation(experts[:, pair:pair + 2, :, h * C:(h + 1) * C],
                                 psum[2 + bank][:, :].rearrange("p (a e n) -> p a e n", a=2, e=EXP), ACT.Copy) \
                     .then_inc(s["ex_ready"], 1)
            with act.Fori(0, NCHUNK) as i:
                act.wait_ge(s["diffs_ready"], i + 1)
                N.activation(weight, diff, ACT.Exp).then_inc(s["weights_ready"], 1)
            act.wait_ge(s["carry_diff"], 1)
            N.activation(ct[:, 6:8, :], ct[:, 4:6, :], ACT.Exp).then_inc(s["carry_w"], 1)
            act.wait_ge(s["node_diff"], 1)
            N.activation(tri2, tri, ACT.Exp).then_inc(s["node_w"], 1)
            act.wait_ge(s["node_var"], 1)
            N.activation(nsm[1], nsm[0], ACT.Sqrt, bias=eps[:, 2:3], scale=1.0 / HE).then_inc(s["node_std"], 1)
            act.wait_ge(s["top_ready"], 1)
            N.activation(nt[5], nt[4], ACT.Exp).then_inc(s["top_exp"], 1)

        @block.vector
        def _(dve):
            V = nc.vector
            done = [0]

            def link(ins):
                done[0] += 1
                ins.then_inc(s["dve"], 1)
                dve.wait_ge(s["dve"], done[0])

            V.memset(zeros[:, :], 0.0).then_inc(s["zeros_ready"], 1)
            V.memset(eps[:, 0:1], LN1_EPS)
            V.memset(eps[:, 1:2], LN2_EPS)
            V.memset(eps[:, 2:3], LN3_EPS)
            V.memset(sources[:, COLS:COLS + 2 * TC], 0)
            dve.wait_ge(s["consts"], 1)
            for b in range(7):
                ins = V.tensor_scalar(signs_i[:, b:b + 1], signs_i[:, 7:8], b, 1, ALU.logical_shift_right, ALU.bitwise_and)
            link(ins)
            V.tensor_scalar(signs[:, :], signs_i[:, 0:7], -2.0, 1.0, ALU.mult, ALU.add).then_inc(s["signs_ready"], 1)
            link(V.tensor_scalar(targets[:, :], targets[:, :], SRC_BITS, KEY_ONE, ALU.logical_shift_left, ALU.bitwise_or))

            dve.wait_ge(s["edges_in"], 32)
            src_i, dst_i = keys[0][:, :].bitcast(I32), keys[1][:, :].bitcast(I32)
            V.tensor_scalar(src_i, src_i, float(NODES - 1), 0.0, ALU.min, ALU.max)
            link(V.tensor_scalar(dst_i, dst_i, float(NODES), 0.0, ALU.min, ALU.max))
            link(V.tensor_scalar(dst_i, dst_i, SRC_BITS, KEY_ONE, ALU.logical_shift_left, ALU.bitwise_or))
            link(V.tensor_tensor(src_i, src_i, dst_i, ALU.bitwise_or))
            link(V.tensor_scalar(keys[0][:, :], keys[0][:, :], signs[:, 0:1], None, ALU.mult))

            dve.wait_ge(s["pad_in"], 16)
            lo, hi = pad_i[:, 0:1], pad_i[:, 1:2]
            pt = [pad_t[:, n:n + 1] for n in range(6)]
            V.tensor_scalar(pt[0], hi, 20, 0x7FF, ALU.logical_shift_right, ALU.bitwise_and)
            V.tensor_scalar(pt[1], hi, 0xFFFFF, 3, ALU.bitwise_and, ALU.logical_shift_left)
            V.tensor_scalar(pt[2], lo, 29, 7, ALU.logical_shift_right, ALU.bitwise_and)
            V.tensor_scalar(pt[3], lo, 28, 1, ALU.logical_shift_right, ALU.bitwise_and)
            link(V.tensor_scalar(pt[4], hi, 31, 31, ALU.logical_shift_right, ALU.logical_shift_left))
            V.tensor_scalar(pad_f[:, 1:2], pt[0], float(1023 - 127), None, ALU.is_gt)
            link(V.tensor_scalar(pt[0], pt[0], -float(1023 - 127), 0.0, ALU.add, ALU.max))
            link(V.tensor_scalar(pt[0], pt[0], 255.0, None, ALU.min))
            link(V.tensor_scalar(pt[0], pt[0], 23, None, ALU.logical_shift_left))
            link(V.tensor_tensor(pt[1], pt[1], pt[2], ALU.bitwise_or))
            link(V.tensor_tensor(pt[1], pt[1], pt[0], ALU.bitwise_or))
            link(V.tensor_tensor(pt[1], pt[1], pt[3], ALU.add))
            link(V.tensor_tensor(pt[1], pt[1], pt[4], ALU.bitwise_or))
            link(V.tensor_tensor(pad_f[:, 0:1], pt[1].bitcast(F32), pad_f[:, 1:2], ALU.mult))
            for n in range(2):
                link(V.memset(padded[n], 0.0))
                link(V.tensor_scalar(padded[n], padded[n], pad_f[:, 0:1], None, ALU.add))

            dve.wait_ge(s["chan_in"], 16 * 6)
            sh = chan[:, 2:3]
            V.tensor_scalar(half_s[:, 2:3], sh, 0.0, None, ALU.is_gt)
            V.tensor_scalar(pow_i[:, 0:1], sh, 126.0, float(1 << 23), ALU.add, ALU.mult)
            link(V.tensor_scalar(pow_i[:, 1:2], sh, -127.0, -float(1 << 23), ALU.add, ALU.mult))
            link(V.tensor_tensor(half_s[:, 0:1], pow_i[:, 0:1].bitcast(F32), half_s[:, 2:3], ALU.mult))
            half_b, inv_b = half_s[:, 0:1], pow_i[:, 1:2].bitcast(F32)

            def stage(src, dst, k, j, signal=None):
                def end(ins):
                    link(ins) if signal is None else ins.then_inc(s[signal], 1)

                if k is None:
                    a = src[:, :].rearrange("p (n t j) -> p n t j", t=2, j=j)
                    b = dst[:, :].rearrange("p (n t j) -> p n t j", t=2, j=j)
                    V.tensor_tensor(b[:, :, 0, :], a[:, :, 0, :], a[:, :, 1, :], ALU.min)
                    end(V.tensor_tensor(b[:, :, 1, :], a[:, :, 0, :], a[:, :, 1, :], ALU.max))
                    return
                a = src[:, :].rearrange("p (g d n t j) -> p g d n t j", d=2, n=k // (2 * j), t=2, j=j)
                b = dst[:, :].rearrange("p (g d n t j) -> p g d n t j", d=2, n=k // (2 * j), t=2, j=j)
                for d in range(2):
                    low, high = (ALU.min, ALU.max) if d == 0 else (ALU.max, ALU.min)
                    V.tensor_tensor(b[:, :, d, :, 0, :], a[:, :, d, :, 0, :], a[:, :, d, :, 1, :], low)
                    ins = V.tensor_tensor(b[:, :, d, :, 1, :], a[:, :, d, :, 0, :], a[:, :, d, :, 1, :], high)
                end(ins)

            def norm1(c):
                cs = slice(c * CH, (c + 1) * CH)
                dve.wait_ge(s["ln1_std"], NCH)
                if c >= 2:
                    dve.wait_ge(s["conv_done"], c - 1)
                link(V.reciprocal(rstd, std1[:, cs]))
                V.tensor_tensor(padded[c % 2][:, :, 1:1 + SIDE, 1:1 + SIDE],
                                centred[:, cs].rearrange("p (b r c) -> p b r c", b=2, r=SIDE),
                                rstd.rearrange("p (b r c) -> p b r c", b=2, r=SIDE), ALU.mult) \
                 .then_inc(s["padded_ready"], 1)
                dve.wait_ge(s["padded_ready"], c + 1)

            def round_down(dst, scratch, value, scalar, op):
                link(V.tensor_scalar(scratch, value, scalar, MAGIC, op, ALU.add))
                link(V.tensor_scalar(scratch, scratch, MAGIC, None, ALU.subtract))
                link(V.scalar_tensor_tensor(out=dst, in0=value, scalar=scalar, in1=scratch, op0=op, op1=ALU.is_lt))
                link(V.tensor_tensor(dst, scratch, dst, ALU.subtract))

            def requantise(c):
                cs = slice(c * CH, (c + 1) * CH)
                dve.wait_ge(s["conv_done"], c + 1)
                link(V.tensor_scalar(qa, ps_conv[:, :], chan[:, 0:1], 32768.0, ALU.add, ALU.add))
                round_down(qb, qc, qa, 2.0 ** -16, ALU.mult)
                link(V.scalar_tensor_tensor(out=qa, in0=qb, scalar=-65536.0, in1=qa, op0=ALU.mult, op1=ALU.add))
                link(V.tensor_scalar(qa, qa, 32768.0, chan[:, 1:2], ALU.subtract, ALU.mult))
                link(V.tensor_scalar(qa, qa, 2.0 ** -15, 32768.0, ALU.mult, ALU.min))
                round_down(qb, qc, qa, 0.0, ALU.max)
                link(V.tensor_scalar(qa, qb, half_b, inv_b, ALU.add, ALU.mult))
                round_down(qb, qc, qa, 0.0, ALU.max)
                link(V.tensor_scalar(qb, qb, 255.0, 32.0, ALU.min, ALU.subtract))
                V.tensor_tensor(x_sb[:, cs], x_sb[:, cs], qb, ALU.add).then_inc(s["x1_ready"], 1)
                dve.wait_ge(s["x1_ready"], c + 1)

            def norm2(c):
                dve.wait_ge(s["ln2_std"], c + 1)
                link(V.reciprocal(rstd, std2[c % 2]))
                V.tensor_tensor(ln2[:, c * CH:(c + 1) * CH], centred2[c % 2], rstd, ALU.mult).then_inc(s["ln2_ready"], 1)
                dve.wait_ge(s["ln2_ready"], c + 1)

            def keep_rows(c):
                dve.wait_ge(s["h_done"], c + 1)
                hp = ps_h[:, 0:CH // P * 2 * HE].rearrange("p (j a n) -> p j a n", a=2, n=HE)
                for h in range(2):
                    ins = V.tensor_copy(table[:, h * PAIRS + 4 * c:h * PAIRS + 4 * c + 4, 0:HE], hp[:, :, h, :])
                ins.then_inc(s["h_used"], 1)

            def attention_terms():
                dve.wait_ge(s["rows_in"], 16 * 5)
                dve.wait_ge(s["h_used"], NCH)
                prod = [ex_flat[:, n * TILES * HE:(n + 1) * TILES * HE] for n in range(2)]
                for n in range(2):
                    ins = V.tensor_tensor(prod[n].rearrange("p (t n) -> p t n", n=HE), table[:, :, 0:HE],
                                          rowc[:, n:n + 1, :].broadcast_to([P, TILES, HE]), ALU.mult)
                link(ins)
                V.tensor_reduce(table[:, :, HE:ROW], prod[0].rearrange("p (t h e) -> p t h e", h=HEADS, e=EXP),
                                AX.X, ALU.add)
                V.tensor_reduce(adst[:, :, :], prod[1].rearrange("p (t h e) -> p t h e", h=HEADS, e=EXP),
                                AX.X, ALU.add).then_inc(s["table_ready"], 1)

            def move(n):
                if n < NCH:
                    norm1(n)
                if 1 <= n < NCH + 1:
                    requantise(n - 1)
                if 2 <= n < NCH + 2:
                    norm2(n - 2)
                if 3 <= n < NCH + 3:
                    keep_rows(n - 3)
                if n == NCH + 3:
                    attention_terms()
                dve.wait_ge(s["banks_moved"], 4 * (n + 1))

            at, n = 0, 0
            for level in range(1, LOG_COLS + 1):
                for bit in range(level - 1, -1, -1):
                    k = None if level == LOG_COLS else 1 << level
                    stage(keys[at], keys[1 - at], k, 1 << bit)
                    at = 1 - at
            for level in LEVELS_T:
                V.tensor_scalar(keys[at][:, :], keys[at][:, :], signs[:, level - 1 - LOG_COLS:level - LOG_COLS], None,
                                ALU.mult).then_inc(s["keys_out"], 1)
                assert MOVES[n][0] == at and MOVES[n][1] == 1 - at
                move(n)
                n, at = n + 1, 1 - at
                for bit in range(level - LOG_COLS - 1, -1, -1):
                    k = None if level == LOG_EDGES else 1 << (level - LOG_COLS)
                    stage(keys[at], keys[1 - at], k, 1 << bit, None if bit else "keys_out")
                    at = 1 - at
                assert MOVES[n][0] == at and MOVES[n][1] == 1 - at
                move(n)
                n, at = n + 1, 1 - at
                for bit in range(LOG_COLS - 1, -1, -1):
                    last = level == LOG_EDGES and bit == 0
                    stage(keys[at], keys[1 - at], None, 1 << bit, "sorted_ready" if last else None)
                    at = 1 - at
            assert at == SORTED
            dve.wait_ge(s["sorted_ready"], 1)
            sk = keys[at][:, :].bitcast(I32)
            other = keys[1 - at][:, :].bitcast(I32)

            link(V.tensor_scalar(sources[:, 0:COLS], sk, NODES - 1, None, ALU.bitwise_and))
            for u in range(2):
                V.tensor_copy(index[u][:, :], sources[:, u * TC:(u + 1) * TC])
            V.tensor_copy(ends[:, 0:1], sk[:, 0:1])
            V.memset(ends[:, 2:3], 0)
            V.memset(ends[:, 3:4], 0)
            link(V.tensor_copy(ends[:, 1:2], sk[:, COLS - 1:COLS]))
            DST_MASK = (1 << (SRC_BITS + 2)) - 1
            link(V.tensor_scalar(ends_i[:, 0:1], ends[:, 0:1], SRC_BITS, DST_MASK, ALU.logical_shift_right, ALU.bitwise_and))
            V.tensor_scalar(dfirst_i[:, :], ends_i[:, 0:1], float(NODES - 1), None, ALU.min).then_inc(s["idx_ready"], 1)
            V.tensor_copy(samples[:, :], sk.rearrange("p (a b) -> p a b", b=SAMPLE)[:, :, 0]).then_inc(s["samples_ready"], 1)
            link(V.tensor_scalar(other, sk, SRC_BITS, None, ALU.logical_shift_right))
            dve.wait_ge(s["zeros_out"], 16 * HEADS)
            link(V.memset(same[:, 0:1], 1.0))
            link(V.tensor_tensor(same[:, 1:COLS], other[:, 1:COLS], other[:, 0:COLS - 1], ALU.is_equal))

            tf = targets[:, :].bitcast(F32)
            junk = keys[1 - at][:, :]
            dve.wait_ge(s["samples_in"], 16)
            for t in range(TILES + 1):
                ins = V.tensor_scalar(junk[:, 0:NSAMP], samples_b, tf[:, t:t + 1], None, ALU.is_lt, ALU.add,
                                      accum_out=count[:, t:t + 1])
                if t < TILES:
                    link(ins)
            link(ins)
            link(V.tensor_scalar(block_f[:, :], count[:, :], -1.0, 0.0, ALU.add, ALU.max))
            V.tensor_copy(block_i[:, :], block_f[:, :]).then_inc(s["block_ready"], 1)
            dve.wait_ge(s["found0"], 16 * SROUND)
            for t in range(TILES + 1):
                if t == SROUND:
                    dve.wait_ge(s["found1"], 16 * (TILES + 1 - SROUND))
                V.tensor_scalar(junk[:, 0:SAMPLE], found[:, t % SROUND, :], tf[:, t:t + 1], None, ALU.is_lt, ALU.add,
                                accum_out=count[:, t:t + 1]).then_inc(s["found_used"], 1)
                dve.wait_ge(s["found_used"], t + 1)
            V.scalar_tensor_tensor(out=first[:, :], in0=block_f[:, :], scalar=float(SAMPLE), in1=count[:, :],
                                   op0=ALU.mult, op1=ALU.add).then_inc(s["first_ready"], 1)
            dve.wait_ge(s["ends_ps"], 1)
            end = ps_h[:, 0:TILES]
            link(V.tensor_tensor(empty[:, :], end, first[:, 0:TILES], ALU.is_equal))
            V.scalar_tensor_tensor(out=scat_f[:, 0, :], in0=empty[:, :], scalar=float(FAR), in1=first[:, 0:TILES],
                                   op0=ALU.mult, op1=ALU.add)
            link(V.tensor_scalar(scat_f[:, 1, :], end, -1.0, 0.0, ALU.add, ALU.max))
            V.tensor_copy(scat_i[:, :, :], scat_f[:, :, :]).then_inc(s["places_ready"], 1)

            dve.wait_ge(s["neigh_in"], 32)
            link(V.tensor_scalar(ends_i[:, :], ends[:, :], SRC_BITS, DST_MASK, ALU.logical_shift_right, ALU.bitwise_and))
            link(V.tensor_copy(ends_f[:, :], ends_i[:, :]))
            V.tensor_tensor(flags[:, 0:1], ends_f[:, 0:1], ends_f[:, 2:3], ALU.is_equal)
            V.tensor_tensor(flags[:, 1:2], ends_f[:, 0:1], ends_f[:, 1:2], ALU.is_equal)
            link(V.tensor_tensor(flags[:, 2:3], ends_f[:, 1:2], ends_f[:, 3:4], ALU.is_equal))
            link(V.tensor_tensor(cidx_f[:, :], flags[:, 1:2], flags[:, 2:3], ALU.mult))
            link(V.tensor_scalar(cidx_f[:, :], cidx_f[:, :], -1.0, 1.0, ALU.mult, ALU.add))
            link(V.tensor_tensor(cidx_f[:, :], cidx_f[:, :], flags[:, 0:1], ALU.mult))
            link(V.tensor_scalar(cidx_f[:, :], cidx_f[:, :], -float(FAR), float(FAR), ALU.mult, ALU.add))
            link(V.tensor_tensor(cidx_f[:, :], cidx_f[:, :], ends_f[:, 0:1], ALU.add))
            link(V.tensor_copy(cidx_i[:, :], cidx_f[:, :]))

            dve.wait_ge(s["ex_ready"], 4 * NCH)
            dve.wait_ge(s["dfirst_in"], 16)
            V.tensor_copy(adst_e[1][:, :, TC - 1], dfirst[:, :])
            V.memset(top_e[1][:, :, TC:TC + 1], 0.0)
            V.memset(state[1][:, TC - 1, HEADS:ST], 0.0)
            link(V.memset(state[1][:, TC - 1, 0:HEADS], -BIG))

            STEPS = 6
            base = done[0]
            with dve.Fori(0, NCHUNK // 2) as i:
                for u in range(2):
                    off = i * (2 * TC) + u * TC
                    step = [0]

                    def after(ins):
                        step[0] += 1
                        ins.then_inc(s["dve"], 1)
                        dve.wait_ge(s["dve"], i * (2 * STEPS) + (base + u * STEPS + step[0]))

                    g, st, last = gathered[u], state[u], 1 - u
                    ad, top = adst_e[u], top_e[u]
                    dve.wait_ge(s[f"gath{u}"], i * (16 * TC) + 16 * TC)
                    dve.wait_ge(s[f"head_in{u}"], i * 16 + 16)
                    dve.wait_ge(s[f"state_out{u}"], i * 16)
                    sm = same[:, bass.ds(off, TC)]
                    after(V.tensor_scalar(fresh, sm, -1.0, BIG, ALU.add, ALU.mult))
                    for h in range(HEADS):
                        V.tensor_tensor_scan(st[:, :, h], fresh, g[:, :, HE + h], state[last][:, TC - 1, h:h + 1],
                                             ALU.add, ALU.max)
                        ins = V.tensor_tensor_scan(ad[:, h, :], sm, headrow[u][:, :, h], adst_e[last][:, h, TC - 1:TC],
                                                   ALU.mult, ALU.add)
                    V.tensor_copy(top[:, :, 0:1], top_e[last][:, :, TC:TC + 1])
                    V.tensor_copy(index[u][:, :], sources[:, bass.ds(off + 2 * TC, TC)])
                    after(ins)
                    V.tensor_tensor(raw[:, 0], g[:, :, HE:ROW].rearrange("p t h -> p h t"), ad, ALU.add)
                    after(V.tensor_tensor(raw[:, 1], st[:, :, 0:HEADS].rearrange("p t h -> p h t"), ad, ALU.add))
                    V.scalar_tensor_tensor(out=raw[:, 0], in0=raw[:, 0], scalar=SLOPE, in1=raw[:, 0], op0=ALU.mult, op1=ALU.max)
                    after(V.scalar_tensor_tensor(out=top[:, :, 1:TC + 1], in0=raw[:, 1], scalar=SLOPE, in1=raw[:, 1],
                                                 op0=ALU.mult, op1=ALU.max))
                    V.tensor_tensor(diff[:, 0], raw[:, 0], top[:, :, 1:TC + 1], ALU.subtract)
                    after(V.tensor_tensor(diff[:, 1], top[:, :, 0:TC], top[:, :, 1:TC + 1], ALU.subtract))
                    V.tensor_scalar(diff[:, 1], diff[:, 1], 0.0, None, ALU.min).then_inc(s["diffs_ready"], 1)
                    dve.wait_ge(s["weights_ready"], i * 2 + (u + 1))
                    for h in range(HEADS):
                        V.tensor_tensor(part[:, h], g[:, :, h * EXP:(h + 1) * EXP].rearrange("p t e -> p e t"),
                                        weight[:, 0, h:h + 1, :].broadcast_to([P, EXP, TC]), ALU.mult)
                    after(V.tensor_tensor(diff[:, 0], weight[:, 1],
                                          same[:, bass.ds(off, TC)].rearrange("p (a t) -> p a t", a=1).broadcast_to([P, HEADS, TC]),
                                          ALU.mult))
                    for h in range(HEADS):
                        c = HEADS + h
                        V.tensor_tensor_scan(st[:, :, c], diff[:, 0, h], weight[:, 0, h], state[last][:, TC - 1, c:c + 1],
                                             ALU.mult, ALU.add)
                        for e in range(EXP):
                            c = 2 * HEADS + h * EXP + e
                            ins = V.tensor_tensor_scan(st[:, :, c], diff[:, 0, h], part[:, h, e],
                                                       state[last][:, TC - 1, c:c + 1], ALU.mult, ALU.add)
                    ins.then_inc(s["state_ready"], 1)
                    dve.wait_ge(s["state_ready"], i * 2 + (u + 1))
                    assert step[0] == STEPS
            done[0] = base + 2 * STEPS * (NCHUNK // 2)

            lastrow = state[1][:, TC - 1, :]
            cg = [cx[:, n, :].rearrange("p (h k) -> p h k", h=HEADS) for n in range(4)]
            V.tensor_copy(cg[0], lastrow[:, 0:HEADS].rearrange("p (h a) -> p h a", a=1).broadcast_to([P, HEADS, 1 + EXP]))
            V.tensor_copy(cg[1][:, :, 0:1], lastrow[:, HEADS:2 * HEADS].rearrange("p (h a) -> p h a", a=1))
            V.tensor_copy(cg[1][:, :, 1:1 + EXP], lastrow[:, 2 * HEADS:ST].rearrange("p (h e) -> p h e", h=HEADS))
            V.tensor_copy(cg[2], adst_e[1][:, :, TC - 1:TC].broadcast_to([P, HEADS, 1 + EXP]))
            link(V.tensor_tensor(cidx_f[:, :], flags[:, 0:1], flags[:, 1:2], ALU.mult))
            V.tensor_copy(cx[:, 3, :], cidx_f[:, 0:1].broadcast_to([P, CHN])).then_inc(s["carry_x"], 1)
            dve.wait_ge(s["carry_t"], 1)
            link(V.tensor_copy(ct[:, 0:4, :], ps_centre[0:CHN, :].rearrange("p (a b) -> p a b", a=4)))
            M_, V_, D_, C_ = (ct[:, n, :] for n in range(4))
            link(V.tensor_scalar(ct[:, 4, :], C_, -1.0, BIG, ALU.add, ALU.mult))
            link(V.tensor_tensor_scan(ct[:, 8, :], ct[:, 4, :], M_, -BIG, ALU.add, ALU.max))
            V.tensor_tensor(ct[:, 9, :], ct[:, 8, :], D_, ALU.add)
            link(V.tensor_tensor(ct[:, 10, :], M_, D_, ALU.add))
            V.scalar_tensor_tensor(out=ct[:, 9, :], in0=ct[:, 9, :], scalar=SLOPE, in1=ct[:, 9, :], op0=ALU.mult, op1=ALU.max)
            link(V.scalar_tensor_tensor(out=ct[:, 10, :], in0=ct[:, 10, :], scalar=SLOPE, in1=ct[:, 10, :], op0=ALU.mult, op1=ALU.max))
            V.memset(ct[:, 5, 0:1], 0.0)
            V.tensor_tensor(ct[:, 4, :], ct[:, 10, :], ct[:, 9, :], ALU.subtract)
            link(V.tensor_tensor(ct[:, 5, 1:P], ct[:, 9, 0:P - 1], ct[:, 9, 1:P], ALU.subtract))
            V.tensor_scalar(ct[:, 5, :], ct[:, 5, :], 0.0, None, ALU.min).then_inc(s["carry_diff"], 1)
            dve.wait_ge(s["carry_w"], 1)
            V.tensor_tensor(ct[:, 7, :], ct[:, 7, :], C_, ALU.mult)
            link(V.tensor_tensor(ct[:, 6, :], ct[:, 6, :], V_, ALU.mult))
            link(V.tensor_tensor_scan(ct[:, 9, :], ct[:, 7, :], ct[:, 6, :], 0.0, ALU.mult, ALU.add))
            V.memset(ct[:, 10, 0:1], -BIG)
            V.memset(ct[:, 11, 0:1], 0.0)
            V.tensor_copy(ct[:, 10, 1:P], ct[:, 8, 0:P - 1])
            V.tensor_copy(ct[:, 11, 1:P], ct[:, 9, 0:P - 1]).then_inc(s["carry_c"], 1)
            dve.wait_ge(s["carry_b"], 1)
            bm = ps_var[:, 0:CHN].rearrange("p (h k) -> p h k", h=HEADS)
            bv = ps_var[:, 32:32 + CHN].rearrange("p (h k) -> p h k", h=HEADS)
            V.tensor_copy(cback[:, 0:HEADS].rearrange("p (h a) -> p h a", a=1), bm[:, :, 0:1])
            V.tensor_copy(cback[:, HEADS:2 * HEADS].rearrange("p (h a) -> p h a", a=1), bv[:, :, 0:1])
            V.tensor_copy(cback[:, 2 * HEADS:ST].rearrange("p (h e) -> p h e", h=HEADS), bv[:, :, 1:1 + EXP]) \
             .then_inc(s["carry_row"], 1)

            dve.wait_ge(s["last_in"], 16 * TILES)
            dve.wait_ge(s["carry_in"], 16)
            link(V.tensor_scalar(nsm[0], empty[:, :], -BIG, None, ALU.mult))
            ec = nsm[0].rearrange("p (t a) -> p t a", a=1).broadcast_to([P, TILES, HEADS])
            link(V.tensor_tensor(nt[0], last_rows[:, :, 0:HEADS], ec, ALU.add))
            link(V.tensor_tensor(nt[1], nt[0], carried[:, :, 0:HEADS], ALU.max))
            link(V.tensor_tensor(nt[1], nt[1], table[:, :, HE:ROW], ALU.max))
            V.tensor_tensor(nt[2], nt[1], adst[:, :, :], ALU.add)
            V.tensor_tensor(tri[:, 0], nt[0], adst[:, :, :], ALU.add)
            V.tensor_tensor(tri[:, 1], carried[:, :, 0:HEADS], adst[:, :, :], ALU.add)
            link(V.tensor_tensor(tri[:, 2], table[:, :, HE:ROW], adst[:, :, :], ALU.add))
            V.scalar_tensor_tensor(out=nt[2], in0=nt[2], scalar=SLOPE, in1=nt[2], op0=ALU.mult, op1=ALU.max)
            link(V.scalar_tensor_tensor(out=tri, in0=tri, scalar=SLOPE, in1=tri, op0=ALU.mult, op1=ALU.max))
            V.tensor_tensor(tri.rearrange("p a t h -> p a (t h)"), tri.rearrange("p a t h -> p a (t h)"),
                            nt[2].rearrange("p (a t) h -> p a (t h)", a=1).broadcast_to([P, 3, NH4]), ALU.subtract) \
             .then_inc(s["node_diff"], 1)
            dve.wait_ge(s["node_w"], 1)

            def spread(x):
                return x.rearrange("p t (h a) -> p t h a", a=1).broadcast_to([P, TILES, HEADS, EXP])

            V.tensor_tensor(nt[0], last_rows[:, :, HEADS:2 * HEADS], tri2[:, 0], ALU.mult)
            V.tensor_tensor(nt[1], carried[:, :, HEADS:2 * HEADS], tri2[:, 1], ALU.mult)
            V.tensor_tensor(n16[0], last_rows[:, :, 2 * HEADS:ST].rearrange("p t (h e) -> p t h e", h=HEADS), spread(tri2[:, 0]), ALU.mult)
            V.tensor_tensor(n16[1], carried[:, :, 2 * HEADS:ST].rearrange("p t (h e) -> p t h e", h=HEADS), spread(tri2[:, 1]), ALU.mult)
            link(V.tensor_tensor(n16[2], table[:, :, 0:HE].rearrange("p t (h e) -> p t h e", h=HEADS), spread(tri2[:, 2]), ALU.mult))
            V.tensor_tensor(nt[0], nt[0], nt[1], ALU.add)
            link(V.tensor_tensor(n16[0], n16[0], n16[1], ALU.add))
            V.tensor_tensor(nt[0], nt[0], tri2[:, 2], ALU.add)
            link(V.tensor_tensor(n16[0], n16[0], n16[2], ALU.add))
            link(V.tensor_scalar(nt[0], nt[0], 1e-16, None, ALU.add))
            link(V.reciprocal(nt[1], nt[0]))
            link(V.tensor_tensor(n16[0], n16[0], spread(nt[1]), ALU.mult))
            flat = [x.rearrange("p t h e -> p t (h e)") for x in n16]

            def per_row(n):
                return rowc[:, n:n + 1, :].broadcast_to([P, TILES, HE])

            def per_node(x):
                return x.rearrange("p (t a) -> p t a", a=1).broadcast_to([P, TILES, HE])

            link(V.tensor_tensor(flat[0], flat[0], per_row(2), ALU.add))
            link(V.tensor_reduce(nsm[0], flat[0], AX.X, ALU.add))
            link(V.tensor_scalar(nsm[0], nsm[0], 1.0 / HE, None, ALU.mult))
            link(V.tensor_tensor(flat[0], flat[0], per_node(nsm[0]), ALU.subtract))
            link(V.tensor_tensor(flat[1], flat[0], flat[0], ALU.mult))
            V.tensor_reduce(nsm[0], flat[1], AX.X, ALU.add).then_inc(s["node_var"], 1)
            dve.wait_ge(s["node_std"], 1)
            link(V.reciprocal(nsm[2], nsm[1]))
            link(V.tensor_tensor(flat[0], flat[0], per_node(nsm[2]), ALU.mult))
            link(V.tensor_tensor(flat[0], flat[0], per_row(3), ALU.mult))
            link(V.tensor_tensor(flat[0], flat[0], per_row(4), ALU.add))
            link(V.tensor_reduce(nt[3], n16[0].rearrange("p t h e -> p t e h"), AX.X, ALU.add))
            link(V.tensor_scalar(nt[3], nt[3], 1.0 / HEADS, None, ALU.mult))
            link(V.memset(nt[6], 0.0))
            for a in range(EXP):
                for b in range(a + 1, EXP):
                    link(V.tensor_tensor(nsm[3], nt[3][:, :, b], nt[3][:, :, a], ALU.is_gt))
                    V.tensor_tensor(nt[6][:, :, a], nt[6][:, :, a], nsm[3], ALU.add)
                    link(V.tensor_scalar(nsm[4], nsm[3], -1.0, 1.0, ALU.mult, ALU.add))
                    link(V.tensor_tensor(nt[6][:, :, b], nt[6][:, :, b], nsm[4], ALU.add))
            V.tensor_scalar(nt[6], nt[6], 2.0, None, ALU.is_lt)
            link(V.tensor_reduce(nsm[5], nt[3], AX.X, ALU.max))

            def per_four(x):
                return x.rearrange("p (t a) -> p t a", a=1).broadcast_to([P, TILES, EXP])

            V.tensor_tensor(nt[4], nt[3], per_four(nsm[5]), ALU.subtract).then_inc(s["top_ready"], 1)
            dve.wait_ge(s["top_exp"], 1)
            link(V.tensor_tensor(nt[5], nt[5], nt[6], ALU.mult))
            link(V.tensor_reduce(nsm[6], nt[5], AX.X, ALU.add))
            link(V.reciprocal(nsm[7], nsm[6]))
            link(V.tensor_tensor(nt[5], nt[5], per_four(nsm[7]), ALU.mult))
            link(V.tensor_copy(gates.rearrange("p e a h -> p a h e"), nt[5].rearrange("p (h a) e -> p a h e", h=2)))

            def finish(c):
                dve.wait_ge(s["out_ps"], c + 1)
                cs = slice(c * CH, (c + 1) * CH)
                V.tensor_tensor(x_sb[:, cs], x_sb[:, cs], psum[c % 2][:, :], ALU.add).then_inc(s["final"], 1)

            for c in range(NCH):
                for e in range(EXP):
                    x = experts[:, 4 * c:4 * c + 4, e, :].rearrange("p a (h n) -> p a h n", h=2)
                    g = gates[:, e, 4 * c:4 * c + 4, :].rearrange("p a (h n) -> p a h n", n=1).broadcast_to([P, 4, 2, C])
                    ins = V.tensor_tensor(x, x, g, ALU.mult)
                ins.then_inc(s["gated"], 1)
                if c >= 1:
                    finish(c - 1)
            finish(NCH - 1)
    return nc


def kernel(**inputs):
    import numpy as np
    import concourse.bacc as bacc
    from concourse.bass_utils import run_bass_kernel_spmd

    nc = bacc.Bacc("TRN2", target_bir_lowering=False, num_devices=1)
    arrays, args = {}, {}
    for name, value in inputs.items():
        a = np.asarray(value)
        if name == "L0_conv_pad_fill":
            a = a.reshape(1).view(np.int64)
            short = "pad"
        else:
            short = name.replace("L0_conv_", "").replace("L0_ffn_", "")
        a = np.ascontiguousarray(a)
        arrays["in_" + short] = a
        args[short] = nc.dram_tensor("in_" + short, a.shape, mybir.dt.from_np(a.dtype), kind="ExternalInput").ap()
    out = nc.dram_tensor("out", (B, C, SIDE, SIDE), F32, kind="ExternalOutput").ap()
    build(nc, args, out)
    return run_bass_kernel_spmd(nc, [arrays], core_ids=[0]).results[0]["out"]
```

```python
import concourse.bass as bass
from concourse import mybir
from contextlib import ExitStack

F32 = mybir.dt.float32
I32 = mybir.dt.int32
ALU = mybir.AluOpType
ACT = mybir.ActivationFunctionType
AX = mybir.AxisListType

P = 128
B, C, S = 32, 64, 256
SIDE = 16
NODES = B * S
EDGES = 262144
COLS = EDGES // P
TILES = NODES // P
HALF = B // 2
TOK = HALF * S
CH = 512
NCH = TOK // CH
PAIRS = TOK // P
HEADS, EXP = 4, 4
HE = HEADS * EXP
HID = 2 * C
SRC_BITS = 13
KEY_ONE = 0x20000000
ROW = HE + HEADS
ST = HEADS + HEADS + HE
TC = 32
PAIRW = 2 * TC
NPAIR = COLS // PAIRW
BLK = 64
NBLK = COLS // BLK
EARLY = 12
NSAMP = NBLK - 1
SROW = NSAMP + 2
GROUP = 8
NGROUP = TILES // GROUP + 1
DROPPED = 9000.0
KEY_END = 2.0 ** -55
BIG = 1.0e30
MAGIC = 12582912.0
FAR = 1 << 20
LN1_EPS, LN2_EPS, LN3_EPS = 1e-6, 1e-5, 1e-5
SLOPE = 0.2
LOG_COLS = 11
LOG_EDGES = 18


def build(nc, A, out):
    ctx = ExitStack()
    with ctx:
        def sb(name, shape, dt=F32):
            return ctx.enter_context(nc.sbuf_tensor(name, shape, dt))

        def sem(name):
            return ctx.enter_context(nc.semaphore(name))

        def dram(name, shape, dt=F32):
            return nc.dram_tensor(name, shape, dt).ap()

        keys_d = dram("keys_d", [P, COLS], I32)
        dests_d = dram("dests_d", [P, COLS])
        rows_d = dram("rows_d", [NODES, ROW])
        adst_d = dram("adst_d", [NODES, HEADS])
        heads_d = dram("heads_d", [EDGES, HEADS])
        state_d = dram("state_d", [EDGES, ST])
        carry_d = dram("carry_d", [NODES, ST])

        x_sb = sb("x_sb", [P, TOK])
        ln2 = sb("ln2", [P, TOK])
        experts = sb("experts", [P, PAIRS, EXP, P])
        ex_flat = experts[:, :, :, :].rearrange("p a e c -> p (a e c)")
        centred = ex_flat[:, 0:TOK]
        square, qb, qc, square2 = (ex_flat[:, 3 * TOK + n * CH:3 * TOK + (n + 1) * CH] for n in range(4))
        qa = [ex_flat[:, TOK + n * CH:TOK + (n + 1) * CH] for n in range(2)]
        SP_ = SIDE + 2
        pad0, padn = 3 * TOK + 5 * CH, 2 * SP_ * SP_
        padded = [ex_flat[:, pad0 + n * padn:pad0 + (n + 1) * padn]
                  .rearrange("p (b r c) -> p b r c", b=2, r=SP_) for n in range(2)]

        LEVELS_T = list(range(LOG_COLS + 1, LOG_EDGES + 1))
        PASSES = 2 * len(LEVELS_T)
        MOVES, at = [], LOG_COLS * (LOG_COLS + 1) // 2 % 2
        for level in LEVELS_T:
            MOVES.append((at, 1 - at, None))
            at = (1 - at + level - LOG_COLS) % 2
            MOVES.append((at, 1 - at, level - LOG_COLS if level < LOG_EDGES else None))
            at = (1 - at + LOG_COLS) % 2
        SORTED = at

        keys = [sb("keys0", [P, COLS]), sb("keys1", [P, COLS])]
        sources = sb("sources", [P, COLS + PAIRW], I32)
        same = sb("same", [P, COLS])
        times = sb("times", [P, COLS])
        work = sb("work", [P, 4096])
        column = work[:, 0:COLS].bitcast(I32)
        nodes1k = work[:, COLS:COLS + GROUP * P].bitcast(I32)
        found = sb("found", [P, TILES + 1, BLK])
        found_flat = found[:, :, :].rearrange("p t b -> p (t b)")
        index = [sb("index0", [P, TC], I32), sb("index1", [P, TC], I32)]
        gathered = [sb("gath0", [P, TC, ROW]), sb("gath1", [P, TC, ROW])]
        state = [sb("state0", [P, TC, ST]), sb("state1", [P, TC, ST])]
        headrow = [sb("headrow0", [P, TC, HEADS]), sb("headrow1", [P, TC, HEADS])]
        o = 0
        adst_e, top_e = [], []
        for n in range(2):
            adst_e.append(work[:, o:o + HEADS * TC].rearrange("p (h t) -> p h t", h=HEADS)); o += HEADS * TC
        for n in range(2):
            top_e.append(work[:, o:o + HEADS * (TC + 1)].rearrange("p (h t) -> p h t", h=HEADS)); o += HEADS * (TC + 1)
        fresh = work[:, o:o + TC]; o += TC
        behind = work[:, o:o + TC]; o += TC
        masked = work[:, o:o + HEADS * TC].rearrange("p (h t) -> p h t", h=HEADS); o += HEADS * TC
        raw = work[:, o:o + 2 * HEADS * TC].rearrange("p (a h t) -> p a h t", a=2, h=HEADS); o += 2 * HEADS * TC
        diff = work[:, o:o + 2 * HEADS * TC].rearrange("p (a h t) -> p a h t", a=2, h=HEADS); o += 2 * HEADS * TC
        weight = work[:, o:o + 2 * HEADS * TC].rearrange("p (a h t) -> p a h t", a=2, h=HEADS); o += 2 * HEADS * TC
        part = work[:, o:o + HE * TC].rearrange("p (h e t) -> p h e t", h=HEADS, e=EXP)
        assert o + HE * TC <= 3072

        table = sb("table", [P, TILES, ROW])
        adst = sb("adst", [P, TILES, HEADS])
        targets = sb("targets", [P, TILES + 1], I32)
        std1 = sb("std1", [P, 2, 2 * PAIRS])
        vtok = sb("vtok", [P, 2, TILES])
        srow = sb("srow", [P, SROW])
        found_row = sb("found_row", [P, 2, TILES + 1])
        block_f = sb("block_f", [P, TILES + 1])
        block_i = sb("block_i", [P, TILES + 1], I32)
        place = sb("place", [P, TILES + 1])
        first = sb("first", [P, TILES + 1])
        bad = sb("bad", [P, 2, TILES])
        empty = sb("empty", [P, TILES])
        scat_f = sb("scat_f", [P, 2, TILES])
        scat_i = sb("scat_i", [P, 2, TILES], I32)
        prev = sb("prev", [P, BLK], I32)
        share = sb("share", [P, 16])
        share_i = sb("share_i", [P, NBLK + 1], I32)
        share_f = sb("share_f", [P, NBLK + 1])
        blocks_i = sb("blocks_i", [P, NBLK + 1], I32)
        group_i = sb("group_i", [P, NGROUP], I32)
        group_f = sb("group_f", [P, 2, NGROUP])
        border = sb("border", [P, 4])
        flags = sb("flags", [P, 4])
        pairs_f = sb("pairs_f", [1, 2])
        pairs_i = sb("pairs_i", [1, 1], I32)
        dfirst_i = sb("dfirst_i", [P, 1], I32)
        cidx_f = sb("cidx_f", [P, 1])
        cidx_i = sb("cidx_i", [P, 1], I32)
        dfirst = sb("dfirst", [P, HEADS])
        hidden = [state[n][:, :, :].rearrange("p t s -> p (t s)")[:, 0:CH] for n in range(2)]

        ident = sb("ident", [P, P])
        blockmean = sb("blockmean", [P, P])
        centring = sb("centring", [P, P])
        taps = sb("taps", [P, 9, P])
        ones = sb("ones", [P, P])
        halves = sb("halves", [P, 2])
        shift1 = sb("shift1", [P, P])
        shift2 = sb("shift2", [P, P])
        onesrow = sb("onesrow", [1, P])
        w3 = sb("w3", [P, 9])
        chan = sb("chan", [P, 3])
        half_s = sb("half_s", [P, 4])
        pow_i = sb("pow_i", [P, 2], I32)
        pad_i = sb("pad_i", [P, 2], I32)
        pad_t = sb("pad_t", [P, 6], I32)
        pad_f = sb("pad_f", [P, 2])
        signs_i = sb("signs_i", [P, 8], I32)
        signs = sb("signs", [P, 7])
        wgat = sb("wgat", [P, 2, HE])
        w1 = work[:, 3072:4096].rearrange("p (h e n) -> p h e n", h=2, e=EXP)
        b1 = sb("b1", [P, EXP])
        w2 = sb("w2", [P, EXP, C])
        b2 = sb("b2", [1, EXP * C])
        rowc = sb("rowc", [P, 5, HE])
        eps = sb("eps", [P, 3])

        psum = [ctx.enter_context(nc.psum_tensor(f"ps{n}", [P, 512], F32)) for n in range(8)]
        tr_ps = psum[0:4]
        ps_centre, ps_var, ps_conv, ps_h = psum[4:8]

        dests = keys[SORTED][:, :]
        onehot = [keys[1 - SORTED][:, n * GROUP * P:(n + 1) * GROUP * P] for n in range(2)]

        rn_flat = sources[:, 0:TILES * ST].bitcast(F32)
        last_rows = rn_flat.rearrange("p (t s) -> p t s", s=ST)
        carried = keys[0][:, 0:TILES * ST].rearrange("p (t s) -> p t s", s=ST)
        neutral = found_flat[:, 0:TILES * ST]
        zeros = same
        NH4 = TILES * HEADS
        nt = [keys[1][:, n * NH4:(n + 1) * NH4].rearrange("p (t h) -> p t h", h=HEADS) for n in range(8)]
        n16 = [ln2[:, n * TILES * HE:(n + 1) * TILES * HE].rearrange("p (t h e) -> p t h e", h=HEADS, e=EXP)
               for n in range(4)]
        gates = found_flat[:, 0:NH4].rearrange("p (e a h) -> p e a h", e=EXP, a=PAIRS)
        nsm = [found_flat[:, NH4 + n * TILES:NH4 + (n + 1) * TILES] for n in range(8)]
        tri, tri2 = (found_flat[:, 1024 + n * 768:1024 + (n + 1) * 768].rearrange("p (a t h) -> p a t h", a=3, h=HEADS)
                     for n in range(2))
        CHN = HEADS * (1 + EXP)
        cx = sb("cx", [P, 4, CHN])
        ct = found_flat[0:CHN, 0:12 * P].rearrange("p (a b) -> p a b", a=12)
        cback = sb("cback", [P, ST])

        names = ("edges_in x_in conv_in chan_in shifts_ready pad_in gat_in rows_in w1_in b1_in w2_in b2_in consts pool made "
                 "taps_made dve signs_ready keys_out keys_moved banks_moved ln1_centred ln1_squared ln1_var "
                 "ln1_std ln1_scale spread_ready acc_out refill_begun padded_ready conv_done x1_ready ln2_centred ln2_squared ln2_ready h_done "
                 "h_used vtok_ready vtok_std table_ready rows_out adst_out keysort_out sorted_ready counted total blocks_ready "
                 "shared_in shared width width_max pairs_ready dests_ready dests_out border_ready border_moved border_used onehot "
                 "sampled sampled_used dve_after edge_step edges_done states_out "
                 "block_ready found_in dfirst_in places_ready first_ready ends_ps idx_ready "
                 "zeros_ready zeros_out heads_out neutral_ready neutral_out gath0 gath1 head_in0 head_in1 "
                 "diffs_ready weights_ready state_ready state_out0 state_out1 "
                 "carry_x carry_t carry_diff carry_w carry_c carry_b carry_row carry_out carry_in carry_idx last_in "
                 "hid_ps hid_ready ex_ps ex_ready node_diff node_w node_var node_std top_ready top_exp "
                 "gated out_ps final out_done").split()
        s = {n: sem(n) for n in names}

        block = ctx.enter_context(nc.Block())

        @block.sync
        def _(sp):
            for n in range(2):
                sp.dma_start(keys[n][:, :].bitcast(I32), A["edge_index"][n].rearrange("(p t) -> p t", p=P)) \
                  .then_inc(s["edges_in"], 16)
            for h in range(2):
                sp.dma_start(x_sb[h * C:(h + 1) * C, :].rearrange("p (b s) -> p b s", b=HALF),
                             A["x"][h * HALF:(h + 1) * HALF].rearrange("b c i j -> c b (i j)")) \
                  .then_inc(s["x_in"], 16)
            for h in range(2):
                rows = slice(h * C, (h + 1) * C)
                sp.dma_start(w3[rows, :], A["weight"].rearrange("c a i j -> c (a i j)")).then_inc(s["conv_in"], 16)
                for n, name in enumerate(("bias", "scl_in", "srarh_shift")):
                    sp.dma_start(chan[rows, n:n + 1], A[name].rearrange("(c a) -> c a", a=1)).then_inc(s["chan_in"], 16)
            sp.dma_start(pad_i[:, :], A["pad"].bitcast(I32).rearrange("(a n) -> a n", a=1).broadcast_to([P, 2])) \
              .then_inc(s["pad_in"], 16)
            sp.wait_ge(s["consts"], 1)
            for h in range(2):
                rows = slice(h * C, (h + 1) * C)
                sp.dma_start(wgat[rows, h, :], A["W_gat"]).then_inc(s["gat_in"], 16)
                sp.dma_start(w1[rows, h, :, :], A["W1"].rearrange("e c n -> c e n")).then_inc(s["w1_in"], 16)
            for n, name in enumerate(("att_src", "att_dst")):
                sp.dma_start(rowc[:, n, :], A[name].rearrange("(a h) e -> a (h e)", a=1).broadcast_to([P, HE])) \
                  .then_inc(s["rows_in"], 16)
            for n, name in enumerate(("b_gat", "ln_gamma", "ln_beta")):
                sp.dma_start(rowc[:, 2 + n, :], A[name].rearrange("(a n) -> a n", a=1).broadcast_to([P, HE])) \
                  .then_inc(s["rows_in"], 16)
            with nc.allow_non_contiguous_dma(reason="small weights"):
                sp.dma_start(b1[:, :], A["b1"].rearrange("e n -> n e")).then_inc(s["b1_in"], 16)
            sp.dma_start(w2[:, :, :], A["W2"].rearrange("e n c -> n e c")).then_inc(s["w2_in"], 16)
            sp.dma_start(b2[:, :], A["b2"].rearrange("(a e) c -> a (e c)", a=1)).then_inc(s["b2_in"], 16)
            sp.wait_ge(s["zeros_ready"], 1)
            for rows, n in ((heads_d, HEADS), (state_d, ST)):
                sp.dma_start(rows.rearrange("(p t) h -> p (t h)", p=P).rearrange("p (a t) -> p a t", a=n),
                             zeros[:, :].rearrange("p (a t) -> p a t", a=1).broadcast_to([P, n, COLS])) \
                  .then_inc(s["zeros_out"], 16)
            sp.wait_ge(s["neutral_ready"], 1)
            sp.dma_start(carry_d.rearrange("(p t) s -> p (t s)", p=P), neutral).then_inc(s["neutral_out"], 16)
            sp.wait_ge(s["table_ready"], 1)
            sp.dma_start(rows_d.rearrange("(t p) r -> p t r", p=P), table[:, :, :]).then_inc(s["rows_out"], 16)
            sp.dma_start(adst_d.rearrange("(t p) r -> p t r", p=P), adst[:, :, :]).then_inc(s["adst_out"], 16)
            sp.wait_ge(s["sorted_ready"], 1)
            sp.dma_start(keys_d, keys[SORTED][:, :].bitcast(I32)).then_inc(s["keysort_out"], 16)
            sp.wait_ge(s["dests_ready"], 1)
            sp.dma_start(dests_d, dests).then_inc(s["dests_out"], 16)
            sp.wait_ge(s["pairs_ready"], 1)
            pairs = sp.value_load(pairs_i[0:1, 0:1], min_val=1, max_val=NPAIR)
            sp.wait_ge(s["heads_out"], 16 * TILES)
            heads_v = heads_d.rearrange("(p t) h -> p t h", p=P)
            state_v = state_d.rearrange("(p t) s -> p t s", p=P)
            for u in range(2):
                sp.dma_start(headrow[u][:, :, :], heads_v[:, u * TC:(u + 1) * TC, :]).then_inc(s[f"head_in{u}"], 16)
            with sp.Fori(0, NPAIR - 1) as i:
                with sp.If(i + 1 < pairs):
                    for u in range(2):
                        sp.wait_ge(s["state_ready"], i * 2 + (u + 1))
                        sp.dma_start(state_v[:, bass.ds(i * PAIRW + u * TC, TC), :], state[u][:, :, :]) \
                          .then_inc(s[f"state_out{u}"], 16)
                        sp.dma_start(headrow[u][:, :, :], heads_v[:, bass.ds(i * PAIRW + (u * TC + PAIRW), TC), :]) \
                          .then_inc(s[f"head_in{u}"], 16)
                with sp.Else():
                    pass
            sp.wait_ge(s["edges_done"], 1)
            for u in range(2):
                sp.dma_start(state_v[:, bass.ds(pairs * PAIRW + (u * TC - PAIRW), TC), :], state[u][:, :, :]) \
                  .then_inc(s[f"state_out{u}"], 16)
            for u in range(2):
                sp.wait_ge(s[f"state_out{u}"], pairs * 16)
            sp.sem_inc(s["states_out"], 1)
            sp.wait_ge(s["carry_out"], 16)
            sp.dma_start(carried, carry_d.rearrange("(t p) s -> p t s", p=P)).then_inc(s["carry_in"], 16)
            for c in range(NCH):
                sp.wait_ge(s["final"], c + 1)
                for h in range(2):
                    sp.dma_start(out[h * HALF + 2 * c:h * HALF + 2 * c + 2].rearrange("b c i j -> c b (i j)"),
                                 x_sb[h * C:(h + 1) * C, c * CH:(c + 1) * CH].rearrange("p (b s) -> p b s", b=2)) \
                      .then_inc(s["out_done"], 16)
            sp.wait_ge(s["out_done"], 16 * 2 * NCH)

        @block.gpsimd
        def _(pool):
            steps = [0]

            def settle(ins):
                steps[0] += 1
                ins.then_inc(s["pool"], 1)
                pool.wait_ge(s["pool"], steps[0])

            settle(pool.memset(wgat[:, :, :], 0.0))
            settle(pool.memset(w1, 0.0))
            settle(pool.iota(signs_i[:, 7:8], [[0, 1]], base=0, channel_multiplier=1))
            pool.iota(targets[:, :], [[P, TILES + 1]], base=0, channel_multiplier=1).then_inc(s["consts"], 1)
            pool.wait_ge(s["consts"], 1)
            for tile in (ident, shift1, shift2, blockmean):
                settle(pool.memset(tile[:, :], 0.0))
            settle(pool.memset(onesrow[:, :], 1.0))
            settle(pool.memset(ones[:, :], 1.0))
            settle(pool.memset(halves[:, :], 0.0))
            settle(pool.memset(halves[0:C, 0:1], 1.0 / C))
            settle(pool.memset(halves[C:P, 1:2], 1.0 / C))
            settle(pool.iota(share_i[:, :], [[1, NBLK + 1]], base=0, channel_multiplier=0))
            settle(pool.iota(group_i[:, :], [[GROUP * P, NGROUP]], base=0, channel_multiplier=0))
            settle(pool.iota(column, [[1, COLS]], base=0, channel_multiplier=0))
            settle(pool.iota(nodes1k, [[1, GROUP * P]], base=0, channel_multiplier=0))
            settle(pool.memset(blockmean[0:C, 0:C], 1.0 / C))
            settle(pool.memset(blockmean[C:P, C:P], 1.0 / C))
            settle(pool.memset(shift2[0:1, P - 1:P], 1.0))
            settle(pool.affine_select(out=ident[:, :], in_=ident[:, :], compare_op=ALU.not_equal, fill=1.0, base=0,
                                      pattern=[[-1, P]], channel_multiplier=1))
            settle(pool.affine_select(out=shift1[:, :], in_=shift1[:, :], compare_op=ALU.not_equal, fill=1.0, base=-1,
                                      pattern=[[-1, P]], channel_multiplier=1))
            pool.tensor_tensor(centring[:, :], ident[:, :], blockmean[:, :], ALU.subtract).then_inc(s["made"], 1)
            pool.wait_ge(s["conv_in"], 32)
            pool.wait_ge(s["made"], 1)
            for k in range(9):
                pool.tensor_scalar(taps[:, k, :], ident[:, :], w3[:, k:k + 1], None, ALU.mult).then_inc(s["taps_made"], 1)
                pool.wait_ge(s["taps_made"], k + 1)
            settle(pool.memset(neutral, 0.0))
            pool.memset(neutral.rearrange("p (t s) -> p t s", s=ST)[:, :, 0:HEADS], -BIG).then_inc(s["neutral_ready"], 1)
            pool.wait_ge(s["neutral_ready"], 1)

            half_b, inv_b = half_s[:, 0:1], pow_i[:, 1:2].bitcast(F32)

            def round_down(value):
                settle(pool.tensor_scalar(qb, value, MAGIC, MAGIC, ALU.add, ALU.subtract))
                settle(pool.tensor_tensor(qc, value, qb, ALU.subtract))
                settle(pool.tensor_scalar(qc, qc, 0.0, None, ALU.is_lt))
                settle(pool.tensor_tensor(qb, qb, qc, ALU.subtract))

            def requantise(c):
                cs = slice(c * CH, (c + 1) * CH)
                a = qa[c % 2]
                pool.wait_ge(s["acc_out"], c + 1)
                settle(pool.tensor_scalar(a, a, 32768.0, 2.0 ** -16, ALU.add, ALU.mult))
                round_down(a)
                settle(pool.tensor_tensor(a, a, qb, ALU.subtract))
                settle(pool.tensor_scalar(a, a, 65536.0, 32768.0, ALU.mult, ALU.subtract))
                settle(pool.tensor_scalar(a, a, chan[:, 1:2], 2.0 ** -15, ALU.mult, ALU.mult))
                settle(pool.tensor_scalar(a, a, 32768.0, 0.0, ALU.min, ALU.max))
                round_down(a)
                settle(pool.tensor_scalar(a, qb, half_b, inv_b, ALU.add, ALU.mult))
                round_down(a)
                settle(pool.tensor_scalar(qb, qb, 255.0, 32.0, ALU.min, ALU.subtract))
                pool.tensor_tensor(x_sb[:, cs], x_sb[:, cs], qb, ALU.add).then_inc(s["x1_ready"], 1)
                pool.wait_ge(s["x1_ready"], c + 1)

            pool.wait_ge(s["shifts_ready"], 1)
            for c in range(NCH):
                requantise(c)

            node_bound, edge_bound, block_bound = (pool.to_reg(n - 1) for n in (NODES, EDGES, P * NBLK))

            def gather_rows(u):
                for t in range(TC):
                    pool.indirect_dma_start(out=gathered[u][:, t, :], out_offset=None, in_=rows_d,
                                            in_offset=bass.IndirectOffsetOnAxis(ap=index[u][:, t:t + 1], axis=0),
                                            bounds_check=node_bound, oob_is_err=False).then_inc(s[f"gath{u}"], 16)

            key_blocks = keys_d.rearrange("p (a b) -> (p a) b", b=BLK)
            pool.wait_ge(s["keysort_out"], 16)
            pool.wait_ge(s["blocks_ready"], 1)
            for j in range(NBLK + 1):
                dst = keys[1 - SORTED][:, j * BLK:(j + 1) * BLK].bitcast(I32) if j < NBLK else prev[:, :]
                pool.indirect_dma_start(out=dst, out_offset=None, in_=key_blocks,
                                        in_offset=bass.IndirectOffsetOnAxis(ap=blocks_i[:, j:j + 1], axis=0),
                                        bounds_check=block_bound, oob_is_err=False).then_inc(s["shared_in"], 16)
            pool.wait_ge(s["rows_out"], 16)
            pool.wait_ge(s["adst_out"], 16)
            pool.wait_ge(s["idx_ready"], 1)
            pool.indirect_dma_start(out=dfirst[:, :], out_offset=None, in_=adst_d,
                                    in_offset=bass.IndirectOffsetOnAxis(ap=dfirst_i[:, :], axis=0),
                                    bounds_check=node_bound, oob_is_err=False).then_inc(s["dfirst_in"], 16)
            gather_rows(0)
            gather_rows(1)
            dest_blocks = dests_d.rearrange("p (a b) -> (p a) b", b=BLK)
            pool.wait_ge(s["dests_out"], 16)
            pool.wait_ge(s["block_ready"], 1)
            pool.wait_ge(s["neutral_out"], 16)
            for t in range(TILES + 1):
                pool.indirect_dma_start(out=found[:, t, :], out_offset=None, in_=dest_blocks,
                                        in_offset=bass.IndirectOffsetOnAxis(ap=block_i[:, t:t + 1], axis=0),
                                        bounds_check=block_bound, oob_is_err=False).then_inc(s["found_in"], 16)
            pool.wait_ge(s["zeros_out"], 32)
            pool.wait_ge(s["places_ready"], 1)
            for t in range(TILES):
                pool.indirect_dma_start(out=heads_d, in_=adst[:, t, :], in_offset=None,
                                        out_offset=bass.IndirectOffsetOnAxis(ap=scat_i[:, 0, t:t + 1], axis=0),
                                        bounds_check=edge_bound, oob_is_err=False).then_inc(s["heads_out"], 16)
            pairs = pool.value_load(pairs_i[0:1, 0:1], min_val=1, max_val=NPAIR)
            with pool.Fori(0, NPAIR - 1) as i:
                with pool.If(i + 1 < pairs):
                    for u in range(2):
                        pool.wait_ge(s["state_ready"], i * 2 + (u + 1))
                        pool.sem_inc(s["refill_begun"], 1)
                        gather_rows(u)
                with pool.Else():
                    pass
            pool.wait_ge(s["neutral_out"], 16)
            pool.wait_ge(s["carry_row"], 1)
            pool.indirect_dma_start(out=carry_d, in_=cback[:, :], in_offset=None,
                                    out_offset=bass.IndirectOffsetOnAxis(ap=cidx_i[:, :], axis=0),
                                    bounds_check=node_bound, oob_is_err=False).then_inc(s["carry_out"], 16)
            pool.wait_ge(s["states_out"], 1)
            for t in range(TILES):
                pool.indirect_dma_start(out=last_rows[:, t, :], out_offset=None, in_=state_d,
                                        in_offset=bass.IndirectOffsetOnAxis(ap=scat_i[:, 1, t:t + 1], axis=0),
                                        bounds_check=edge_bound, oob_is_err=False).then_inc(s["last_in"], 16)

        @block.tensor
        def _(pe):
            T = nc.tensor
            def expert_out(g, e):
                k = g * EXP + e
                pe.wait_ge(s["hid_ready"], k + 1)
                for j in range(4):
                    last = T.matmul(psum[2 + j // 2][:, (j % 2) * EXP * C + e * C:(j % 2) * EXP * C + (e + 1) * C],
                                    hidden[k % 2][:, j * P:(j + 1) * P], w2[:, e, :], start=False,
                                    stop=(e == EXP - 1), skip_group_check=True)
                last.then_inc(s["ex_ps"], 1)

            pe.wait_ge(s["made"], 1)
            pe.wait_ge(s["x_in"], 32)
            with pe.Fori(0, NCH) as i:
                pe.wait_ge(s["ln1_squared"], i)
                T.matmul(ps_centre[:, :], centring[:, :], x_sb[:, bass.ds(i * CH, CH)], start=True, stop=True) \
                    .then_inc(s["ln1_centred"], 1)
                pe.wait_ge(s["ln1_squared"], i + 1)
                pe.wait_ge(s["ln1_std"], i)
                for j in range(CH // P):
                    last = T.matmul(ps_var[:, 2 * j:2 * j + 2], square[:, j * P:(j + 1) * P], halves[:, :],
                                    start=True, stop=True)
                last.then_inc(s["ln1_var"], 1)
            pe.wait_ge(s["taps_made"], 9)
            pe.wait_ge(s["gat_in"], 32)
            wg = wgat[:, :, :].rearrange("p a n -> p (a n)")

            def conv(c):
                pe.wait_ge(s["padded_ready"], c + 1)
                if c >= 1:
                    pe.wait_ge(s["acc_out"], c)
                for k in range(9):
                    last = T.matmul(ps_conv[:, :], taps[:, k, :],
                                    padded[c % 2][:, :, k // 3:k // 3 + SIDE, k % 3:k % 3 + SIDE],
                                    start=(k == 0), stop=(k == 8))
                last.then_inc(s["conv_done"], 1)

            def spread(bank, scales):
                for j in range(CH // P):
                    for h in range(2):
                        last = T.matmul(bank[h * C:(h + 1) * C, j * P:(j + 1) * P], scales(j, h).broadcast_to([P, C]),
                                        ident[:, :], start=True, stop=True)
                last.then_inc(s["spread_ready"], 1)

            def spread1(c):
                pe.wait_ge(s["ln1_scale"], 1)
                if c >= 1:
                    pe.wait_ge(s["padded_ready"], c)
                spread(ps_var, lambda j, h: std1[:, 1, c * 8 + 2 * j + h:c * 8 + 2 * j + h + 1])

            def norm2(c):
                pe.wait_ge(s["x1_ready"], c + 1)
                if c == 0:
                    pe.wait_ge(s["ln1_std"], NCH)
                T.matmul(ps_centre[:, :], centring[:, :], x_sb[:, c * CH:(c + 1) * CH], start=True, stop=True) \
                    .then_inc(s["ln2_centred"], 1)
                pe.wait_ge(s["ln2_squared"], c + 1)
                if c >= 1:
                    pe.wait_ge(s["h_used"], c)
                for j in range(CH // P):
                    o = j * (2 * HE + 2)
                    T.matmul(ps_h[:, o:o + 2 * HE], ln2[:, c * CH + j * P:c * CH + (j + 1) * P], wg,
                             start=True, stop=True)
                    last = T.matmul(ps_h[:, o + 2 * HE:o + 2 * HE + 2], square2[:, j * P:(j + 1) * P], halves[:, :],
                                    start=True, stop=True)
                last.then_inc(s["h_done"], 1)

            spread1(0)
            for n in range(PASSES):
                pe.wait_ge(s["keys_out"], n + 1)
                src = keys[MOVES[n][0]]
                for b in range(4):
                    for j in range(4):
                        cs = (b * 4 + j) * P
                        last = T.transpose(tr_ps[b][:, j * P:(j + 1) * P], src[:, cs:cs + P], ident[:, :])
                    last.then_inc(s["keys_moved"], 1)
                if n < NCH:
                    conv(n)
                if n + 1 < NCH:
                    spread1(n + 1)
                if 2 <= n < NCH + 2:
                    norm2(n - 2)
                if n >= PASSES - 2:
                    pe.wait_ge(s["table_ready"], 1)
                    for c in range((n - PASSES + 2) * 4, (n - PASSES + 3) * 4):
                        if c >= 4:
                            pe.wait_ge(s["ln2_ready"], c - 3)
                        spread(psum[4 + c % 4], lambda j, h: vtok[:, 0, h * PAIRS + 4 * c + j:h * PAIRS + 4 * c + j + 1])

            pe.wait_ge(s["counted"], 1)
            T.matmul(ps_conv[:, 0:1], ones[:, :], share[:, 0:1], start=True, stop=True).then_inc(s["total"], 1)
            pe.wait_ge(s["banks_moved"], 4 * PASSES)
            pe.wait_ge(s["ln2_ready"], NCH)
            pe.wait_ge(s["w1_in"], 32)
            pe.wait_ge(s["w2_in"], 16)
            pe.wait_ge(s["b2_in"], 16)

            def experts_group(g):
                c, h = g // 2, g % 2
                if g >= 1:
                    pe.wait_ge(s["ex_ready"], 2 * g)
                for bank in range(2):
                    T.matmul(psum[2 + bank][:, :].rearrange("p (a n) -> p a n", a=2), onesrow[:, :],
                             b2[:, :].rearrange("p (a n) -> p a n", a=1).broadcast_to([1, 2, EXP * C]),
                             start=True, stop=False, skip_group_check=True)
                for e in range(EXP):
                    k = g * EXP + e
                    if k >= 2:
                        pe.wait_ge(s["hid_ready"], k - 1)
                    T.matmul(psum[k % 2][:, :], w1[:, h, e, :], ln2[:, c * CH:(c + 1) * CH], start=True, stop=True) \
                        .then_inc(s["hid_ps"], 1)
                    if e >= 1:
                        expert_out(g, e - 1)
                expert_out(g, EXP - 1)

            for g in range(EARLY):
                experts_group(g)
            pe.wait_ge(s["width"], 1)
            T.matmul(ps_conv[0:1, 128:256], srow[:, SROW - 1:SROW], ident[:, :], start=True, stop=True) \
                .then_inc(s["width_max"], 1)
            pe.wait_ge(s["border_ready"], 1)
            T.matmul(ps_conv[:, 0:3], shift1[:, :], border[:, 0:3], start=True, stop=True).then_inc(s["border_moved"], 1)
            for c in range(NGROUP):
                tiles = GROUP if c < NGROUP - 1 else 1
                pe.wait_ge(s["onehot"], c + 1)
                if c == 2:
                    pe.wait_ge(s["border_used"], 1)
                if c >= 4:
                    pe.wait_ge(s["sampled_used"], c - 3)
                for j in range(tiles):
                    last = T.matmul(psum[4 + c % 4][:, j * SROW:(j + 1) * SROW],
                                    onehot[c % 2][:, j * P:(j + 1) * P], srow[:, :], start=True, stop=True)
                last.then_inc(s["sampled"], 1)

            for g in range(EARLY, 2 * NCH):
                experts_group(g)

            pe.wait_ge(s["first_ready"], 1)
            T.matmul(ps_h[:, 0:TILES], shift1[:, :], first[:, 0:TILES], start=True, stop=False)
            T.matmul(ps_h[:, 0:TILES], shift2[:, :], first[:, 1:TILES + 1], start=False, stop=True) \
                .then_inc(s["ends_ps"], 1)

            pe.wait_ge(s["carry_x"], 1)
            for n in range(4):
                last = T.transpose(ps_centre[0:CHN, n * P:(n + 1) * P], cx[:, n, :], ident[:, :])
            last.then_inc(s["carry_t"], 1)
            pe.wait_ge(s["carry_c"], 1)
            for n in range(2):
                last = T.transpose(ps_var[:, n * 32:n * 32 + CHN], ct[:, 10 + n, :], ident[0:CHN, 0:CHN])
            last.then_inc(s["carry_b"], 1)

            for c in range(NCH):
                pe.wait_ge(s["gated"], c + 1)
                if c >= 2:
                    pe.wait_ge(s["final"], c - 1)
                for j in range(CH // P):
                    for e in range(EXP):
                        last = T.matmul(psum[c % 2][:, j * P:(j + 1) * P], experts[:, c * 4 + j, e, :], ident[:, :],
                                        start=(e == 0), stop=(e == EXP - 1))
                last.then_inc(s["out_ps"], 1)

        @block.scalar
        def _(act):
            N = nc.scalar
            act.wait_ge(s["signs_ready"], 1)
            with act.Fori(0, NCH) as i:
                act.wait_ge(s["ln1_centred"], i + 1)
                N.activation(centred[:, bass.ds(i * CH, CH)], ps_centre[:, :], ACT.Copy)
                N.activation(square, ps_centre[:, :], ACT.Square).then_inc(s["ln1_squared"], 1)
                act.wait_ge(s["ln1_var"], i + 1)
                N.activation(std1[:, 0, bass.ds(i * 8, 8)], ps_var[:, 0:8], ACT.Sqrt, bias=eps[:, 0:1]) \
                 .then_inc(s["ln1_std"], 1)
            for n in range(PASSES):
                dst = keys[MOVES[n][1]]
                for b in range(4):
                    act.wait_ge(s["keys_moved"], 4 * n + b + 1)
                    sign = 1.0 if MOVES[n][2] is None else signs[:, MOVES[n][2]:MOVES[n][2] + 1]
                    N.activation(dst[:, b * 512:(b + 1) * 512], tr_ps[b][:, :], ACT.Copy, scale=sign) \
                     .then_inc(s["banks_moved"], 1)
                if n < NCH:
                    act.wait_ge(s["conv_done"], n + 1)
                    if n == 0:
                        act.wait_ge(s["chan_in"], 16 * 6)
                    if n >= 2:
                        act.wait_ge(s["x1_ready"], n - 1)
                    N.activation(qa[n % 2], ps_conv[:, :], ACT.Identity, bias=chan[:, 0:1]).then_inc(s["acc_out"], 1)
                if 2 <= n < NCH + 2:
                    c = n - 2
                    act.wait_ge(s["ln2_centred"], c + 1)
                    N.activation(ln2[:, c * CH:(c + 1) * CH], ps_centre[:, :], ACT.Copy)
                    N.activation(square2, ps_centre[:, :], ACT.Square).then_inc(s["ln2_squared"], 1)
                if n == NCH + 2:
                    act.wait_ge(s["vtok_ready"], 1)
                    N.activation(vtok[:, 1, :], vtok[:, 0, :], ACT.Sqrt, bias=eps[:, 1:2]).then_inc(s["vtok_std"], 1)
            act.wait_ge(s["b1_in"], 16)
            act.wait_ge(s["table_ready"], 1)
            act.wait_ge(s["ln2_ready"], NCH)
            for g in range(2 * NCH):
                c, h = g // 2, g % 2
                for e in range(EXP):
                    k = g * EXP + e
                    act.wait_ge(s["hid_ps"], k + 1)
                    if k >= 2:
                        act.wait_ge(s["ex_ps"], k - 1)
                    N.activation(hidden[k % 2], psum[k % 2][:, :], ACT.Gelu, bias=b1[:, e:e + 1]) \
                     .then_inc(s["hid_ready"], 1)
                act.wait_ge(s["ex_ps"], (g + 1) * EXP)
                for bank in range(2):
                    pair = 4 * c + 2 * bank
                    N.activation(experts[:, pair:pair + 2, :, h * C:(h + 1) * C],
                                 psum[2 + bank][:, :].rearrange("p (a e n) -> p a e n", a=2, e=EXP), ACT.Copy) \
                     .then_inc(s["ex_ready"], 1)
            act.wait_ge(s["pairs_ready"], 1)
            pairs = act.value_load(pairs_i[0:1, 0:1], min_val=1, max_val=NPAIR)
            with act.Fori(0, NPAIR) as i:
                with act.If(i < pairs):
                    for u in range(2):
                        act.wait_ge(s["diffs_ready"], i * 2 + (u + 1))
                        N.activation(weight, diff, ACT.Exp).then_inc(s["weights_ready"], 1)
                with act.Else():
                    pass
            act.wait_ge(s["carry_diff"], 1)
            N.activation(ct[:, 6:8, :], ct[:, 4:6, :], ACT.Exp).then_inc(s["carry_w"], 1)
            act.wait_ge(s["node_diff"], 1)
            N.activation(tri2, tri, ACT.Exp).then_inc(s["node_w"], 1)
            act.wait_ge(s["node_var"], 1)
            N.activation(nsm[1], nsm[0], ACT.Sqrt, bias=eps[:, 2:3], scale=1.0 / HE).then_inc(s["node_std"], 1)
            act.wait_ge(s["top_ready"], 1)
            N.activation(nt[5], nt[4], ACT.Exp).then_inc(s["top_exp"], 1)

        @block.vector
        def _(dve):
            V = nc.vector
            done = [0]

            def link(ins):
                done[0] += 1
                ins.then_inc(s["dve"], 1)
                dve.wait_ge(s["dve"], done[0])

            V.memset(zeros[:, :], 0.0).then_inc(s["zeros_ready"], 1)
            V.memset(eps[:, 0:1], LN1_EPS)
            V.memset(eps[:, 1:2], LN2_EPS)
            V.memset(eps[:, 2:3], LN3_EPS)
            V.memset(sources[:, COLS:COLS + PAIRW], 0)
            dve.wait_ge(s["consts"], 1)
            for b in range(7):
                ins = V.tensor_scalar(signs_i[:, b:b + 1], signs_i[:, 7:8], b, 1, ALU.logical_shift_right, ALU.bitwise_and)
            link(ins)
            V.tensor_scalar(signs[:, :], signs_i[:, 0:7], -2.0, 1.0, ALU.mult, ALU.add).then_inc(s["signs_ready"], 1)

            dve.wait_ge(s["edges_in"], 32)
            src_i, dst_i = keys[0][:, :].bitcast(I32), keys[1][:, :].bitcast(I32)
            V.tensor_scalar(src_i, src_i, float(NODES - 1), 0.0, ALU.min, ALU.max)
            link(V.tensor_scalar(dst_i, dst_i, float(NODES), 0.0, ALU.min, ALU.max))
            link(V.tensor_scalar(dst_i, dst_i, SRC_BITS, KEY_ONE, ALU.logical_shift_left, ALU.bitwise_or))
            link(V.tensor_tensor(src_i, src_i, dst_i, ALU.bitwise_or))
            link(V.tensor_scalar(keys[0][:, :], keys[0][:, :], signs[:, 0:1], None, ALU.mult))

            dve.wait_ge(s["pad_in"], 16)
            lo, hi = pad_i[:, 0:1], pad_i[:, 1:2]
            pt = [pad_t[:, n:n + 1] for n in range(6)]
            V.tensor_scalar(pt[0], hi, 20, 0x7FF, ALU.logical_shift_right, ALU.bitwise_and)
            V.tensor_scalar(pt[1], hi, 0xFFFFF, 3, ALU.bitwise_and, ALU.logical_shift_left)
            V.tensor_scalar(pt[2], lo, 29, 7, ALU.logical_shift_right, ALU.bitwise_and)
            V.tensor_scalar(pt[3], lo, 28, 1, ALU.logical_shift_right, ALU.bitwise_and)
            link(V.tensor_scalar(pt[4], hi, 31, 31, ALU.logical_shift_right, ALU.logical_shift_left))
            V.tensor_scalar(pad_f[:, 1:2], pt[0], float(1023 - 127), None, ALU.is_gt)
            link(V.tensor_scalar(pt[0], pt[0], -float(1023 - 127), 0.0, ALU.add, ALU.max))
            link(V.tensor_scalar(pt[0], pt[0], 255.0, None, ALU.min))
            link(V.tensor_scalar(pt[0], pt[0], 23, None, ALU.logical_shift_left))
            link(V.tensor_tensor(pt[1], pt[1], pt[2], ALU.bitwise_or))
            link(V.tensor_tensor(pt[1], pt[1], pt[0], ALU.bitwise_or))
            link(V.tensor_tensor(pt[1], pt[1], pt[3], ALU.add))
            link(V.tensor_tensor(pt[1], pt[1], pt[4], ALU.bitwise_or))
            link(V.tensor_tensor(pad_f[:, 0:1], pt[1].bitcast(F32), pad_f[:, 1:2], ALU.mult))
            for n in range(2):
                link(V.memset(padded[n], 0.0))
                link(V.tensor_scalar(padded[n], padded[n], pad_f[:, 0:1], None, ALU.add))

            dve.wait_ge(s["chan_in"], 16 * 6)
            sh = chan[:, 2:3]
            V.tensor_scalar(half_s[:, 2:3], sh, 0.0, None, ALU.is_gt)
            V.tensor_scalar(pow_i[:, 0:1], sh, 126.0, float(1 << 23), ALU.add, ALU.mult)
            link(V.tensor_scalar(pow_i[:, 1:2], sh, -127.0, -float(1 << 23), ALU.add, ALU.mult))
            V.tensor_tensor(half_s[:, 0:1], pow_i[:, 0:1].bitcast(F32), half_s[:, 2:3], ALU.mult).then_inc(s["shifts_ready"], 1)

            def stage(src, dst, k, j, signal=None):
                def end(ins):
                    link(ins) if signal is None else ins.then_inc(s[signal], 1)

                if k is None:
                    a = src[:, :].rearrange("p (n t j) -> p n t j", t=2, j=j)
                    b = dst[:, :].rearrange("p (n t j) -> p n t j", t=2, j=j)
                    V.tensor_tensor(b[:, :, 0, :], a[:, :, 0, :], a[:, :, 1, :], ALU.min)
                    end(V.tensor_tensor(b[:, :, 1, :], a[:, :, 0, :], a[:, :, 1, :], ALU.max))
                    return
                a = src[:, :].rearrange("p (g d n t j) -> p g d n t j", d=2, n=k // (2 * j), t=2, j=j)
                b = dst[:, :].rearrange("p (g d n t j) -> p g d n t j", d=2, n=k // (2 * j), t=2, j=j)
                for d in range(2):
                    low, high = (ALU.min, ALU.max) if d == 0 else (ALU.max, ALU.min)
                    V.tensor_tensor(b[:, :, d, :, 0, :], a[:, :, d, :, 0, :], a[:, :, d, :, 1, :], low)
                    ins = V.tensor_tensor(b[:, :, d, :, 1, :], a[:, :, d, :, 0, :], a[:, :, d, :, 1, :], high)
                end(ins)

            def norm1(c):
                cs = slice(c * CH, (c + 1) * CH)
                if c == 0:
                    dve.wait_ge(s["ln1_std"], NCH)
                    V.reciprocal(std1[:, 1, :], std1[:, 0, :]).then_inc(s["ln1_scale"], 1)
                dve.wait_ge(s["spread_ready"], c + 1)
                if c >= 2:
                    dve.wait_ge(s["conv_done"], c - 1)
                V.tensor_tensor(padded[c % 2][:, :, 1:1 + SIDE, 1:1 + SIDE],
                                centred[:, cs].rearrange("p (b r c) -> p b r c", b=2, r=SIDE),
                                ps_var[:, :].rearrange("p (b r c) -> p b r c", b=2, r=SIDE), ALU.mult) \
                 .then_inc(s["padded_ready"], 1)
                dve.wait_ge(s["padded_ready"], c + 1)

            def round_down(dst, scratch, value, scalar, op):
                link(V.tensor_scalar(scratch, value, scalar, MAGIC, op, ALU.add))
                link(V.tensor_scalar(scratch, scratch, MAGIC, None, ALU.subtract))
                link(V.scalar_tensor_tensor(out=dst, in0=value, scalar=scalar, in1=scratch, op0=op, op1=ALU.is_lt))
                link(V.tensor_tensor(dst, scratch, dst, ALU.subtract))

            def norm2(c):
                cs = slice(c * CH, (c + 1) * CH)
                dve.wait_ge(s["spread_ready"], NCH + c + 1)
                V.tensor_tensor(ln2[:, cs], ln2[:, cs], psum[4 + c % 4][:, :], ALU.mult).then_inc(s["ln2_ready"], 1)
                dve.wait_ge(s["ln2_ready"], c + 1)

            def keep_rows(c):
                dve.wait_ge(s["h_done"], c + 1)
                hp = ps_h[:, 0:CH // P * (2 * HE + 2)].rearrange("p (j n) -> p j n", n=2 * HE + 2)
                for h in range(2):
                    t0 = h * PAIRS + 4 * c
                    V.tensor_copy(table[:, t0:t0 + 4, 0:HE], hp[:, :, h * HE:(h + 1) * HE])
                    ins = V.tensor_copy(vtok[:, 0, t0:t0 + 4], hp[:, :, 2 * HE + h])
                ins.then_inc(s["h_used"], 1)

            def attention_terms():
                dve.wait_ge(s["rows_in"], 16 * 5)
                dve.wait_ge(s["vtok_std"], 1)
                link(V.reciprocal(vtok[:, 0, :], vtok[:, 1, :]))
                link(V.tensor_tensor(table[:, :, 0:HE], table[:, :, 0:HE],
                                     vtok[:, 0, :].rearrange("p (t a) -> p t a", a=1).broadcast_to([P, TILES, HE]), ALU.mult))
                prod = [ex_flat[:, n * TILES * HE:(n + 1) * TILES * HE] for n in range(2)]
                for n in range(2):
                    ins = V.tensor_tensor(prod[n].rearrange("p (t n) -> p t n", n=HE), table[:, :, 0:HE],
                                          rowc[:, n:n + 1, :].broadcast_to([P, TILES, HE]), ALU.mult)
                link(ins)
                V.tensor_reduce(table[:, :, HE:ROW], prod[0].rearrange("p (t h e) -> p t h e", h=HEADS, e=EXP),
                                AX.X, ALU.add)
                V.tensor_reduce(adst[:, :, :], prod[1].rearrange("p (t h e) -> p t h e", h=HEADS, e=EXP),
                                AX.X, ALU.add).then_inc(s["table_ready"], 1)

            def move(n):
                if n < NCH:
                    norm1(n)
                if 3 <= n < NCH + 3:
                    keep_rows(n - 3)
                if n == NCH + 2:
                    dve.wait_ge(s["h_used"], NCH)
                    V.tensor_copy(vtok[:, 1, :], vtok[:, 0, :]).then_inc(s["vtok_ready"], 1)
                if n == NCH + 3:
                    attention_terms()
                if n >= PASSES - 2:
                    for c in range((n - PASSES + 2) * 4, (n - PASSES + 3) * 4):
                        norm2(c)
                dve.wait_ge(s["banks_moved"], 4 * (n + 1))

            at, n = 0, 0
            for level in range(1, LOG_COLS + 1):
                for bit in range(level - 1, -1, -1):
                    k = None if level == LOG_COLS else 1 << level
                    stage(keys[at], keys[1 - at], k, 1 << bit)
                    at = 1 - at
            for level in LEVELS_T:
                V.tensor_scalar(keys[at][:, :], keys[at][:, :], signs[:, level - 1 - LOG_COLS:level - LOG_COLS], None,
                                ALU.mult).then_inc(s["keys_out"], 1)
                assert MOVES[n][0] == at and MOVES[n][1] == 1 - at
                move(n)
                n, at = n + 1, 1 - at
                for bit in range(level - LOG_COLS - 1, -1, -1):
                    k = None if level == LOG_EDGES else 1 << (level - LOG_COLS)
                    stage(keys[at], keys[1 - at], k, 1 << bit, None if bit else "keys_out")
                    at = 1 - at
                assert MOVES[n][0] == at and MOVES[n][1] == 1 - at
                move(n)
                n, at = n + 1, 1 - at
                for bit in range(LOG_COLS - 1, -1, -1):
                    last = level == LOG_EDGES and bit == 0
                    stage(keys[at], keys[1 - at], None, 1 << bit, "sorted_ready" if last else None)
                    at = 1 - at
            assert at == SORTED
            dve.wait_ge(s["sorted_ready"], 1)
            sk = keys[at][:, :].bitcast(I32)
            other = keys[1 - at][:, :].bitcast(I32)

            link(V.tensor_scalar(keys[1 - at][:, :], keys[at][:, :], KEY_END, None, ALU.is_lt, ALU.add,
                                 accum_out=share[:, 1:2]))
            V.tensor_copy(share[:, 0:1], share[:, 1:2]).then_inc(s["counted"], 1)
            V.tensor_copy(share_f[:, :], share_i[:, :])
            V.tensor_copy(share[:, 2:3], signs_i[:, 7:8])
            dve.wait_ge(s["total"], 1)
            link(V.tensor_scalar(share[:, 3:4], ps_conv[:, 0:1], float(P * BLK - 1), 1.0 / (P * BLK), ALU.add, ALU.mult))
            round_down(share[:, 4:5], share[:, 5:6], share[:, 3:4], 1.0, ALU.mult)
            link(V.tensor_scalar(share[:, 4:5], share[:, 4:5], 1.0, None, ALU.max))
            V.tensor_scalar(share[:, 7:8], share[:, 4:5], float(BLK), None, ALU.mult)
            link(V.tensor_tensor(share[:, 6:7], share[:, 4:5], share[:, 2:3], ALU.mult))
            V.tensor_scalar(blocks_i[:, 0:NBLK], share_f[:, 0:NBLK], share[:, 6:7], float(P * NBLK - 1), ALU.add, ALU.min)
            V.tensor_scalar(blocks_i[:, NBLK:NBLK + 1], share[:, 6:7], -1.0, 0.0, ALU.add, ALU.max) \
             .then_inc(s["blocks_ready"], 1)
            dve.wait_ge(s["shared_in"], 16 * (NBLK + 1))
            dve.wait_ge(s["blocks_ready"], 1)
            own = keys[1 - at]
            own_i = own[:, :].bitcast(I32)
            kept = sources[:, 0:COLS].bitcast(F32)
            real = same
            far = [keys[at][:, :].bitcast(I32), found_flat[:, 0:COLS].bitcast(I32)]
            moves = found_flat[:, COLS:2 * COLS].bitcast(I32)
            dve.wait_ge(s["neutral_out"], 16)
            dve.wait_ge(s["zeros_out"], 32)
            dve.wait_ge(s["keysort_out"], 16)
            link(V.tensor_scalar(kept, column, share[:, 7:8], None, ALU.is_lt))
            link(V.scalar_tensor_tensor(out=real[:, :], in0=own[:, :], scalar=KEY_END, in1=kept,
                                        op0=ALU.is_lt, op1=ALU.mult, accum_out=share[:, 8:9]))
            V.tensor_copy(kept[:, 0:1], real[:, 0:1])
            link(V.tensor_tensor(kept[:, 1:COLS], own[:, 1:COLS], own[:, 0:COLS - 1], ALU.not_equal))
            link(V.tensor_tensor(kept[:, 1:COLS], kept[:, 1:COLS], real[:, 1:COLS], ALU.mult))
            link(V.tensor_tensor_scan(times[:, :], ones[:, 0:1].broadcast_to([P, COLS]), kept, 0.0, ALU.mult, ALU.add))
            V.tensor_copy(srow[:, SROW - 1:SROW], times[:, COLS - 1:COLS]).then_inc(s["width"], 1)
            link(V.scalar_tensor_tensor(out=real[:, :], in0=column, scalar=1.0, in1=times[:, :], op0=ALU.add, op1=ALU.subtract))
            link(V.tensor_tensor(far[0], real[:, :], kept, ALU.mult))
            f = 0
            for b in range(LOG_COLS):
                k = 1 << b
                link(V.tensor_scalar(moves, far[f], k, None, ALU.bitwise_and))
                V.copy_predicated(own_i[:, 0:COLS - k], moves[:, k:COLS], own_i[:, k:COLS])
                link(V.scalar_tensor_tensor(out=far[1 - f], in0=moves, scalar=0.0, in1=far[f], op0=ALU.is_equal, op1=ALU.mult))
                link(V.copy_predicated(far[1 - f][:, 0:COLS - k], moves[:, k:COLS], far[f][:, k:COLS]))
                f = 1 - f
            dve.wait_ge(s["width_max"], 1)
            link(V.tensor_reduce(pairs_f[:, 0:1], ps_conv[0:1, 128:256], AX.X, ALU.max))
            link(V.tensor_scalar(pairs_f[:, 0:1], pairs_f[:, 0:1], float(PAIRW - 1), 1.0 / PAIRW, ALU.add, ALU.mult))
            link(V.tensor_scalar(pairs_f[:, 0:1], pairs_f[:, 0:1], (1.0 / PAIRW - 1.0) / 2.0, MAGIC, ALU.add, ALU.add))
            link(V.tensor_scalar(pairs_f[:, 0:1], pairs_f[:, 0:1], MAGIC, 1.0, ALU.subtract, ALU.max))
            V.tensor_copy(pairs_i[:, :], pairs_f[:, 0:1]).then_inc(s["pairs_ready"], 1)
            width = srow[:, SROW - 1:SROW]
            within, behind_v = far[1 - f].bitcast(F32), moves.bitcast(F32)
            link(V.tensor_scalar(sources[:, 0:COLS], own_i, NODES - 1, None, ALU.bitwise_and))
            for u in range(2):
                V.tensor_copy(index[u][:, :], sources[:, u * TC:(u + 1) * TC])
            V.tensor_scalar(own_i, own_i, SRC_BITS, (1 << (SRC_BITS + 2)) - 1, ALU.logical_shift_right, ALU.bitwise_and)
            link(V.tensor_scalar(within, column, width, None, ALU.is_lt))
            V.scalar_tensor_tensor(out=real[:, :], in0=far[f], scalar=share[:, 8:9], in1=column, op0=ALU.subtract, op1=ALU.add)
            link(V.tensor_scalar(behind_v, within, -DROPPED, DROPPED, ALU.mult, ALU.add))
            link(V.tensor_tensor(real[:, :], real[:, :], within, ALU.mult))
            V.tensor_tensor(times[:, 0:COLS - 1], real[:, 1:COLS], real[:, 0:COLS - 1], ALU.subtract)
            V.tensor_scalar(times[:, COLS - 1:COLS], real[:, COLS - 1:COLS], -1.0, None, ALU.mult)
            V.tensor_tensor(dests, own_i, behind_v, ALU.max).then_inc(s["dests_ready"], 1)
            dve.wait_ge(s["dests_ready"], 1)
            V.tensor_scalar(dfirst_i[:, :], dests[:, 0:1], float(NODES - 1), None, ALU.min).then_inc(s["idx_ready"], 1)
            V.tensor_scalar(srow[:, 0:NSAMP], dests.rearrange("p (a b) -> p a b", b=BLK)[:, 1:NBLK, 0], 0.0, None, ALU.add)
            V.tensor_scalar(srow[:, NSAMP:NSAMP + 1], share[:, 2:3], float(COLS), None, ALU.mult)
            V.tensor_copy(border[:, 3:4], dests[:, 0:1])
            V.tensor_scalar(share[:, 9:10], share[:, 2:3], 0.0, None, ALU.is_gt)
            link(V.tensor_scalar(prev[:, 0:1], prev[:, BLK - 1:BLK], SRC_BITS, (1 << (SRC_BITS + 2)) - 1,
                                 ALU.logical_shift_right, ALU.bitwise_and))
            V.tensor_copy(border[:, 1:2], prev[:, 0:1])
            V.tensor_scalar(border[:, 2:3], border[:, 3:4], -2.0 * DROPPED, None, ALU.add)
            link(V.tensor_tensor(flags[:, 0:1], border[:, 3:4], prev[:, 0:1], ALU.is_equal))
            link(V.tensor_tensor(flags[:, 0:1], flags[:, 0:1], share[:, 9:10], ALU.mult))
            V.tensor_copy(border[:, 0:1], flags[:, 0:1]).then_inc(s["border_ready"], 1)
            link(V.tensor_tensor(same[:, 1:COLS], dests[:, 1:COLS], dests[:, 0:COLS - 1], ALU.is_equal))
            V.memset(same[:, 0:1], 1.0)
            link(V.scalar_tensor_tensor(out=same[:, 1:COLS], in0=behind_v[:, 1:COLS], scalar=0.0, in1=same[:, 1:COLS],
                                        op0=ALU.is_gt, op1=ALU.max))
            dve.wait_ge(s["border_moved"], 1)
            V.tensor_copy(flags[:, 2:3], ps_conv[:, 0:1])
            V.tensor_tensor(flags[:, 1:2], border[:, 3:4], ps_conv[:, 1:2], ALU.is_equal)
            link(V.tensor_scalar(share[:, 10:11], ps_conv[:, 2:3], 2.0 * DROPPED, None, ALU.add))
            link(V.tensor_tensor(cidx_f[:, :], flags[:, 1:2], flags[:, 2:3], ALU.mult))
            link(V.tensor_scalar(cidx_f[:, :], cidx_f[:, :], -1.0, 1.0, ALU.mult, ALU.add))
            link(V.tensor_tensor(cidx_f[:, :], cidx_f[:, :], flags[:, 0:1], ALU.mult))
            link(V.tensor_scalar(cidx_f[:, :], cidx_f[:, :], -float(FAR), float(FAR), ALU.mult, ALU.add))
            link(V.tensor_tensor(cidx_f[:, :], cidx_f[:, :], border[:, 3:4], ALU.add))
            link(V.tensor_copy(cidx_i[:, :], cidx_f[:, :]))

            V.memset(border[0:1, 3:4], -1.0)
            link(V.tensor_copy(group_f[:, 1, :], group_i[:, :]))
            V.tensor_tensor(group_f[:, 0, :], border[:, 3:4].broadcast_to([P, NGROUP]), group_f[:, 1, :], ALU.subtract)
            link(V.tensor_scalar(share[:, 11:12], share[:, 10:11], 0.0, None, ALU.add))
            ins = V.tensor_tensor(group_f[:, 1, :], share[:, 11:12].broadcast_to([P, NGROUP]), group_f[:, 1, :], ALU.subtract)
            ins.then_inc(s["border_used"], 1)
            dve.wait_ge(s["border_used"], 1)
            above = found_flat[:, 0:GROUP * P]

            def count_samples(c):
                tiles = GROUP if c < NGROUP - 1 else 1
                ts = slice(c * GROUP, c * GROUP + tiles)
                dve.wait_ge(s["sampled"], c + 1)
                ps = psum[4 + c % 4][:, 0:tiles * SROW].rearrange("p (t n) -> p t n", n=SROW)
                cmp = found_flat[:, 2048:2048 + tiles * NSAMP].rearrange("p (t n) -> p t n", n=NSAMP)
                V.tensor_copy(found_row[:, 0, ts], ps[:, :, NSAMP])
                V.tensor_copy(found_row[:, 1, ts], ps[:, :, NSAMP + 1])
                V.tensor_tensor(cmp, ps[:, :, 0:NSAMP],
                                targets[:, ts].rearrange("p (t a) -> p t a", a=1).broadcast_to([P, tiles, NSAMP]),
                                ALU.is_lt).then_inc(s["sampled_used"], 1)
                dve.wait_ge(s["sampled_used"], c + 1)
                link(V.tensor_reduce(block_f[:, ts], cmp, AX.X, ALU.add))

            for c in range(NGROUP):
                n = GROUP * P if c < NGROUP - 1 else P
                if c >= 2:
                    dve.wait_ge(s["sampled"], c - 1)
                link(V.tensor_scalar(above[:, 0:n], nodes1k[:, 0:n], group_f[:, 1, c:c + 1], None, ALU.is_gt))
                V.scalar_tensor_tensor(out=onehot[c % 2][:, 0:n], in0=nodes1k[:, 0:n], scalar=group_f[:, 0, c:c + 1],
                                       in1=above[:, 0:n], op0=ALU.is_gt, op1=ALU.subtract).then_inc(s["onehot"], 1)
                dve.wait_ge(s["onehot"], c + 1)
                if c >= 1:
                    count_samples(c - 1)
            count_samples(NGROUP - 1)
            link(V.tensor_scalar(place[:, :], found_row[:, 0, :], 1.0 / BLK, None, ALU.mult))
            link(V.tensor_tensor(place[:, :], place[:, :], block_f[:, :], ALU.add))
            V.tensor_copy(block_i[:, :], place[:, :]).then_inc(s["block_ready"], 1)
            dve.wait_ge(s["block_ready"], 1)
            dve.wait_ge(s["found_in"], 16 * (TILES + 1))
            link(V.tensor_tensor(found[:, :, :], found[:, :, :],
                                 targets[:, :].rearrange("p (t a) -> p t a", a=1).broadcast_to([P, TILES + 1, BLK]), ALU.is_lt))
            link(V.tensor_reduce(place[:, :], found[:, :, :], AX.X, ALU.add))
            link(V.scalar_tensor_tensor(out=place[:, :], in0=block_f[:, :], scalar=float(BLK), in1=place[:, :],
                                        op0=ALU.mult, op1=ALU.add))
            V.tensor_tensor(first[:, :], place[:, :], found_row[:, 0, :], ALU.add).then_inc(s["first_ready"], 1)
            dve.wait_ge(s["ends_ps"], 1)
            end = ps_h[:, 0:TILES]
            link(V.tensor_tensor(empty[:, :], end, first[:, 0:TILES], ALU.is_equal))
            V.scalar_tensor_tensor(out=bad[:, 0, :], in0=place[:, 0:TILES], scalar=0.0, in1=empty[:, :],
                                   op0=ALU.is_equal, op1=ALU.max)
            link(V.tensor_tensor(bad[:, 1, :], place[:, 0:TILES], found_row[:, 1, 0:TILES], ALU.is_equal))
            link(V.tensor_tensor(bad[:, 0, :], bad[:, 0, :], bad[:, 1, :], ALU.max))
            V.scalar_tensor_tensor(out=scat_f[:, 0, :], in0=bad[:, 0, :], scalar=float(FAR), in1=first[:, 0:TILES],
                                   op0=ALU.mult, op1=ALU.add)
            link(V.tensor_scalar(scat_f[:, 1, :], end, -1.0, 0.0, ALU.add, ALU.max))
            V.tensor_copy(scat_i[:, :, :], scat_f[:, :, :]).then_inc(s["places_ready"], 1)

            dve.wait_ge(s["ex_ready"], 4 * NCH)
            dve.wait_ge(s["dfirst_in"], 16)
            V.tensor_copy(adst_e[1][:, :, TC - 1], dfirst[:, :])
            V.memset(top_e[1][:, :, TC:TC + 1], 0.0)
            V.memset(state[1][:, TC - 1, HEADS:ST], 0.0)
            link(V.memset(state[1][:, TC - 1, 0:HEADS], -BIG))

            STEPS = 8
            pairs = dve.value_load(pairs_i[0:1, 0:1], min_val=1, max_val=NPAIR)

            def edge_chunk(i, u):
                off = i * PAIRW + u * TC
                step = [0]

                def after(ins):
                    step[0] += 1
                    ins.then_inc(s["edge_step"], 1)
                    dve.wait_ge(s["edge_step"], i * (2 * STEPS) + (u * STEPS + step[0]))

                g, st, last = gathered[u], state[u], 1 - u
                ad, top = adst_e[u], top_e[u]
                sm, mult = same[:, bass.ds(off, TC)], times[:, bass.ds(off, TC)]

                def by_head(row):
                    return row.rearrange("p (a t) -> p a t", a=1).broadcast_to([P, HEADS, TC])

                dve.wait_ge(s[f"gath{u}"], i * (16 * TC) + 16 * TC)
                dve.wait_ge(s[f"head_in{u}"], i * 16 + 16)
                dve.wait_ge(s[f"state_out{u}"], i * 16)
                dve.wait_ge(s["state_ready"], i * 2 + u)
                V.tensor_scalar(fresh, sm, -1.0, BIG, ALU.add, ALU.mult)
                after(V.tensor_scalar(behind, mult, 0.0, -BIG, ALU.is_equal, ALU.mult))
                after(V.tensor_tensor(masked, g[:, :, HE:ROW].rearrange("p t h -> p h t"), by_head(behind), ALU.add))
                for h in range(HEADS):
                    V.tensor_tensor_scan(st[:, :, h], fresh, masked[:, h, :], state[last][:, TC - 1, h:h + 1],
                                         ALU.add, ALU.max)
                    ins = V.tensor_tensor_scan(ad[:, h, :], sm, headrow[u][:, :, h], adst_e[last][:, h, TC - 1:TC],
                                               ALU.mult, ALU.add)
                V.tensor_copy(top[:, :, 0:1], top_e[last][:, :, TC:TC + 1])
                V.tensor_copy(index[u][:, :], sources[:, bass.ds(off + PAIRW, TC)])
                after(ins)
                V.tensor_tensor(raw[:, 0], masked, ad, ALU.add)
                after(V.tensor_tensor(raw[:, 1], st[:, :, 0:HEADS].rearrange("p t h -> p h t"), ad, ALU.add))
                V.scalar_tensor_tensor(out=raw[:, 0], in0=raw[:, 0], scalar=SLOPE, in1=raw[:, 0], op0=ALU.mult, op1=ALU.max)
                after(V.scalar_tensor_tensor(out=top[:, :, 1:TC + 1], in0=raw[:, 1], scalar=SLOPE, in1=raw[:, 1],
                                             op0=ALU.mult, op1=ALU.max))
                V.tensor_tensor(diff[:, 0], raw[:, 0], top[:, :, 1:TC + 1], ALU.subtract)
                after(V.tensor_tensor(diff[:, 1], top[:, :, 0:TC], top[:, :, 1:TC + 1], ALU.subtract))
                V.tensor_scalar(diff[:, 1], diff[:, 1], 0.0, None, ALU.min).then_inc(s["diffs_ready"], 1)
                dve.wait_ge(s["weights_ready"], i * 2 + (u + 1))
                V.tensor_tensor(diff[:, 0], weight[:, 1], by_head(sm), ALU.mult)
                after(V.tensor_tensor(raw[:, 0], weight[:, 0], by_head(mult), ALU.mult))
                for h in range(HEADS):
                    ins = V.tensor_tensor(part[:, h], g[:, :, h * EXP:(h + 1) * EXP].rearrange("p t e -> p e t"),
                                          raw[:, 0, h:h + 1, :].broadcast_to([P, EXP, TC]), ALU.mult)
                after(ins)
                for h in range(HEADS):
                    c = HEADS + h
                    V.tensor_tensor_scan(st[:, :, c], diff[:, 0, h], raw[:, 0, h], state[last][:, TC - 1, c:c + 1],
                                         ALU.mult, ALU.add)
                    for e in range(EXP):
                        c = 2 * HEADS + h * EXP + e
                        ins = V.tensor_tensor_scan(st[:, :, c], diff[:, 0, h], part[:, h, e],
                                                   state[last][:, TC - 1, c:c + 1], ALU.mult, ALU.add)
                ins.then_inc(s["state_ready"], 1)
                assert step[0] == STEPS

            with dve.Fori(0, NPAIR) as i:
                with dve.If(i < pairs):
                    for u in range(2):
                        edge_chunk(i, u)
                with dve.Else():
                    pass
            dve.wait_ge(s["state_ready"], pairs * 2)
            dve.sem_inc(s["edges_done"], 1)

            lastrow = state[1][:, TC - 1, :]
            cg = [cx[:, n, :].rearrange("p (h k) -> p h k", h=HEADS) for n in range(4)]
            V.tensor_copy(cg[0], lastrow[:, 0:HEADS].rearrange("p (h a) -> p h a", a=1).broadcast_to([P, HEADS, 1 + EXP]))
            V.tensor_copy(cg[1][:, :, 0:1], lastrow[:, HEADS:2 * HEADS].rearrange("p (h a) -> p h a", a=1))
            V.tensor_copy(cg[1][:, :, 1:1 + EXP], lastrow[:, 2 * HEADS:ST].rearrange("p (h e) -> p h e", h=HEADS))
            V.tensor_copy(cg[2], adst_e[1][:, :, TC - 1:TC].broadcast_to([P, HEADS, 1 + EXP]))
            link(V.tensor_tensor(cidx_f[:, :], flags[:, 0:1], flags[:, 1:2], ALU.mult))
            V.tensor_copy(cx[:, 3, :], cidx_f[:, 0:1].broadcast_to([P, CHN])).then_inc(s["carry_x"], 1)
            dve.wait_ge(s["carry_t"], 1)
            link(V.tensor_copy(ct[:, 0:4, :], ps_centre[0:CHN, :].rearrange("p (a b) -> p a b", a=4)))
            M_, V_, D_, C_ = (ct[:, n, :] for n in range(4))
            link(V.tensor_scalar(ct[:, 4, :], C_, -1.0, BIG, ALU.add, ALU.mult))
            link(V.tensor_tensor_scan(ct[:, 8, :], ct[:, 4, :], M_, -BIG, ALU.add, ALU.max))
            V.tensor_tensor(ct[:, 9, :], ct[:, 8, :], D_, ALU.add)
            link(V.tensor_tensor(ct[:, 10, :], M_, D_, ALU.add))
            V.scalar_tensor_tensor(out=ct[:, 9, :], in0=ct[:, 9, :], scalar=SLOPE, in1=ct[:, 9, :], op0=ALU.mult, op1=ALU.max)
            link(V.scalar_tensor_tensor(out=ct[:, 10, :], in0=ct[:, 10, :], scalar=SLOPE, in1=ct[:, 10, :], op0=ALU.mult, op1=ALU.max))
            V.memset(ct[:, 5, 0:1], 0.0)
            V.tensor_tensor(ct[:, 4, :], ct[:, 10, :], ct[:, 9, :], ALU.subtract)
            link(V.tensor_tensor(ct[:, 5, 1:P], ct[:, 9, 0:P - 1], ct[:, 9, 1:P], ALU.subtract))
            V.tensor_scalar(ct[:, 5, :], ct[:, 5, :], 0.0, None, ALU.min).then_inc(s["carry_diff"], 1)
            dve.wait_ge(s["carry_w"], 1)
            V.tensor_tensor(ct[:, 7, :], ct[:, 7, :], C_, ALU.mult)
            link(V.tensor_tensor(ct[:, 6, :], ct[:, 6, :], V_, ALU.mult))
            link(V.tensor_tensor_scan(ct[:, 9, :], ct[:, 7, :], ct[:, 6, :], 0.0, ALU.mult, ALU.add))
            V.memset(ct[:, 10, 0:1], -BIG)
            V.memset(ct[:, 11, 0:1], 0.0)
            V.tensor_copy(ct[:, 10, 1:P], ct[:, 8, 0:P - 1])
            V.tensor_copy(ct[:, 11, 1:P], ct[:, 9, 0:P - 1]).then_inc(s["carry_c"], 1)
            dve.wait_ge(s["carry_b"], 1)
            bm = ps_var[:, 0:CHN].rearrange("p (h k) -> p h k", h=HEADS)
            bv = ps_var[:, 32:32 + CHN].rearrange("p (h k) -> p h k", h=HEADS)
            V.tensor_copy(cback[:, 0:HEADS].rearrange("p (h a) -> p h a", a=1), bm[:, :, 0:1])
            V.tensor_copy(cback[:, HEADS:2 * HEADS].rearrange("p (h a) -> p h a", a=1), bv[:, :, 0:1])
            V.tensor_copy(cback[:, 2 * HEADS:ST].rearrange("p (h e) -> p h e", h=HEADS), bv[:, :, 1:1 + EXP]) \
             .then_inc(s["carry_row"], 1)

            dve.wait_ge(s["last_in"], 16 * TILES)
            dve.wait_ge(s["carry_in"], 16)
            link(V.tensor_scalar(nsm[0], empty[:, :], -BIG, None, ALU.mult))
            ec = nsm[0].rearrange("p (t a) -> p t a", a=1).broadcast_to([P, TILES, HEADS])
            link(V.tensor_tensor(nt[0], last_rows[:, :, 0:HEADS], ec, ALU.add))
            link(V.tensor_tensor(nt[1], nt[0], carried[:, :, 0:HEADS], ALU.max))
            link(V.tensor_tensor(nt[1], nt[1], table[:, :, HE:ROW], ALU.max))
            V.tensor_tensor(nt[2], nt[1], adst[:, :, :], ALU.add)
            V.tensor_tensor(tri[:, 0], nt[0], adst[:, :, :], ALU.add)
            V.tensor_tensor(tri[:, 1], carried[:, :, 0:HEADS], adst[:, :, :], ALU.add)
            link(V.tensor_tensor(tri[:, 2], table[:, :, HE:ROW], adst[:, :, :], ALU.add))
            V.scalar_tensor_tensor(out=nt[2], in0=nt[2], scalar=SLOPE, in1=nt[2], op0=ALU.mult, op1=ALU.max)
            link(V.scalar_tensor_tensor(out=tri, in0=tri, scalar=SLOPE, in1=tri, op0=ALU.mult, op1=ALU.max))
            V.tensor_tensor(tri.rearrange("p a t h -> p a (t h)"), tri.rearrange("p a t h -> p a (t h)"),
                            nt[2].rearrange("p (a t) h -> p a (t h)", a=1).broadcast_to([P, 3, NH4]), ALU.subtract) \
             .then_inc(s["node_diff"], 1)
            dve.wait_ge(s["node_w"], 1)

            def spread(x):
                return x.rearrange("p t (h a) -> p t h a", a=1).broadcast_to([P, TILES, HEADS, EXP])

            V.tensor_tensor(nt[0], last_rows[:, :, HEADS:2 * HEADS], tri2[:, 0], ALU.mult)
            V.tensor_tensor(nt[1], carried[:, :, HEADS:2 * HEADS], tri2[:, 1], ALU.mult)
            V.tensor_tensor(n16[0], last_rows[:, :, 2 * HEADS:ST].rearrange("p t (h e) -> p t h e", h=HEADS), spread(tri2[:, 0]), ALU.mult)
            V.tensor_tensor(n16[1], carried[:, :, 2 * HEADS:ST].rearrange("p t (h e) -> p t h e", h=HEADS), spread(tri2[:, 1]), ALU.mult)
            link(V.tensor_tensor(n16[2], table[:, :, 0:HE].rearrange("p t (h e) -> p t h e", h=HEADS), spread(tri2[:, 2]), ALU.mult))
            V.tensor_tensor(nt[0], nt[0], nt[1], ALU.add)
            link(V.tensor_tensor(n16[0], n16[0], n16[1], ALU.add))
            V.tensor_tensor(nt[0], nt[0], tri2[:, 2], ALU.add)
            link(V.tensor_tensor(n16[0], n16[0], n16[2], ALU.add))
            link(V.tensor_scalar(nt[0], nt[0], 1e-16, None, ALU.add))
            link(V.reciprocal(nt[1], nt[0]))
            link(V.tensor_tensor(n16[0], n16[0], spread(nt[1]), ALU.mult))
            flat = [x.rearrange("p t h e -> p t (h e)") for x in n16]

            def per_row(n):
                return rowc[:, n:n + 1, :].broadcast_to([P, TILES, HE])

            def per_node(x):
                return x.rearrange("p (t a) -> p t a", a=1).broadcast_to([P, TILES, HE])

            link(V.tensor_tensor(flat[0], flat[0], per_row(2), ALU.add))
            link(V.tensor_reduce(nsm[0], flat[0], AX.X, ALU.add))
            link(V.tensor_scalar(nsm[0], nsm[0], 1.0 / HE, None, ALU.mult))
            link(V.tensor_tensor(flat[0], flat[0], per_node(nsm[0]), ALU.subtract))
            link(V.tensor_tensor(flat[1], flat[0], flat[0], ALU.mult))
            V.tensor_reduce(nsm[0], flat[1], AX.X, ALU.add).then_inc(s["node_var"], 1)
            dve.wait_ge(s["node_std"], 1)
            link(V.reciprocal(nsm[2], nsm[1]))
            link(V.tensor_tensor(flat[0], flat[0], per_node(nsm[2]), ALU.mult))
            link(V.tensor_tensor(flat[0], flat[0], per_row(3), ALU.mult))
            link(V.tensor_tensor(flat[0], flat[0], per_row(4), ALU.add))
            link(V.tensor_reduce(nt[3], n16[0].rearrange("p t h e -> p t e h"), AX.X, ALU.add))
            link(V.tensor_scalar(nt[3], nt[3], 1.0 / HEADS, None, ALU.mult))
            link(V.memset(nt[6], 0.0))
            for a in range(EXP):
                for b in range(a + 1, EXP):
                    link(V.tensor_tensor(nsm[3], nt[3][:, :, b], nt[3][:, :, a], ALU.is_gt))
                    V.tensor_tensor(nt[6][:, :, a], nt[6][:, :, a], nsm[3], ALU.add)
                    link(V.tensor_scalar(nsm[4], nsm[3], -1.0, 1.0, ALU.mult, ALU.add))
                    link(V.tensor_tensor(nt[6][:, :, b], nt[6][:, :, b], nsm[4], ALU.add))
            V.tensor_scalar(nt[6], nt[6], 2.0, None, ALU.is_lt)
            link(V.tensor_reduce(nsm[5], nt[3], AX.X, ALU.max))

            def per_four(x):
                return x.rearrange("p (t a) -> p t a", a=1).broadcast_to([P, TILES, EXP])

            V.tensor_tensor(nt[4], nt[3], per_four(nsm[5]), ALU.subtract).then_inc(s["top_ready"], 1)
            dve.wait_ge(s["top_exp"], 1)
            link(V.tensor_tensor(nt[5], nt[5], nt[6], ALU.mult))
            link(V.tensor_reduce(nsm[6], nt[5], AX.X, ALU.add))
            link(V.reciprocal(nsm[7], nsm[6]))
            link(V.tensor_tensor(nt[5], nt[5], per_four(nsm[7]), ALU.mult))
            link(V.tensor_copy(gates.rearrange("p e a h -> p a h e"), nt[5].rearrange("p (h a) e -> p a h e", h=2)))

            def finish(c):
                dve.wait_ge(s["out_ps"], c + 1)
                cs = slice(c * CH, (c + 1) * CH)
                V.tensor_tensor(x_sb[:, cs], x_sb[:, cs], psum[c % 2][:, :], ALU.add).then_inc(s["final"], 1)

            for c in range(NCH):
                for e in range(EXP):
                    x = experts[:, 4 * c:4 * c + 4, e, :].rearrange("p a (h n) -> p a h n", h=2)
                    g = gates[:, e, 4 * c:4 * c + 4, :].rearrange("p a (h n) -> p a h n", n=1).broadcast_to([P, 4, 2, C])
                    ins = V.tensor_tensor(x, x, g, ALU.mult)
                ins.then_inc(s["gated"], 1)
                if c >= 1:
                    finish(c - 1)
            finish(NCH - 1)
    return nc


def kernel(**inputs):
    import numpy as np
    import concourse.bacc as bacc
    from concourse.bass_utils import run_bass_kernel_spmd

    nc = bacc.Bacc("TRN2", target_bir_lowering=False, num_devices=1)
    arrays, args = {}, {}
    for name, value in inputs.items():
        a = np.asarray(value)
        if name == "L0_conv_pad_fill":
            a = a.reshape(1).view(np.int64)
            short = "pad"
        else:
            short = name.replace("L0_conv_", "").replace("L0_ffn_", "")
        a = np.ascontiguousarray(a)
        arrays["in_" + short] = a
        args[short] = nc.dram_tensor("in_" + short, a.shape, mybir.dt.from_np(a.dtype), kind="ExternalInput").ap()
    out = nc.dram_tensor("out", (B, C, SIDE, SIDE), F32, kind="ExternalOutput").ap()
    build(nc, args, out)
    return run_bass_kernel_spmd(nc, [arrays], core_ids=[0]).results[0]["out"]
```

```python
import concourse.bass as bass
from concourse import mybir
from contextlib import ExitStack

F32 = mybir.dt.float32
I32 = mybir.dt.int32
ALU = mybir.AluOpType
ACT = mybir.ActivationFunctionType
AX = mybir.AxisListType

P = 128
B, C, S = 32, 64, 256
SIDE = 16
NODES = B * S
EDGES = 262144
COLS = EDGES // P
TILES = NODES // P
HALF = B // 2
TOK = HALF * S
CH = 512
NCH = TOK // CH
PAIRS = TOK // P
HEADS, EXP = 4, 4
HE = HEADS * EXP
HID = 2 * C
SRC_BITS = 13
KEY_ONE = 0x20000000
ROW = HE + HEADS
ST = HEADS + HEADS + HE
TC = 32
PAIRW = 2 * TC
NPAIR = COLS // PAIRW
SLOTS = 4
QUADW = SLOTS * TC
NQUAD = COLS // QUADW
RAWC = PAIRW
BLK = 64
NBLK = COLS // BLK
SHARES = (COLS // 4, COLS * 3 // 8, COLS // 2, COLS // 2 + 16, COLS // 2 + 64, COLS * 9 // 16, COLS * 5 // 8,
          COLS * 3 // 4, COLS * 7 // 8, COLS)
NARROW = 3
EARLY_CHUNKS = 5
CHUNK_STAGES = 11
EARLY, MIDDLE = 4, 11
NSAMP = NBLK - 1
SROW = NSAMP + 2
FOUND_HALF = 33
SPLIT1, SPLIT2 = 12, 20
CARRY_AFTER = 24
GROUP = 8
NGROUP = TILES // GROUP + 1


def paired(tile):
    return 2 * (tile % PAIRS) + tile // PAIRS


DROPPED = 9000.0
KEY_END = 2.0 ** -55
BIG = 1.0e30
MAGIC = 12582912.0
FAR = 1 << 20
LN1_EPS, LN2_EPS, LN3_EPS = 1e-6, 1e-5, 1e-5
SLOPE = 0.2
LOG_COLS = 11
LOG_EDGES = 18


def build(nc, A, out):
    ctx = ExitStack()
    with ctx:
        def sb(name, shape, dt=F32):
            return ctx.enter_context(nc.sbuf_tensor(name, shape, dt))

        def sem(name):
            return ctx.enter_context(nc.semaphore(name))

        def dram(name, shape, dt=F32):
            return nc.dram_tensor(name, shape, dt).ap()

        keys_d = dram("keys_d", [P, COLS], I32)
        dests_d = dram("dests_d", [P, COLS])
        rows_d = dram("rows_d", [NODES, ROW])
        adst_d = dram("adst_d", [NODES, HEADS])
        heads_d = dram("heads_d", [EDGES, HEADS])
        state_d = dram("state_d", [EDGES, ST])
        carry_d = dram("carry_d", [NODES, ST])

        x_sb = sb("x_sb", [P, TOK])
        ln2 = sb("ln2", [P, TOK])
        experts = sb("experts", [P, PAIRS, EXP, P])
        ex_flat = experts[:, :, :, :].rearrange("p a e c -> p (a e c)")
        centred = ex_flat[:, 0:TOK]
        square, qb, qc, square2 = (ex_flat[:, 3 * TOK + n * CH:3 * TOK + (n + 1) * CH] for n in range(4))
        qa = [ex_flat[:, TOK + n * CH:TOK + (n + 1) * CH] for n in range(2)]
        SP_ = SIDE + 2
        pad0, padn = 3 * TOK + 5 * CH, 2 * SP_ * SP_
        padded = [ex_flat[:, pad0 + n * padn:pad0 + (n + 1) * padn]
                  .rearrange("p (b r c) -> p b r c", b=2, r=SP_) for n in range(2)]

        LEVELS_T = list(range(LOG_COLS + 1, LOG_EDGES + 1))
        PASSES = 2 * len(LEVELS_T)
        SCALE_SLOT = PASSES - NCH // 2
        ROWS_SLOT = SCALE_SLOT - 2
        MOVES, at = [], LOG_COLS * (LOG_COLS + 1) // 2 % 2
        for level in LEVELS_T:
            MOVES.append((at, 1 - at, None))
            at = (1 - at + level - LOG_COLS) % 2
            MOVES.append((at, 1 - at, level - LOG_COLS if level < LOG_EDGES else None))
            at = (1 - at + LOG_COLS) % 2
        SORTED = at

        keys = [sb("keys0", [P, COLS]), sb("keys1", [P, COLS])]
        sources = sb("sources", [P, COLS + QUADW], I32)
        same = sb("same", [P, COLS])
        times = sb("times", [P, COLS])
        work = sb("work", [P, 4096])
        column = work[:, 0:COLS].bitcast(I32)
        nodes1k = work[:, COLS:COLS + GROUP * P].bitcast(I32)
        found = sb("found", [P, TILES + 1, BLK])
        found_flat = found[:, :, :].rearrange("p t b -> p (t b)")
        index = [sb(f"index{v}", [P, TC], I32) for v in range(SLOTS)]
        gathered = [sb(f"gath{v}", [P, TC, ROW])[:, :, :] for v in range(SLOTS - 1)]
        state = [sb("state0", [P, TC, ST]), sb("state1", [P, TC, ST])]
        headrow = [sb("headrow0", [P, TC, HEADS]), sb("headrow1", [P, TC, HEADS])]
        o = 0
        adst_e, top_e = [], []
        for n in range(2):
            adst_e.append(work[:, o:o + HEADS * TC].rearrange("p (h t) -> p h t", h=HEADS)); o += HEADS * TC
        for n in range(2):
            top_e.append(work[:, o:o + HEADS * (TC + 1)].rearrange("p (h t) -> p h t", h=HEADS)); o += HEADS * (TC + 1)
        fresh = work[:, o:o + TC]; o += TC
        behind = work[:, o:o + TC]; o += TC
        masked = work[:, o:o + HEADS * TC].rearrange("p (h t) -> p h t", h=HEADS); o += HEADS * TC
        raw = work[:, o:o + 2 * HEADS * TC].rearrange("p (a h t) -> p a h t", a=2, h=HEADS); o += 2 * HEADS * TC
        diff = work[:, o:o + 2 * HEADS * TC].rearrange("p (a h t) -> p a h t", a=2, h=HEADS); o += 2 * HEADS * TC
        weight = work[:, o:o + 2 * HEADS * TC].rearrange("p (a h t) -> p a h t", a=2, h=HEADS); o += 2 * HEADS * TC
        part = work[:, o:o + HE * TC].rearrange("p (h e t) -> p h e t", h=HEADS, e=EXP)
        assert o + HE * TC <= 3072

        table = sb("table", [P, TILES, ROW])
        adst = sb("adst", [P, TILES, HEADS])
        targets = sb("targets", [P, TILES + 1], I32)
        std1 = sb("std1", [P, 2, 2 * PAIRS])
        vtok = sb("vtok", [P, 2, TILES])
        srow = sb("srow", [P, SROW])
        found_row = sb("found_row", [P, 2, TILES + 1])
        block_f = sb("block_f", [P, TILES + 1])
        block_i = sb("block_i", [P, TILES + 1], I32)
        place = sb("place", [P, TILES + 1])
        first = sb("first", [P, TILES + 1])
        bad = vtok[:, :, :]
        empty = sb("empty", [P, TILES])
        void = sb("void", [P, TILES])
        scat_f = sb("scat_f", [P, 2, TILES])
        scat_i = sb("scat_i", [P, 2, TILES], I32)
        prev = sb("prev", [P, 1], I32)
        share = sb("share", [P, 16])
        limits = sb("limits", [P, 4, len(SHARES) - 1])
        group_i = sb("group_i", [P, NGROUP], I32)
        group_f = sb("group_f", [P, 2, NGROUP])
        border = sb("border", [P, 4])
        flags = sb("flags", [P, 4])
        pairs_f = sb("pairs_f", [1, 4])
        pairs_i = sb("pairs_i", [1, 3], I32)
        choice_i = sb("choice_i", [1, 1], I32)
        dfirst_i = sb("dfirst_i", [P, 1], I32)
        cidx_f = sb("cidx_f", [P, 1])
        cidx_i = sb("cidx_i", [P, 1], I32)
        dfirst = sb("dfirst", [P, HEADS])

        ident = sb("ident", [P, P])
        blockmean = sb("blockmean", [P, P])
        centring = sb("centring", [P, P])
        taps = sb("taps", [P, 9, P])
        gathered.append(taps[:, :, :].rearrange("p k n -> p (k n)")[:, 0:TC * ROW].rearrange("p (t r) -> p t r", r=ROW))
        hidden = [taps[:, :, :].rearrange("p k n -> p (k n)")[:, TC * ROW:TC * ROW + CH], sb("hidden1", [P, CH])[:, :]]
        ones = sb("ones", [P, P])
        halves = sb("halves", [P, 2])
        shift1 = sb("shift1", [P, P])
        shift2 = sb("shift2", [P, P])
        onesrow = ones[0:1, :]
        w3 = sb("w3", [P, 9])
        chan = sb("chan", [P, 3])
        half_s = sb("half_s", [P, 4])
        pow_i = sb("pow_i", [P, 2], I32)
        pad_i = sb("pad_i", [P, 2], I32)
        pad_t = sb("pad_t", [P, 6], I32)
        pad_f = sb("pad_f", [P, 2])
        signs_i = sb("signs_i", [P, 8], I32)
        signs = sb("signs", [P, 7])
        wgat = sb("wgat", [P, 2, HE])
        w1 = work[:, 3072:4096].rearrange("p (h e n) -> p h e n", h=2, e=EXP)
        b1 = sb("b1", [P, EXP])
        w2 = sb("w2", [P, EXP, C])
        b2 = sb("b2", [1, EXP * C])
        rowc = sb("rowc", [P, 5, HE])
        eps = sb("eps", [P, 3])

        psum = [ctx.enter_context(nc.psum_tensor(f"ps{n}", [P, 512], F32)) for n in range(8)]
        tr_ps = psum[0:4]
        ps_centre, ps_var, ps_conv, ps_h = psum[4:8]

        dests = keys[SORTED][:, :]
        onehot = [keys[1 - SORTED][:, n * GROUP * P:(n + 1) * GROUP * P] for n in range(2)]

        rn_flat = sources[:, 0:TILES * ST].bitcast(F32)
        last_rows = rn_flat.rearrange("p (t s) -> p t s", s=ST)
        carried = keys[0][:, 0:TILES * ST].rearrange("p (t s) -> p t s", s=ST)
        neutral = found_flat[:, 0:TILES * ST]
        zeros = same
        NH4 = TILES * HEADS
        nt = [keys[1][:, n * NH4:(n + 1) * NH4].rearrange("p (t h) -> p t h", h=HEADS) for n in range(8)]
        n16 = [ln2[:, n * TILES * HE:(n + 1) * TILES * HE].rearrange("p (t h e) -> p t h e", h=HEADS, e=EXP)
               for n in range(4)]
        gates = found_flat[:, 0:NH4].rearrange("p (e a h) -> p e a h", e=EXP, a=PAIRS)
        nsm = [found_flat[:, NH4 + n * TILES:NH4 + (n + 1) * TILES] for n in range(8)]
        tri, tri2 = (found_flat[:, 1024 + n * 768:1024 + (n + 1) * 768].rearrange("p (a t h) -> p a t h", a=3, h=HEADS)
                     for n in range(2))
        CHN = HEADS * (1 + EXP)
        cx = sb("cx", [P, 4, CHN])
        ct = found_flat[0:CHN, 0:12 * P].rearrange("p (a b) -> p a b", a=12)
        cback = sb("cback", [P, ST])

        names = ("edges_in x_in conv_in chan_in shifts_ready pad_in gat_in rows_in w1_in b1_in w2_in b2_in consts pool made "
                 "taps_made dve signs_ready keys_out keys_moved banks_moved ln1_centred ln1_squared ln1_var "
                 "ln1_std ln1_scale spread_ready acc_out refill_begun rows_taken padded_ready conv_done "
                 "x1_ready ln2_centred ln2_squared ln2_ready h_done "
                 "h_used vtok_ready vtok_std table_ready rows_out adst_out keysort_out sorted_ready counted total choice_ready "
                 "shared_in width width_max pairs_ready dests_ready dests_out border_ready border_moved border_used onehot "
                 "sampled sampled_used edge_step  states_out "
                 "block_ready found_in0 found_in1 dfirst_in places_ready first_ready ends_ps idx_ready "
                 "zeros_ready zeros_out heads_out neutral_ready neutral_out "
                 "gath0 gath1 gath2 gath3 rest0 rest1 rest2 rest3 early_index head_in0 head_in1 "
                 "diffs_ready weights_ready state_ready state_out0 state_out1 "
                 "carry_x carry_t carry_diff carry_w carry_c carry_b carry_row carry_out carry_in last_in0 last_in1 "
                 "hid_ps hid_ready ex_ps ex_ready node_diff node_w node_var node_std top_ready top_exp "
                 "gated out_ps final out_done").split()
        s = {n: sem(n) for n in names}

        block = ctx.enter_context(nc.Block())

        @block.sync
        def _(sp):
            for n in range(2):
                sp.dma_start(keys[n][:, :].bitcast(I32), A["edge_index"][n].rearrange("(p t) -> p t", p=P)) \
                  .then_inc(s["edges_in"], 16)
            for h in range(2):
                sp.dma_start(x_sb[h * C:(h + 1) * C, :].rearrange("p (b s) -> p b s", b=HALF),
                             A["x"][h * HALF:(h + 1) * HALF].rearrange("b c i j -> c b (i j)")) \
                  .then_inc(s["x_in"], 16)
            for h in range(2):
                rows = slice(h * C, (h + 1) * C)
                sp.dma_start(w3[rows, :], A["weight"].rearrange("c a i j -> c (a i j)")).then_inc(s["conv_in"], 16)
                for n, name in enumerate(("bias", "scl_in", "srarh_shift")):
                    sp.dma_start(chan[rows, n:n + 1], A[name].rearrange("(c a) -> c a", a=1)).then_inc(s["chan_in"], 16)
            sp.dma_start(pad_i[:, :], A["pad"].bitcast(I32).rearrange("(a n) -> a n", a=1).broadcast_to([P, 2])) \
              .then_inc(s["pad_in"], 16)
            sp.wait_ge(s["consts"], 1)
            for h in range(2):
                rows = slice(h * C, (h + 1) * C)
                sp.dma_start(wgat[rows, h, :], A["W_gat"]).then_inc(s["gat_in"], 16)
                sp.dma_start(w1[rows, h, :, :], A["W1"].rearrange("e c n -> c e n")).then_inc(s["w1_in"], 16)
            for n, name in enumerate(("att_src", "att_dst")):
                sp.dma_start(rowc[:, n, :], A[name].rearrange("(a h) e -> a (h e)", a=1).broadcast_to([P, HE])) \
                  .then_inc(s["rows_in"], 16)
            for n, name in enumerate(("b_gat", "ln_gamma", "ln_beta")):
                sp.dma_start(rowc[:, 2 + n, :], A[name].rearrange("(a n) -> a n", a=1).broadcast_to([P, HE])) \
                  .then_inc(s["rows_in"], 16)
            with nc.allow_non_contiguous_dma(reason="small weights"):
                sp.dma_start(b1[:, :], A["b1"].rearrange("e n -> n e")).then_inc(s["b1_in"], 16)
            sp.dma_start(w2[:, :, :], A["W2"].rearrange("e n c -> n e c")).then_inc(s["w2_in"], 16)
            sp.dma_start(b2[:, :], A["b2"].rearrange("(a e) c -> a (e c)", a=1)).then_inc(s["b2_in"], 16)
            sp.wait_ge(s["zeros_ready"], 1)
            state_rows = state_d.rearrange("(p t) h -> p (t h)", p=P).rearrange("p (a t) -> p a t", a=ST)
            for rows, n, done in ((heads_d.rearrange("(p t) h -> p (t h)", p=P).rearrange("p (a t) -> p a t", a=HEADS),
                                   HEADS, "zeros_out"),
                                  (state_rows[:, 0:ST // 2], ST // 2, "state_out0"),
                                  (state_rows[:, ST // 2:ST], ST // 2, "state_out1")):
                sp.dma_start(rows, zeros[:, :].rearrange("p (a t) -> p a t", a=1).broadcast_to([P, n, COLS])) \
                  .then_inc(s[done], 16)
            sp.wait_ge(s["neutral_ready"], 1)
            sp.dma_start(carry_d.rearrange("(p t) s -> p (t s)", p=P), neutral).then_inc(s["neutral_out"], 16)
            sp.wait_ge(s["table_ready"], 1)
            for h in range(2):
                half = slice(h * NODES // 2, (h + 1) * NODES // 2)
                sp.dma_start(rows_d[half].rearrange("(q p) r -> p q r", p=P), table[:, h:TILES:2, :]).then_inc(s["rows_out"], 16)
                sp.dma_start(adst_d[half].rearrange("(q p) r -> p q r", p=P), adst[:, h:TILES:2, :]).then_inc(s["adst_out"], 16)
            sp.wait_ge(s["sorted_ready"], 1)
            sp.dma_start(keys_d, keys[SORTED][:, :].bitcast(I32)).then_inc(s["keysort_out"], 16)
            keys_line = keys_d.rearrange("p t -> (p t)")
            sp.wait_ge(s["keysort_out"], 16)
            sp.wait_ge(s["choice_ready"], 1)
            choice = sp.value_load(choice_i[0:1, 0:1], min_val=0, max_val=len(SHARES) - 1)
            for n, width in enumerate(SHARES):
                with sp.If(choice == n):
                    sp.dma_start(keys[1 - SORTED][:, 0:width].bitcast(I32),
                                 keys_line[0:P * width].rearrange("(p t) -> p t", p=P)).then_inc(s["shared_in"], 16)
                    with nc.allow_non_contiguous_dma(reason="one key of each partition"):
                        sp.dma_start(prev[1:P, :], keys_line[0:(P - 1) * width]
                                     .rearrange("(p t) -> p t", p=P - 1)[:, width - 1:width]).then_inc(s["shared_in"], 16)
                with sp.Else():
                    pass
            sp.wait_ge(s["dests_ready"], 1)
            sp.dma_start(dests_d, dests).then_inc(s["dests_out"], 16)
            sp.wait_ge(s["pairs_ready"], 1)
            pairs = sp.value_load(pairs_i[0:1, 0:1], min_val=1, max_val=NPAIR)
            sp.wait_ge(s["heads_out"], 16 * TILES)
            heads_v = heads_d.rearrange("(p t) h -> p t h", p=P)
            state_v = state_d.rearrange("(p t) s -> p t s", p=P)
            for u in range(2):
                sp.dma_start(headrow[u][:, :, :], heads_v[:, u * TC:(u + 1) * TC, :]).then_inc(s[f"head_in{u}"], 16)
            with sp.Fori(0, NPAIR - 1) as i:
                with sp.If(i + 1 < pairs):
                    for u in range(2):
                        sp.wait_ge(s["state_ready"], i * 2 + (u + 2))
                        sp.dma_start(state_v[:, bass.ds(i * PAIRW + u * TC, TC), :], state[u][:, :, :]) \
                          .then_inc(s[f"state_out{u}"], 16)
                        sp.dma_start(headrow[u][:, :, :], heads_v[:, bass.ds(i * PAIRW + (u * TC + PAIRW), TC), :]) \
                          .then_inc(s[f"head_in{u}"], 16)
                with sp.Else():
                    pass
            for u in range(2):
                sp.wait_ge(s["state_ready"], pairs * 2 + u)
                sp.dma_start(state_v[:, bass.ds(pairs * PAIRW + (u * TC - PAIRW), TC), :], state[u][:, :, :]) \
                  .then_inc(s[f"state_out{u}"], 16)
            for u in range(2):
                sp.wait_ge(s[f"state_out{u}"], pairs * 16 + 16)
            sp.sem_inc(s["states_out"], 1)
            sp.wait_ge(s["carry_out"], 16)
            for h in range(2):
                sp.dma_start(carried[:, h:TILES:2, :],
                             carry_d[h * NODES // 2:(h + 1) * NODES // 2].rearrange("(q p) s -> p q s", p=P)) \
                  .then_inc(s["carry_in"], 16)
            for c in range(NCH):
                sp.wait_ge(s["final"], c + 1)
                for h in range(2):
                    sp.dma_start(out[h * HALF + 2 * c:h * HALF + 2 * c + 2].rearrange("b c i j -> c b (i j)"),
                                 x_sb[h * C:(h + 1) * C, c * CH:(c + 1) * CH].rearrange("p (b s) -> p b s", b=2)) \
                      .then_inc(s["out_done"], 16)
            sp.wait_ge(s["out_done"], 16 * 2 * NCH)

        @block.gpsimd
        def _(pool):
            steps = [0]

            def settle(ins):
                steps[0] += 1
                ins.then_inc(s["pool"], 1)
                pool.wait_ge(s["pool"], steps[0])

            settle(pool.memset(wgat[:, :, :], 0.0))
            settle(pool.memset(w1, 0.0))
            settle(pool.iota(signs_i[:, 7:8], [[0, 1]], base=0, channel_multiplier=1))
            pool.iota(targets[:, :], [[P, TILES + 1]], base=0, channel_multiplier=1).then_inc(s["consts"], 1)
            pool.wait_ge(s["consts"], 1)
            for tile in (ident, shift1, shift2, blockmean):
                settle(pool.memset(tile[:, :], 0.0))
            settle(pool.memset(ones[:, :], 1.0))
            settle(pool.memset(halves[:, :], 0.0))
            settle(pool.memset(halves[0:C, 0:1], 1.0 / C))
            settle(pool.memset(halves[C:P, 1:2], 1.0 / C))
            settle(pool.iota(group_i[:, :], [[GROUP * P, NGROUP]], base=0, channel_multiplier=0))
            settle(pool.iota(column, [[1, COLS]], base=0, channel_multiplier=0))
            settle(pool.iota(nodes1k, [[1, GROUP * P]], base=0, channel_multiplier=0))
            settle(pool.memset(blockmean[0:C, 0:C], 1.0 / C))
            settle(pool.memset(blockmean[C:P, C:P], 1.0 / C))
            settle(pool.memset(shift2[0:1, P - 1:P], 1.0))
            settle(pool.affine_select(out=ident[:, :], in_=ident[:, :], compare_op=ALU.not_equal, fill=1.0, base=0,
                                      pattern=[[-1, P]], channel_multiplier=1))
            settle(pool.affine_select(out=shift1[:, :], in_=shift1[:, :], compare_op=ALU.not_equal, fill=1.0, base=-1,
                                      pattern=[[-1, P]], channel_multiplier=1))
            pool.tensor_tensor(centring[:, :], ident[:, :], blockmean[:, :], ALU.subtract).then_inc(s["made"], 1)
            pool.wait_ge(s["conv_in"], 32)
            pool.wait_ge(s["made"], 1)
            for k in range(9):
                pool.tensor_scalar(taps[:, k, :], ident[:, :], w3[:, k:k + 1], None, ALU.mult).then_inc(s["taps_made"], 1)
                pool.wait_ge(s["taps_made"], k + 1)
            settle(pool.memset(neutral, 0.0))
            pool.memset(neutral.rearrange("p (t s) -> p t s", s=ST)[:, :, 0:HEADS], -BIG).then_inc(s["neutral_ready"], 1)
            pool.wait_ge(s["neutral_ready"], 1)

            half_b, inv_b = half_s[:, 0:1], pow_i[:, 1:2].bitcast(F32)

            def round_down(value):
                settle(pool.tensor_scalar(qb, value, 1.0, MAGIC, ALU.mult, ALU.add))
                settle(pool.tensor_scalar(qb, qb, 1.0, -MAGIC, ALU.mult, ALU.add))
                settle(pool.tensor_tensor(qc, value, qb, ALU.subtract))
                settle(pool.tensor_scalar(qc, qc, 0.0, None, ALU.is_lt))
                settle(pool.tensor_tensor(qb, qb, qc, ALU.subtract))

            def requantise(c):
                cs = slice(c * CH, (c + 1) * CH)
                a = qa[c % 2]
                pool.wait_ge(s["acc_out"], c + 1)
                settle(pool.tensor_scalar(a, a, 32768.0, 2.0 ** -16, ALU.add, ALU.mult))
                round_down(a)
                settle(pool.tensor_tensor(a, a, qb, ALU.subtract))
                settle(pool.tensor_scalar(a, a, 65536.0, -32768.0, ALU.mult, ALU.add))
                settle(pool.tensor_scalar(a, a, chan[:, 1:2], 2.0 ** -15, ALU.mult, ALU.mult))
                settle(pool.tensor_scalar(a, a, 32768.0, 0.0, ALU.min, ALU.max))
                round_down(a)
                settle(pool.tensor_scalar(a, qb, half_b, inv_b, ALU.add, ALU.mult))
                round_down(a)
                settle(pool.tensor_scalar(qb, qb, 255.0, -32.0, ALU.min, ALU.add))
                pool.tensor_tensor(x_sb[:, cs], x_sb[:, cs], qb, ALU.add).then_inc(s["x1_ready"], 1)
                pool.wait_ge(s["x1_ready"], c + 1)

            pool.wait_ge(s["shifts_ready"], 1)
            for c in range(NCH):
                requantise(c)

            node_bound, edge_bound, block_bound = (pool.to_reg(n - 1) for n in (NODES, EDGES, P * NBLK))

            def gather_rows(u, begin=0, end=TC):
                for t in range(begin, end):
                    pool.indirect_dma_start(out=gathered[u][:, t, :], out_offset=None, in_=rows_d,
                                            in_offset=bass.IndirectOffsetOnAxis(ap=index[u][:, t:t + 1], axis=0),
                                            bounds_check=node_bound, oob_is_err=False) \
                        .then_inc(s[f"{'gath' if t < TC // 2 else 'rest'}{u}"], 16)

            pool.wait_ge(s["rows_out"], 32)
            pool.wait_ge(s["early_index"], 1)
            gather_rows(0)
            gather_rows(1)
            pool.wait_ge(s["adst_out"], 32)
            pool.wait_ge(s["idx_ready"], 1)
            pool.indirect_dma_start(out=dfirst[:, :], out_offset=None, in_=adst_d,
                                    in_offset=bass.IndirectOffsetOnAxis(ap=dfirst_i[:, :], axis=0),
                                    bounds_check=node_bound, oob_is_err=False).then_inc(s["dfirst_in"], 16)
            gather_rows(2)
            gather_rows(3, 0, SPLIT1)
            dest_blocks = dests_d.rearrange("p (a b) -> (p a) b", b=BLK)
            pool.wait_ge(s["dests_out"], 16)
            pool.wait_ge(s["block_ready"], 1)
            pool.wait_ge(s["neutral_out"], 16)
            for t in range(TILES + 1):
                pool.indirect_dma_start(out=found[:, t, :], out_offset=None, in_=dest_blocks,
                                        in_offset=bass.IndirectOffsetOnAxis(ap=block_i[:, t:t + 1], axis=0),
                                        bounds_check=block_bound, oob_is_err=False) \
                    .then_inc(s[f"found_in{t // FOUND_HALF}"], 16)
            gather_rows(3, SPLIT1, SPLIT2)
            pool.wait_ge(s["zeros_out"], 16)
            pool.wait_ge(s["places_ready"], 1)
            for t in range(TILES):
                pool.indirect_dma_start(out=heads_d, in_=adst[:, paired(t), :], in_offset=None,
                                        out_offset=bass.IndirectOffsetOnAxis(ap=scat_i[:, 0, t:t + 1], axis=0),
                                        bounds_check=edge_bound, oob_is_err=False).then_inc(s["heads_out"], 16)
            gather_rows(3, SPLIT2, TC)
            chunks = pool.value_load(pairs_i[0:1, 1:2], min_val=1, max_val=2 * NPAIR)
            half_chunks = pool.value_load(pairs_i[0:1, 2:3], min_val=1, max_val=4 * NPAIR)
            with pool.Fori(0, NQUAD - 1) as i:
                with pool.If(i * SLOTS + SLOTS < chunks):
                    for v in range(SLOTS):
                        with pool.If(i * SLOTS + (SLOTS + v) < chunks):
                            pool.wait_ge(s["state_ready"], i * SLOTS + (v + 2))
                            pool.sem_inc(s["refill_begun"], 1)
                            gather_rows(v, 0, TC // 2)
                            with pool.If(i * (2 * SLOTS) + (2 * SLOTS + 2 * v + 1) < half_chunks):
                                gather_rows(v, TC // 2, TC)
                            with pool.Else():
                                pass
                        with pool.Else():
                            pass
                with pool.Else():
                    pass
            pool.wait_ge(s["states_out"], 1)
            for t in range(TILES):
                if t == CARRY_AFTER:
                    pool.wait_ge(s["neutral_out"], 16)
                    pool.wait_ge(s["carry_row"], 1)
                    pool.indirect_dma_start(out=carry_d, in_=cback[:, :], in_offset=None,
                                            out_offset=bass.IndirectOffsetOnAxis(ap=cidx_i[:, :], axis=0),
                                            bounds_check=node_bound, oob_is_err=False).then_inc(s["carry_out"], 16)
                tile = t % 2 * PAIRS + t // 2
                pool.indirect_dma_start(out=last_rows[:, t, :], out_offset=None, in_=state_d,
                                        in_offset=bass.IndirectOffsetOnAxis(ap=scat_i[:, 1, tile:tile + 1], axis=0),
                                        bounds_check=edge_bound, oob_is_err=False).then_inc(s[f"last_in{t // PAIRS}"], 16)

        @block.tensor
        def _(pe):
            T = nc.tensor
            def expert_out(k):
                g, e = k // EXP, k % EXP
                if e == 0:
                    if g >= 1:
                        pe.wait_ge(s["ex_ready"], 2 * g)
                    for bank in range(2):
                        T.matmul(psum[2 + bank][:, :].rearrange("p (a n) -> p a n", a=2), onesrow,
                                 b2[:, :].rearrange("p (a n) -> p a n", a=1).broadcast_to([1, 2, EXP * C]),
                                 start=True, stop=False, skip_group_check=True)
                pe.wait_ge(s["hid_ready"], k + 1)
                for j in range(4):
                    last = T.matmul(psum[2 + j // 2][:, (j % 2) * EXP * C + e * C:(j % 2) * EXP * C + (e + 1) * C],
                                    hidden[k % 2][:, j * P:(j + 1) * P], w2[:, e, :], start=False,
                                    stop=(e == EXP - 1), skip_group_check=True)
                last.then_inc(s["ex_ps"], 1)

            pe.wait_ge(s["made"], 1)
            pe.wait_ge(s["x_in"], 32)
            with pe.Fori(0, NCH) as i:
                pe.wait_ge(s["ln1_squared"], i + 1)
                T.matmul(ps_centre[:, :], centring[:, :], x_sb[:, bass.ds(i * CH, CH)], start=True, stop=True) \
                    .then_inc(s["ln1_centred"], 1)
                pe.wait_ge(s["ln1_squared"], i + 2)
                pe.wait_ge(s["ln1_std"], i + 1)
                for j in range(CH // P):
                    last = T.matmul(ps_var[:, 2 * j:2 * j + 2], square[:, j * P:(j + 1) * P], halves[:, :],
                                    start=True, stop=True)
                last.then_inc(s["ln1_var"], 1)
            pe.wait_ge(s["taps_made"], 9)
            pe.wait_ge(s["gat_in"], 32)
            wg = wgat[:, :, :].rearrange("p a n -> p (a n)")

            def conv(c):
                pe.wait_ge(s["padded_ready"], c + 1)
                if c >= 1:
                    pe.wait_ge(s["acc_out"], c)
                for k in range(9):
                    last = T.matmul(ps_conv[:, :], taps[:, k, :],
                                    padded[c % 2][:, :, k // 3:k // 3 + SIDE, k % 3:k % 3 + SIDE],
                                    start=(k == 0), stop=(k == 8))
                last.then_inc(s["conv_done"], 1)

            def spread(bank, scales):
                for j in range(CH // P):
                    for h in range(2):
                        last = T.matmul(bank[h * C:(h + 1) * C, j * P:(j + 1) * P], scales(j, h).broadcast_to([P, C]),
                                        ident[:, :], start=True, stop=True)
                last.then_inc(s["spread_ready"], 1)

            def spread1(c):
                pe.wait_ge(s["ln1_scale"], 1)
                if c >= 1:
                    pe.wait_ge(s["padded_ready"], c)
                spread(ps_var, lambda j, h: std1[:, 1, c * 8 + 2 * j + h:c * 8 + 2 * j + h + 1])

            def norm2(c):
                pe.wait_ge(s["x1_ready"], c + 1)
                if c == 0:
                    pe.wait_ge(s["ln1_std"], NCH + 1)
                T.matmul(ps_centre[:, :], centring[:, :], x_sb[:, c * CH:(c + 1) * CH], start=True, stop=True) \
                    .then_inc(s["ln2_centred"], 1)
                pe.wait_ge(s["ln2_squared"], c + 1)
                if c >= 1:
                    pe.wait_ge(s["h_used"], c)
                for j in range(CH // P):
                    o = j * (2 * HE + 2)
                    T.matmul(ps_h[:, o:o + 2 * HE], ln2[:, c * CH + j * P:c * CH + (j + 1) * P], wg,
                             start=True, stop=True)
                    last = T.matmul(ps_h[:, o + 2 * HE:o + 2 * HE + 2], square2[:, j * P:(j + 1) * P], halves[:, :],
                                    start=True, stop=True)
                last.then_inc(s["h_done"], 1)

            for c in range(EARLY_CHUNKS):
                spread1(c)
                conv(c)
                if c >= 1:
                    norm2(c - 1)

            for n in range(PASSES):
                src = keys[MOVES[n][0]]
                for b in range(4):
                    if b % 2 == 0:
                        pe.wait_ge(s["keys_out"], 2 * n + b // 2 + 1)
                    for j in range(4):
                        cs = (b * 4 + j) * P
                        last = T.transpose(tr_ps[b][:, j * P:(j + 1) * P], src[:, cs:cs + P], ident[:, :])
                    last.then_inc(s["keys_moved"], 1)
                c = EARLY_CHUNKS + n // 2
                if n % 2 == 0 and c < NCH:
                    spread1(c)
                if n % 2 == 1 and c < NCH:
                    conv(c)
                if n % 2 == 1 and c <= NCH:
                    norm2(c - 1)
                if SCALE_SLOT - 1 <= n < PASSES - 1:
                    pe.wait_ge(s["table_ready"], 1)
                    for c in range((n - SCALE_SLOT + 1) * 2, (n - SCALE_SLOT + 1) * 2 + 2):
                        if c >= 4:
                            pe.wait_ge(s["ln2_ready"], c - 3)
                        spread(psum[4 + c % 4], lambda j, h: vtok[:, 0, 8 * c + 2 * j + h:8 * c + 2 * j + h + 1])

            pe.wait_ge(s["counted"], 1)
            T.matmul(ps_conv[:, 0:1], ones[:, :], share[:, 0:1], start=True, stop=True).then_inc(s["total"], 1)
            pe.wait_ge(s["banks_moved"], 4 * PASSES)
            pe.wait_ge(s["ln2_ready"], NCH)
            pe.wait_ge(s["w1_in"], 32)
            pe.wait_ge(s["w2_in"], 16)
            pe.wait_ge(s["b2_in"], 16)

            def experts_run(begin, end):
                for k in range(begin * EXP, end * EXP):
                    c, h, e = k // (2 * EXP), k // EXP % 2, k % EXP
                    if k >= 2:
                        pe.wait_ge(s["hid_ready"], k - 1)
                    T.matmul(psum[k % 2][:, :], w1[:, h, e, :], ln2[:, c * CH:(c + 1) * CH], start=True, stop=True) \
                        .then_inc(s["hid_ps"], 1)
                    if k >= 1:
                        expert_out(k - 1)

            experts_run(0, EARLY)
            pe.wait_ge(s["width"], 1)
            T.matmul(ps_conv[0:1, 128:256], srow[:, SROW - 1:SROW], ident[:, :], start=True, stop=True) \
                .then_inc(s["width_max"], 1)
            pe.wait_ge(s["border_ready"], 1)
            T.matmul(ps_conv[:, 0:3], shift1[:, :], border[:, 0:3], start=True, stop=True).then_inc(s["border_moved"], 1)
            for c in range(NGROUP):
                tiles = GROUP if c < NGROUP - 1 else 1
                pe.wait_ge(s["onehot"], c + 1)
                if c == 2:
                    pe.wait_ge(s["border_used"], 1)
                if c >= 4:
                    pe.wait_ge(s["sampled_used"], c - 3)
                for j in range(tiles):
                    last = T.matmul(psum[4 + c % 4][:, j * SROW:(j + 1) * SROW],
                                    onehot[c % 2][:, j * P:(j + 1) * P], srow[:, :], start=True, stop=True)
                last.then_inc(s["sampled"], 1)

            experts_run(EARLY, MIDDLE)

            pe.wait_ge(s["first_ready"], 1)
            T.matmul(ps_h[:, 0:TILES], shift1[:, :], first[:, 0:TILES], start=True, stop=False)
            T.matmul(ps_h[:, 0:TILES], shift2[:, :], first[:, 1:TILES + 1], start=False, stop=True) \
                .then_inc(s["ends_ps"], 1)

            experts_run(MIDDLE, 2 * NCH)
            expert_out(2 * NCH * EXP - 1)

            pe.wait_ge(s["carry_x"], 1)
            for n in range(4):
                last = T.transpose(ps_centre[0:CHN, n * P:(n + 1) * P], cx[:, n, :], ident[:, :])
            last.then_inc(s["carry_t"], 1)
            pe.wait_ge(s["carry_c"], 1)
            for n in range(2):
                last = T.transpose(ps_var[:, n * 32:n * 32 + CHN], ct[:, 10 + n, :], ident[0:CHN, 0:CHN])
            last.then_inc(s["carry_b"], 1)

            for c in range(NCH):
                pe.wait_ge(s["gated"], c + 1)
                if c >= 2:
                    pe.wait_ge(s["final"], c - 1)
                for j in range(CH // P):
                    for e in range(EXP):
                        last = T.matmul(psum[c % 2][:, j * P:(j + 1) * P], experts[:, c * 4 + j, e, :], ident[:, :],
                                        start=(e == 0), stop=(e == EXP - 1))
                last.then_inc(s["out_ps"], 1)

        @block.scalar
        def _(act):
            N = nc.scalar
            act.wait_ge(s["signs_ready"], 1)
            act.sem_inc(s["ln1_squared"], 1)
            act.sem_inc(s["ln1_std"], 1)
            with act.Fori(0, NCH) as i:
                act.wait_ge(s["ln1_centred"], i + 1)
                N.activation(centred[:, bass.ds(i * CH, CH)], ps_centre[:, :], ACT.Copy)
                N.activation(square, ps_centre[:, :], ACT.Square).then_inc(s["ln1_squared"], 1)
                act.wait_ge(s["ln1_var"], i + 1)
                N.activation(std1[:, 0, bass.ds(i * 8, 8)], ps_var[:, 0:8], ACT.Sqrt, bias=eps[:, 0:1]) \
                 .then_inc(s["ln1_std"], 1)

            def conv_out(c):
                act.wait_ge(s["conv_done"], c + 1)
                if c == 0:
                    act.wait_ge(s["chan_in"], 16 * 6)
                if c >= 2:
                    act.wait_ge(s["x1_ready"], c - 1)
                N.activation(qa[c % 2], ps_conv[:, :], ACT.Identity, bias=chan[:, 0:1]).then_inc(s["acc_out"], 1)

            def centre2(c):
                act.wait_ge(s["ln2_centred"], c + 1)
                N.activation(ln2[:, c * CH:(c + 1) * CH], ps_centre[:, :], ACT.Copy)
                N.activation(square2, ps_centre[:, :], ACT.Square).then_inc(s["ln2_squared"], 1)

            for c in range(EARLY_CHUNKS):
                conv_out(c)
                if c >= 1:
                    centre2(c - 1)
            for n in range(PASSES):
                dst = keys[MOVES[n][1]]
                for b in range(4):
                    act.wait_ge(s["keys_moved"], 4 * n + b + 1)
                    sign = 1.0 if MOVES[n][2] is None else signs[:, MOVES[n][2]:MOVES[n][2] + 1]
                    N.activation(dst[:, b * 512:(b + 1) * 512], tr_ps[b][:, :], ACT.Copy, scale=sign) \
                     .then_inc(s["banks_moved"], 1)
                c = EARLY_CHUNKS + n // 2
                if n % 2 == 1 and c < NCH:
                    conv_out(c)
                if n % 2 == 1 and c <= NCH:
                    centre2(c - 1)
                if n == ROWS_SLOT:
                    act.wait_ge(s["vtok_ready"], 1)
                    N.activation(vtok[:, 1, :], vtok[:, 0, :], ACT.Sqrt, bias=eps[:, 1:2]).then_inc(s["vtok_std"], 1)
            act.wait_ge(s["b1_in"], 16)
            act.wait_ge(s["table_ready"], 1)
            act.wait_ge(s["ln2_ready"], NCH)
            for g in range(2 * NCH):
                c, h = g // 2, g % 2
                for e in range(EXP):
                    k = g * EXP + e
                    act.wait_ge(s["hid_ps"], k + 1)
                    if k >= 2:
                        act.wait_ge(s["ex_ps"], k - 1)
                    N.activation(hidden[k % 2], psum[k % 2][:, :], ACT.Gelu, bias=b1[:, e:e + 1]) \
                     .then_inc(s["hid_ready"], 1)
                act.wait_ge(s["ex_ps"], (g + 1) * EXP)
                for bank in range(2):
                    pair = 4 * c + 2 * bank
                    N.activation(experts[:, pair:pair + 2, :, h * C:(h + 1) * C],
                                 psum[2 + bank][:, :].rearrange("p (a e n) -> p a e n", a=2, e=EXP), ACT.Copy) \
                     .then_inc(s["ex_ready"], 1)
            act.wait_ge(s["pairs_ready"], 1)
            pairs = act.value_load(pairs_i[0:1, 0:1], min_val=1, max_val=NPAIR)
            chunks = act.value_load(pairs_i[0:1, 1:2], min_val=1, max_val=2 * NPAIR)
            with act.Fori(0, NPAIR) as i:
                with act.If(i < pairs):
                    act.wait_ge(s["diffs_ready"], i * 2 + 1)
                    N.activation(weight, diff, ACT.Exp).then_inc(s["weights_ready"], 1)
                    with act.If(i * 2 + 1 < chunks):
                        act.wait_ge(s["diffs_ready"], i * 2 + 2)
                        N.activation(weight, diff, ACT.Exp).then_inc(s["weights_ready"], 1)
                    with act.Else():
                        pass
                with act.Else():
                    pass
            act.wait_ge(s["carry_diff"], 1)
            N.activation(ct[:, 6:8, :], ct[:, 4:6, :], ACT.Exp).then_inc(s["carry_w"], 1)
            for k in range(2):
                ts = slice(k * PAIRS, (k + 1) * PAIRS)
                act.wait_ge(s["node_diff"], k + 1)
                N.activation(tri2[:, :, ts, :], tri[:, :, ts, :], ACT.Exp).then_inc(s["node_w"], 1)
                act.wait_ge(s["node_var"], k + 1)
                N.activation(nsm[1][:, ts], nsm[0][:, ts], ACT.Sqrt, bias=eps[:, 2:3], scale=1.0 / HE).then_inc(s["node_std"], 1)
                act.wait_ge(s["top_ready"], k + 1)
                N.activation(nt[5][:, ts, :], nt[4][:, ts, :], ACT.Exp).then_inc(s["top_exp"], 1)

        @block.vector
        def _(dve):
            V = nc.vector
            done = [0]

            def link(ins):
                done[0] += 1
                ins.then_inc(s["dve"], 1)
                dve.wait_ge(s["dve"], done[0])

            V.memset(zeros[:, :], 0.0).then_inc(s["zeros_ready"], 1)
            for n in range(len(SHARES) - 1):
                V.memset(limits[:, 0, n:n + 1], float(P * SHARES[n]))
                V.memset(limits[:, 1, n:n + 1], float(SHARES[n + 1] - SHARES[n]))
            V.memset(prev[:, :], 0)
            V.memset(eps[:, 0:1], LN1_EPS)
            V.memset(eps[:, 1:2], LN2_EPS)
            V.memset(eps[:, 2:3], LN3_EPS)
            V.memset(sources[:, COLS:COLS + QUADW], 0)
            dve.wait_ge(s["consts"], 1)
            for b in range(7):
                ins = V.tensor_scalar(signs_i[:, b:b + 1], signs_i[:, 7:8], b, 1, ALU.logical_shift_right, ALU.bitwise_and)
            link(ins)
            V.tensor_scalar(signs[:, :], signs_i[:, 0:7], -2.0, 1.0, ALU.mult, ALU.add).then_inc(s["signs_ready"], 1)

            dve.wait_ge(s["edges_in"], 32)
            src_i, dst_i = keys[0][:, :].bitcast(I32), keys[1][:, :].bitcast(I32)
            V.tensor_scalar(src_i, src_i, float(NODES - 1), 0.0, ALU.min, ALU.max)
            link(V.tensor_scalar(dst_i, dst_i, float(NODES), 0.0, ALU.min, ALU.max))
            link(V.tensor_scalar(dst_i, dst_i, SRC_BITS, KEY_ONE, ALU.logical_shift_left, ALU.bitwise_or))
            link(V.tensor_tensor(src_i, src_i, dst_i, ALU.bitwise_or))
            link(V.tensor_scalar(keys[0][:, :], keys[0][:, :], signs[:, 0:1], None, ALU.mult))

            dve.wait_ge(s["pad_in"], 16)
            lo, hi = pad_i[:, 0:1], pad_i[:, 1:2]
            pt = [pad_t[:, n:n + 1] for n in range(6)]
            V.tensor_scalar(pt[0], hi, 20, 0x7FF, ALU.logical_shift_right, ALU.bitwise_and)
            V.tensor_scalar(pt[1], hi, 0xFFFFF, 3, ALU.bitwise_and, ALU.logical_shift_left)
            V.tensor_scalar(pt[2], lo, 29, 7, ALU.logical_shift_right, ALU.bitwise_and)
            V.tensor_scalar(pt[3], lo, 28, 1, ALU.logical_shift_right, ALU.bitwise_and)
            link(V.tensor_scalar(pt[4], hi, 31, 31, ALU.logical_shift_right, ALU.logical_shift_left))
            V.tensor_scalar(pad_f[:, 1:2], pt[0], float(1023 - 127), None, ALU.is_gt)
            link(V.tensor_scalar(pt[0], pt[0], -float(1023 - 127), 0.0, ALU.add, ALU.max))
            link(V.tensor_scalar(pt[0], pt[0], 255.0, None, ALU.min))
            link(V.tensor_scalar(pt[0], pt[0], 23, None, ALU.logical_shift_left))
            link(V.tensor_tensor(pt[1], pt[1], pt[2], ALU.bitwise_or))
            link(V.tensor_tensor(pt[1], pt[1], pt[0], ALU.bitwise_or))
            link(V.tensor_tensor(pt[1], pt[1], pt[3], ALU.add))
            link(V.tensor_tensor(pt[1], pt[1], pt[4], ALU.bitwise_or))
            link(V.tensor_tensor(pad_f[:, 0:1], pt[1].bitcast(F32), pad_f[:, 1:2], ALU.mult))
            for n in range(2):
                link(V.memset(padded[n], 0.0))
                link(V.tensor_scalar(padded[n], padded[n], pad_f[:, 0:1], None, ALU.add))

            dve.wait_ge(s["chan_in"], 16 * 6)
            sh = chan[:, 2:3]
            V.tensor_scalar(half_s[:, 2:3], sh, 0.0, None, ALU.is_gt)
            V.tensor_scalar(pow_i[:, 0:1], sh, 126.0, float(1 << 23), ALU.add, ALU.mult)
            link(V.tensor_scalar(pow_i[:, 1:2], sh, -127.0, -float(1 << 23), ALU.add, ALU.mult))
            V.tensor_tensor(half_s[:, 0:1], pow_i[:, 0:1].bitcast(F32), half_s[:, 2:3], ALU.mult).then_inc(s["shifts_ready"], 1)

            def stage(src, dst, k, j, signal=None, half=None):
                def end(ins):
                    link(ins) if signal is None else ins.then_inc(s[signal], 1)

                src, dst = src[:, :], dst[:, :]
                if half is not None and j < COLS // 2:
                    src, dst = (x[:, half * COLS // 2:(half + 1) * COLS // 2] for x in (src, dst))
                if k is None:
                    a = src.rearrange("p (n t j) -> p n t j", t=2, j=j)
                    b = dst.rearrange("p (n t j) -> p n t j", t=2, j=j)
                    if half is not None and j == COLS // 2:
                        a, b = (x[:, :, :, half * j // 2:(half + 1) * j // 2] for x in (a, b))
                    V.tensor_tensor(b[:, :, 0, :], a[:, :, 0, :], a[:, :, 1, :], ALU.min)
                    end(V.tensor_tensor(b[:, :, 1, :], a[:, :, 0, :], a[:, :, 1, :], ALU.max))
                    return
                a = src.rearrange("p (g d n t j) -> p g d n t j", d=2, n=k // (2 * j), t=2, j=j)
                b = dst.rearrange("p (g d n t j) -> p g d n t j", d=2, n=k // (2 * j), t=2, j=j)
                for d in range(2):
                    low, high = (ALU.min, ALU.max) if d == 0 else (ALU.max, ALU.min)
                    V.tensor_tensor(b[:, :, d, :, 0, :], a[:, :, d, :, 0, :], a[:, :, d, :, 1, :], low)
                    ins = V.tensor_tensor(b[:, :, d, :, 1, :], a[:, :, d, :, 0, :], a[:, :, d, :, 1, :], high)
                end(ins)

            def norm1(c):
                cs = slice(c * CH, (c + 1) * CH)
                if c == 0:
                    dve.wait_ge(s["ln1_std"], NCH + 1)
                    V.reciprocal(std1[:, 1, :], std1[:, 0, :]).then_inc(s["ln1_scale"], 1)
                dve.wait_ge(s["spread_ready"], c + 1)
                if c >= 2:
                    dve.wait_ge(s["conv_done"], c - 1)
                V.tensor_tensor(padded[c % 2][:, :, 1:1 + SIDE, 1:1 + SIDE],
                                centred[:, cs].rearrange("p (b r c) -> p b r c", b=2, r=SIDE),
                                ps_var[:, :].rearrange("p (b r c) -> p b r c", b=2, r=SIDE), ALU.mult) \
                 .then_inc(s["padded_ready"], 1)
                dve.wait_ge(s["padded_ready"], c + 1)

            def round_down(dst, scratch, value, scalar, op):
                link(V.tensor_scalar(scratch, value, scalar, MAGIC, op, ALU.add))
                link(V.tensor_scalar(scratch, scratch, MAGIC, None, ALU.subtract))
                link(V.scalar_tensor_tensor(out=dst, in0=value, scalar=scalar, in1=scratch, op0=op, op1=ALU.is_lt))
                link(V.tensor_tensor(dst, scratch, dst, ALU.subtract))

            def norm2(c):
                cs = slice(c * CH, (c + 1) * CH)
                dve.wait_ge(s["spread_ready"], NCH + c + 1)
                V.tensor_tensor(ln2[:, cs], ln2[:, cs], psum[4 + c % 4][:, :], ALU.mult).then_inc(s["ln2_ready"], 1)
                dve.wait_ge(s["ln2_ready"], c + 1)

            def keep_rows(c):
                dve.wait_ge(s["h_done"], c + 1)
                hp = ps_h[:, 0:CH // P * (2 * HE + 2)].rearrange("p (j n) -> p j n", n=2 * HE + 2)
                for h in range(2):
                    ts = slice(8 * c + h, 8 * c + 8, 2)
                    V.tensor_copy(table[:, ts, 0:HE], hp[:, :, h * HE:(h + 1) * HE])
                    ins = V.tensor_copy(vtok[:, 0, ts], hp[:, :, 2 * HE + h])
                ins.then_inc(s["h_used"], 1)

            def attention_terms():
                dve.wait_ge(s["rows_in"], 16 * 5)
                dve.wait_ge(s["vtok_std"], 1)
                link(V.reciprocal(vtok[:, 0, :], vtok[:, 1, :]))
                link(V.tensor_tensor(table[:, :, 0:HE], table[:, :, 0:HE],
                                     vtok[:, 0, :].rearrange("p (t a) -> p t a", a=1).broadcast_to([P, TILES, HE]), ALU.mult))
                prod = [ex_flat[:, n * TILES * HE:(n + 1) * TILES * HE] for n in range(2)]
                for n in range(2):
                    ins = V.tensor_tensor(prod[n].rearrange("p (t n) -> p t n", n=HE), table[:, :, 0:HE],
                                          rowc[:, n:n + 1, :].broadcast_to([P, TILES, HE]), ALU.mult)
                link(ins)
                V.tensor_reduce(table[:, :, HE:ROW], prod[0].rearrange("p (t h e) -> p t h e", h=HEADS, e=EXP),
                                AX.X, ALU.add)
                V.tensor_reduce(adst[:, :, :], prod[1].rearrange("p (t h e) -> p t h e", h=HEADS, e=EXP),
                                AX.X, ALU.add).then_inc(s["table_ready"], 1)

            def move(n):
                c = EARLY_CHUNKS + n // 2
                if n % 2 == 1 and c < NCH:
                    norm1(c)
                if n % 2 == 0 and n < ROWS_SLOT and EARLY_CHUNKS - 2 + n // 2 < NCH - 1:
                    keep_rows(EARLY_CHUNKS - 2 + n // 2)
                if n == ROWS_SLOT:
                    keep_rows(NCH - 1)
                    dve.wait_ge(s["h_used"], NCH)
                    V.tensor_copy(vtok[:, 1, :], vtok[:, 0, :]).then_inc(s["vtok_ready"], 1)
                if n == ROWS_SLOT + 1:
                    attention_terms()
                if n >= SCALE_SLOT:
                    for c in range((n - SCALE_SLOT) * 2, (n - SCALE_SLOT) * 2 + 2):
                        norm2(c)

            def stage_moved(n, src, dst, k, j, signal=None):
                for half in range(2):
                    last_bank = 4 if half == 1 else 3 if j == COLS // 2 else 2
                    dve.wait_ge(s["banks_moved"], 4 * n + last_bank)
                    stage(src, dst, k, j, signal, half)

            def last_stage(src, dst, k, level):
                for half in range(2):
                    stage(src, dst, k, 1, None, half)
                    hs = slice(half * COLS // 2, (half + 1) * COLS // 2)
                    V.tensor_scalar(dst[:, hs], dst[:, hs], signs[:, level - LOG_COLS:level + 1 - LOG_COLS], None, ALU.mult) \
                     .then_inc(s["keys_out"], 1)

            at, n, stages = 0, 0, 0
            token_stages = [LOG_COLS * (LOG_COLS + 1) // 2 - 3 - CHUNK_STAGES * c for c in reversed(range(EARLY_CHUNKS))]
            for level in range(1, LOG_COLS + 1):
                for bit in range(level - 1, -1, -1):
                    k = None if level == LOG_COLS else 1 << level
                    if level == LOG_COLS and bit == 0:
                        last_stage(keys[at], keys[1 - at], k, level)
                    else:
                        stage(keys[at], keys[1 - at], k, 1 << bit)
                    at = 1 - at
                    stages += 1
                    if stages in token_stages:
                        c = token_stages.index(stages)
                        norm1(c)
                        if c >= 2:
                            keep_rows(c - 2)
            for level in LEVELS_T:
                assert MOVES[n][0] == at and MOVES[n][1] == 1 - at
                move(n)
                n, at = n + 1, 1 - at
                for bit in range(level - LOG_COLS - 1, -1, -1):
                    k = None if level == LOG_EDGES else 1 << (level - LOG_COLS)
                    signal = None if bit else "keys_out"
                    if bit == level - LOG_COLS - 1:
                        stage_moved(n - 1, keys[at], keys[1 - at], k, 1 << bit, signal)
                    elif bit == 0:
                        for half in range(2):
                            stage(keys[at], keys[1 - at], k, 1, signal, half)
                    else:
                        stage(keys[at], keys[1 - at], k, 1 << bit)
                    at = 1 - at
                assert MOVES[n][0] == at and MOVES[n][1] == 1 - at
                move(n)
                n, at = n + 1, 1 - at
                for bit in range(LOG_COLS - 1, -1, -1):
                    if bit == LOG_COLS - 1:
                        stage_moved(n - 1, keys[at], keys[1 - at], None, 1 << bit)
                    elif bit == 0 and level < LOG_EDGES:
                        last_stage(keys[at], keys[1 - at], None, level)
                    else:
                        stage(keys[at], keys[1 - at], None, 1 << bit, None if bit else "sorted_ready")
                    at = 1 - at
            assert at == SORTED
            dve.wait_ge(s["sorted_ready"], 1)

            link(V.tensor_scalar(keys[1 - at][:, :], keys[at][:, :], KEY_END, None, ALU.is_lt, ALU.add,
                                 accum_out=share[:, 1:2]))
            V.tensor_copy(share[:, 0:1], share[:, 1:2]).then_inc(s["counted"], 1)
            V.tensor_copy(share[:, 2:3], signs_i[:, 7:8])
            dve.wait_ge(s["total"], 1)
            link(V.tensor_copy(share[:, 3:4], ps_conv[:, 0:1]))
            V.tensor_scalar(limits[:, 3, :], limits[:, 0, :], share[:, 3:4], None, ALU.is_lt, ALU.add,
                            accum_out=share[:, 5:6])
            link(V.scalar_tensor_tensor(out=limits[:, 2, :], in0=limits[:, 0, :], scalar=share[:, 3:4], in1=limits[:, 1, :],
                                        op0=ALU.is_lt, op1=ALU.mult, accum_out=share[:, 4:5]))
            V.tensor_scalar(share[:, 7:8], share[:, 4:5], float(SHARES[0]), None, ALU.add)
            V.tensor_copy(choice_i[:, :], share[0:1, 5:6]).then_inc(s["choice_ready"], 1)
            dve.wait_ge(s["choice_ready"], 1)
            choice = dve.value_load(choice_i[0:1, 0:1], min_val=0, max_val=len(SHARES) - 1)
            width = srow[:, SROW - 1:SROW]
            own = keys[1 - at]

            def take_share(W):
                col = column[:, 0:W]
                dve.wait_ge(s["shared_in"], 16 * 2)
                own_i = own[:, 0:W].bitcast(I32)
                kept = sources[:, 0:W].bitcast(F32)
                real = same[:, 0:W]
                far = [keys[at][:, 0:W].bitcast(I32), found_flat[:, 0:W].bitcast(I32)]
                moves = found_flat[:, COLS:COLS + W].bitcast(I32)
                for u in range(2):
                    ins = V.tensor_scalar(index[u][:, :], own_i[:, u * TC:(u + 1) * TC], NODES - 1, None, ALU.bitwise_and)
                ins.then_inc(s["early_index"], 1)
                dve.wait_ge(s["neutral_out"], 16)
                dve.wait_ge(s["zeros_out"], 16)
                for u in range(2):
                    dve.wait_ge(s[f"state_out{u}"], 16)
                dve.wait_ge(s["keysort_out"], 16)
                link(V.tensor_scalar(kept, col, share[:, 7:8], None, ALU.is_lt))
                link(V.scalar_tensor_tensor(out=real, in0=own[:, 0:W], scalar=KEY_END, in1=kept,
                                            op0=ALU.is_lt, op1=ALU.mult, accum_out=share[:, 8:9]))
                V.tensor_copy(kept[:, 0:RAWC], real[:, 0:RAWC])
                link(V.tensor_tensor(kept[:, RAWC:W], own[:, RAWC:W], own[:, RAWC - 1:W - 1], ALU.not_equal))
                link(V.tensor_tensor(kept[:, RAWC:W], kept[:, RAWC:W], real[:, RAWC:W], ALU.mult))
                link(V.tensor_tensor_scan(times[:, 0:W], ones[:, 0:1].broadcast_to([P, W]), kept, 0.0, ALU.mult, ALU.add))
                V.tensor_copy(srow[:, SROW - 1:SROW], times[:, W - 1:W]).then_inc(s["width"], 1)
                link(V.scalar_tensor_tensor(out=real, in0=col, scalar=1.0, in1=times[:, 0:W], op0=ALU.add, op1=ALU.subtract))
                link(V.tensor_tensor(far[0], real, kept, ALU.mult))
                f = 0
                for b in range(LOG_COLS):
                    k = 1 << b
                    link(V.tensor_scalar(moves, far[f], k, None, ALU.bitwise_and))
                    V.copy_predicated(own_i[:, 0:W - k], moves[:, k:W], own_i[:, k:W])
                    link(V.scalar_tensor_tensor(out=far[1 - f], in0=moves, scalar=0.0, in1=far[f], op0=ALU.is_equal, op1=ALU.mult))
                    link(V.copy_predicated(far[1 - f][:, 0:W - k], moves[:, k:W], far[f][:, k:W]))
                    f = 1 - f
                dve.wait_ge(s["width_max"], 1)
                link(V.tensor_reduce(pairs_f[:, 3:4], ps_conv[0:1, 128:256], AX.X, ALU.max))
                for n, w in enumerate((PAIRW, TC, TC // 2)):
                    pf = pairs_f[:, n:n + 1]
                    link(V.tensor_scalar(pf, pairs_f[:, 3:4], float(w - 1), 1.0 / w, ALU.add, ALU.mult))
                    link(V.tensor_scalar(pf, pf, (1.0 / w - 1.0) / 2.0, MAGIC, ALU.add, ALU.add))
                    link(V.tensor_scalar(pf, pf, MAGIC, float((1, SLOTS, 2 * SLOTS)[n]), ALU.subtract, ALU.max))
                V.tensor_copy(pairs_i[:, :], pairs_f[:, 0:3]).then_inc(s["pairs_ready"], 1)
                within, behind_v = far[1 - f].bitcast(F32), moves.bitcast(F32)
                link(V.tensor_scalar(sources[:, 0:W], own_i, NODES - 1, None, ALU.bitwise_and))
                if W < COLS:
                    V.memset(sources[:, W:COLS], 0)
                    V.memset(times[:, W:COLS], 0.0)
                    V.memset(same[:, W:COLS], 1.0)
                    V.memset(dests[:, W:COLS], DROPPED)
                for u in range(2, SLOTS):
                    V.tensor_copy(index[u][:, :], sources[:, u * TC:(u + 1) * TC])
                V.tensor_scalar(own_i, own_i, SRC_BITS, (1 << (SRC_BITS + 2)) - 1, ALU.logical_shift_right, ALU.bitwise_and)
                link(V.tensor_scalar(within, col, width, None, ALU.is_lt))
                V.scalar_tensor_tensor(out=real, in0=far[f], scalar=share[:, 8:9], in1=col, op0=ALU.subtract, op1=ALU.add)
                link(V.tensor_scalar(behind_v, within, -DROPPED, DROPPED, ALU.mult, ALU.add))
                link(V.tensor_tensor(real, real, within, ALU.mult))
                V.tensor_tensor(times[:, 0:W - 1], real[:, 1:W], real[:, 0:W - 1], ALU.subtract)
                V.tensor_scalar(times[:, W - 1:W], real[:, W - 1:W], -1.0, None, ALU.mult)
                V.tensor_tensor(dests[:, 0:W], own_i, behind_v, ALU.max).then_inc(s["dests_ready"], 1)
                dve.wait_ge(s["dests_ready"], 1)
                V.tensor_scalar(dfirst_i[:, :], dests[:, 0:1], float(NODES - 1), None, ALU.min).then_inc(s["idx_ready"], 1)
                V.tensor_scalar(srow[:, 0:NSAMP], dests.rearrange("p (a b) -> p a b", b=BLK)[:, 1:NBLK, 0], 0.0, None, ALU.add)
                V.tensor_scalar(srow[:, NSAMP:NSAMP + 1], share[:, 2:3], float(COLS), None, ALU.mult)
                V.tensor_copy(border[:, 3:4], dests[:, 0:1])
                V.tensor_scalar(share[:, 9:10], share[:, 2:3], 0.0, None, ALU.is_gt)
                link(V.tensor_scalar(prev[:, 0:1], prev[:, 0:1], SRC_BITS, (1 << (SRC_BITS + 2)) - 1,
                                     ALU.logical_shift_right, ALU.bitwise_and))
                V.tensor_copy(border[:, 1:2], prev[:, 0:1])
                V.tensor_scalar(border[:, 2:3], border[:, 3:4], -2.0 * DROPPED, None, ALU.add)
                link(V.tensor_tensor(flags[:, 0:1], border[:, 3:4], prev[:, 0:1], ALU.is_equal))
                link(V.tensor_tensor(flags[:, 0:1], flags[:, 0:1], share[:, 9:10], ALU.mult))
                V.tensor_copy(border[:, 0:1], flags[:, 0:1]).then_inc(s["border_ready"], 1)
                link(V.tensor_tensor(same[:, 1:W], dests[:, 1:W], dests[:, 0:W - 1], ALU.is_equal))
                V.memset(same[:, 0:1], 1.0)
                link(V.scalar_tensor_tensor(out=same[:, 1:W], in0=behind_v[:, 1:W], scalar=0.0, in1=same[:, 1:W],
                                            op0=ALU.is_gt, op1=ALU.max))

            begun = done[0]
            with dve.If(choice < NARROW + 1):
                take_share(SHARES[NARROW])
            with dve.Else():
                done[0] = begun
                take_share(COLS)
            dve.wait_ge(s["border_moved"], 1)
            V.tensor_copy(flags[:, 2:3], ps_conv[:, 0:1])
            V.tensor_tensor(flags[:, 1:2], border[:, 3:4], ps_conv[:, 1:2], ALU.is_equal)
            link(V.tensor_scalar(share[:, 10:11], ps_conv[:, 2:3], 2.0 * DROPPED, None, ALU.add))
            link(V.tensor_tensor(cidx_f[:, :], flags[:, 1:2], flags[:, 2:3], ALU.mult))
            link(V.tensor_scalar(cidx_f[:, :], cidx_f[:, :], -1.0, 1.0, ALU.mult, ALU.add))
            link(V.tensor_tensor(cidx_f[:, :], cidx_f[:, :], flags[:, 0:1], ALU.mult))
            link(V.tensor_scalar(cidx_f[:, :], cidx_f[:, :], -float(FAR), float(FAR), ALU.mult, ALU.add))
            link(V.tensor_tensor(cidx_f[:, :], cidx_f[:, :], border[:, 3:4], ALU.add))
            link(V.tensor_copy(cidx_i[:, :], cidx_f[:, :]))

            V.memset(border[0:1, 3:4], -1.0)
            link(V.tensor_copy(group_f[:, 1, :], group_i[:, :]))
            V.tensor_tensor(group_f[:, 0, :], border[:, 3:4].broadcast_to([P, NGROUP]), group_f[:, 1, :], ALU.subtract)
            link(V.tensor_scalar(share[:, 11:12], share[:, 10:11], 0.0, None, ALU.add))
            ins = V.tensor_tensor(group_f[:, 1, :], share[:, 11:12].broadcast_to([P, NGROUP]), group_f[:, 1, :], ALU.subtract)
            ins.then_inc(s["border_used"], 1)
            dve.wait_ge(s["border_used"], 1)
            above = found_flat[:, 0:GROUP * P]

            def count_samples(c):
                tiles = GROUP if c < NGROUP - 1 else 1
                ts = slice(c * GROUP, c * GROUP + tiles)
                dve.wait_ge(s["sampled"], c + 1)
                ps = psum[4 + c % 4][:, 0:tiles * SROW].rearrange("p (t n) -> p t n", n=SROW)
                cmp = found_flat[:, 2048:2048 + tiles * NSAMP].rearrange("p (t n) -> p t n", n=NSAMP)
                V.tensor_copy(found_row[:, 0, ts], ps[:, :, NSAMP])
                V.tensor_copy(found_row[:, 1, ts], ps[:, :, NSAMP + 1])
                V.tensor_tensor(cmp, ps[:, :, 0:NSAMP],
                                targets[:, ts].rearrange("p (t a) -> p t a", a=1).broadcast_to([P, tiles, NSAMP]),
                                ALU.is_lt).then_inc(s["sampled_used"], 1)
                dve.wait_ge(s["sampled_used"], c + 1)
                link(V.tensor_reduce(block_f[:, ts], cmp, AX.X, ALU.add))

            for c in range(NGROUP):
                n = GROUP * P if c < NGROUP - 1 else P
                if c >= 2:
                    dve.wait_ge(s["sampled"], c - 1)
                link(V.tensor_scalar(above[:, 0:n], nodes1k[:, 0:n], group_f[:, 1, c:c + 1], None, ALU.is_gt))
                V.scalar_tensor_tensor(out=onehot[c % 2][:, 0:n], in0=nodes1k[:, 0:n], scalar=group_f[:, 0, c:c + 1],
                                       in1=above[:, 0:n], op0=ALU.is_gt, op1=ALU.subtract).then_inc(s["onehot"], 1)
                dve.wait_ge(s["onehot"], c + 1)
                if c >= 1:
                    count_samples(c - 1)
            count_samples(NGROUP - 1)
            link(V.tensor_scalar(place[:, :], found_row[:, 0, :], 1.0 / BLK, None, ALU.mult))
            link(V.tensor_tensor(place[:, :], place[:, :], block_f[:, :], ALU.add))
            V.tensor_copy(block_i[:, :], place[:, :]).then_inc(s["block_ready"], 1)
            dve.wait_ge(s["block_ready"], 1)
            for n, (a, b) in enumerate(((0, FOUND_HALF), (FOUND_HALF, TILES + 1))):
                dve.wait_ge(s[f"found_in{n}"], 16 * (b - a))
                link(V.tensor_tensor(found[:, a:b, :], found[:, a:b, :],
                                     targets[:, a:b].rearrange("p (t a) -> p t a", a=1).broadcast_to([P, b - a, BLK]), ALU.is_lt))
                link(V.tensor_reduce(place[:, a:b], found[:, a:b, :], AX.X, ALU.add))
            link(V.scalar_tensor_tensor(out=place[:, :], in0=block_f[:, :], scalar=float(BLK), in1=place[:, :],
                                        op0=ALU.mult, op1=ALU.add))
            V.tensor_tensor(first[:, :], place[:, :], found_row[:, 0, :], ALU.add).then_inc(s["first_ready"], 1)
            dve.wait_ge(s["ends_ps"], 1)
            end = ps_h[:, 0:TILES]
            link(V.tensor_tensor(empty[:, :], end, first[:, 0:TILES], ALU.is_equal))
            V.tensor_scalar(void[:, :].rearrange("p (q h) -> p h q", h=2), empty[:, :].rearrange("p (h q) -> p h q", h=2),
                            -BIG, None, ALU.mult)
            V.scalar_tensor_tensor(out=bad[:, 0, :], in0=place[:, 0:TILES], scalar=0.0, in1=empty[:, :],
                                   op0=ALU.is_equal, op1=ALU.max)
            link(V.tensor_tensor(bad[:, 1, :], place[:, 0:TILES], found_row[:, 1, 0:TILES], ALU.is_equal))
            link(V.tensor_tensor(bad[:, 0, :], bad[:, 0, :], bad[:, 1, :], ALU.max))
            V.scalar_tensor_tensor(out=scat_f[:, 0, :], in0=bad[:, 0, :], scalar=float(FAR), in1=first[:, 0:TILES],
                                   op0=ALU.mult, op1=ALU.add)
            link(V.tensor_scalar(scat_f[:, 1, :], end, -1.0, 0.0, ALU.add, ALU.max))
            V.tensor_copy(scat_i[:, :, :], scat_f[:, :, :]).then_inc(s["places_ready"], 1)

            dve.wait_ge(s["dfirst_in"], 16)
            V.tensor_copy(adst_e[1][:, :, TC - 1], dfirst[:, :])
            V.memset(top_e[1][:, :, TC:TC + 1], 0.0)
            V.memset(state[1][:, TC - 1, HEADS:ST], 0.0)
            link(V.memset(state[1][:, TC - 1, 0:HEADS], -BIG))
            dve.sem_inc(s["state_ready"], 1)

            STEPS = 8
            pairs = dve.value_load(pairs_i[0:1, 0:1], min_val=1, max_val=NPAIR)
            chunks = dve.value_load(pairs_i[0:1, 1:2], min_val=1, max_val=2 * NPAIR)
            half_chunks = dve.value_load(pairs_i[0:1, 2:3], min_val=1, max_val=4 * NPAIR)

            def edge_chunk(i, v):
                u, w = v % 2, v // 2
                off = i * QUADW + v * TC
                step = [0]

                def after(ins):
                    step[0] += 1
                    ins.then_inc(s["edge_step"], 1)
                    dve.wait_ge(s["edge_step"], i * (SLOTS * STEPS) + (v * STEPS + step[0]))

                g, st, last = gathered[v], state[u], 1 - u
                ad, top = adst_e[u], top_e[u]
                sm, mult = same[:, bass.ds(off, TC)], times[:, bass.ds(off, TC)]

                def by_head(row):
                    return row.rearrange("p (a t) -> p a t", a=1).broadcast_to([P, HEADS, TC])

                dve.wait_ge(s[f"gath{v}"], i * (8 * TC) + 8 * TC)
                with dve.If(i * (2 * SLOTS) + (2 * v + 1) < half_chunks):
                    dve.wait_ge(s[f"rest{v}"], i * (8 * TC) + 8 * TC)
                    dve.sem_inc(s["rows_taken"], 1)
                with dve.Else():
                    pass
                dve.wait_ge(s[f"head_in{u}"], i * 32 + (w * 16 + 16))
                dve.wait_ge(s[f"state_out{u}"], i * 32 + (w * 16 + 16))
                dve.wait_ge(s["state_ready"], i * SLOTS + (v + 1))
                V.tensor_scalar(fresh, sm, -1.0, BIG, ALU.add, ALU.mult)
                after(V.tensor_scalar(behind, mult, 0.0, -BIG, ALU.is_equal, ALU.mult))
                after(V.tensor_tensor(masked, g[:, :, HE:ROW].rearrange("p t h -> p h t"), by_head(behind), ALU.add))
                for h in range(HEADS):
                    V.tensor_tensor_scan(st[:, :, h], fresh, masked[:, h, :], state[last][:, TC - 1, h:h + 1],
                                         ALU.add, ALU.max)
                    ins = V.tensor_tensor_scan(ad[:, h, :], sm, headrow[u][:, :, h], adst_e[last][:, h, TC - 1:TC],
                                               ALU.mult, ALU.add)
                V.tensor_copy(top[:, :, 0:1], top_e[last][:, :, TC:TC + 1])
                V.tensor_copy(index[v][:, :], sources[:, bass.ds(off + QUADW, TC)])
                after(ins)
                V.tensor_tensor(raw[:, 0], masked, ad, ALU.add)
                after(V.tensor_tensor(raw[:, 1], st[:, :, 0:HEADS].rearrange("p t h -> p h t"), ad, ALU.add))
                V.scalar_tensor_tensor(out=raw[:, 0], in0=raw[:, 0], scalar=SLOPE, in1=raw[:, 0], op0=ALU.mult, op1=ALU.max)
                after(V.scalar_tensor_tensor(out=top[:, :, 1:TC + 1], in0=raw[:, 1], scalar=SLOPE, in1=raw[:, 1],
                                             op0=ALU.mult, op1=ALU.max))
                V.tensor_tensor(diff[:, 0], raw[:, 0], top[:, :, 1:TC + 1], ALU.subtract)
                after(V.tensor_tensor(diff[:, 1], top[:, :, 0:TC], top[:, :, 1:TC + 1], ALU.subtract))
                V.tensor_scalar(diff[:, 1], diff[:, 1], 0.0, None, ALU.min).then_inc(s["diffs_ready"], 1)
                dve.wait_ge(s["weights_ready"], i * SLOTS + (v + 1))
                V.tensor_tensor(diff[:, 0], weight[:, 1], by_head(sm), ALU.mult)
                after(V.tensor_tensor(raw[:, 0], weight[:, 0], by_head(mult), ALU.mult))
                for h in range(HEADS):
                    ins = V.tensor_tensor(part[:, h], g[:, :, h * EXP:(h + 1) * EXP].rearrange("p t e -> p e t"),
                                          raw[:, 0, h:h + 1, :].broadcast_to([P, EXP, TC]), ALU.mult)
                after(ins)
                for h in range(HEADS):
                    c = HEADS + h
                    V.tensor_tensor_scan(st[:, :, c], diff[:, 0, h], raw[:, 0, h], state[last][:, TC - 1, c:c + 1],
                                         ALU.mult, ALU.add)
                    for e in range(EXP):
                        c = 2 * HEADS + h * EXP + e
                        ins = V.tensor_tensor_scan(st[:, :, c], diff[:, 0, h], part[:, h, e],
                                                   state[last][:, TC - 1, c:c + 1], ALU.mult, ALU.add)
                ins.then_inc(s["state_ready"], 1)
                assert step[0] == STEPS

            with dve.Fori(0, NQUAD) as i:
                for w in range(2):
                    with dve.If(i * 2 + w < pairs):
                        edge_chunk(i, w * 2)
                        with dve.If(i * SLOTS + (w * 2 + 1) < chunks):
                            edge_chunk(i, w * 2 + 1)
                        with dve.Else():
                            dve.wait_ge(s["state_out1"], i * 32 + (w * 16 + 16))
                            dve.wait_ge(s["state_ready"], i * SLOTS + (w * 2 + 2))
                            V.tensor_copy(adst_e[1][:, :, TC - 1], adst_e[0][:, :, TC - 1])
                            V.tensor_copy(state[1][:, TC - 1, :], state[0][:, TC - 1, :]).then_inc(s["state_ready"], 1)
                    with dve.Else():
                        pass
            dve.wait_ge(s["state_ready"], pairs * 2 + 1)

            lastrow = state[1][:, TC - 1, :]
            cg = [cx[:, n, :].rearrange("p (h k) -> p h k", h=HEADS) for n in range(4)]
            V.tensor_copy(cg[0], lastrow[:, 0:HEADS].rearrange("p (h a) -> p h a", a=1).broadcast_to([P, HEADS, 1 + EXP]))
            V.tensor_copy(cg[1][:, :, 0:1], lastrow[:, HEADS:2 * HEADS].rearrange("p (h a) -> p h a", a=1))
            V.tensor_copy(cg[1][:, :, 1:1 + EXP], lastrow[:, 2 * HEADS:ST].rearrange("p (h e) -> p h e", h=HEADS))
            V.tensor_copy(cg[2], adst_e[1][:, :, TC - 1:TC].broadcast_to([P, HEADS, 1 + EXP]))
            link(V.tensor_tensor(cidx_f[:, :], flags[:, 0:1], flags[:, 1:2], ALU.mult))
            V.tensor_copy(cx[:, 3, :], cidx_f[:, 0:1].broadcast_to([P, CHN])).then_inc(s["carry_x"], 1)
            dve.wait_ge(s["carry_t"], 1)
            link(V.tensor_copy(ct[:, 0:4, :], ps_centre[0:CHN, :].rearrange("p (a b) -> p a b", a=4)))
            M_, V_, D_, C_ = (ct[:, n, :] for n in range(4))
            link(V.tensor_scalar(ct[:, 4, :], C_, -1.0, BIG, ALU.add, ALU.mult))
            link(V.tensor_tensor_scan(ct[:, 8, :], ct[:, 4, :], M_, -BIG, ALU.add, ALU.max))
            V.tensor_tensor(ct[:, 9, :], ct[:, 8, :], D_, ALU.add)
            link(V.tensor_tensor(ct[:, 10, :], M_, D_, ALU.add))
            V.scalar_tensor_tensor(out=ct[:, 9, :], in0=ct[:, 9, :], scalar=SLOPE, in1=ct[:, 9, :], op0=ALU.mult, op1=ALU.max)
            link(V.scalar_tensor_tensor(out=ct[:, 10, :], in0=ct[:, 10, :], scalar=SLOPE, in1=ct[:, 10, :], op0=ALU.mult, op1=ALU.max))
            V.memset(ct[:, 5, 0:1], 0.0)
            V.tensor_tensor(ct[:, 4, :], ct[:, 10, :], ct[:, 9, :], ALU.subtract)
            link(V.tensor_tensor(ct[:, 5, 1:P], ct[:, 9, 0:P - 1], ct[:, 9, 1:P], ALU.subtract))
            V.tensor_scalar(ct[:, 5, :], ct[:, 5, :], 0.0, None, ALU.min).then_inc(s["carry_diff"], 1)
            dve.wait_ge(s["carry_w"], 1)
            V.tensor_tensor(ct[:, 7, :], ct[:, 7, :], C_, ALU.mult)
            link(V.tensor_tensor(ct[:, 6, :], ct[:, 6, :], V_, ALU.mult))
            link(V.tensor_tensor_scan(ct[:, 9, :], ct[:, 7, :], ct[:, 6, :], 0.0, ALU.mult, ALU.add))
            V.memset(ct[:, 10, 0:1], -BIG)
            V.memset(ct[:, 11, 0:1], 0.0)
            V.tensor_copy(ct[:, 10, 1:P], ct[:, 8, 0:P - 1])
            V.tensor_copy(ct[:, 11, 1:P], ct[:, 9, 0:P - 1]).then_inc(s["carry_c"], 1)
            dve.wait_ge(s["carry_b"], 1)
            bm = ps_var[:, 0:CHN].rearrange("p (h k) -> p h k", h=HEADS)
            bv = ps_var[:, 32:32 + CHN].rearrange("p (h k) -> p h k", h=HEADS)
            V.tensor_copy(cback[:, 0:HEADS].rearrange("p (h a) -> p h a", a=1), bm[:, :, 0:1])
            V.tensor_copy(cback[:, HEADS:2 * HEADS].rearrange("p (h a) -> p h a", a=1), bv[:, :, 0:1])
            V.tensor_copy(cback[:, 2 * HEADS:ST].rearrange("p (h e) -> p h e", h=HEADS), bv[:, :, 1:1 + EXP]) \
             .then_inc(s["carry_row"], 1)

            def nodes(k):
                ts = slice(k * PAIRS, (k + 1) * PAIRS)
                last, before, own_rows, own_dst = (x[:, ts, :] for x in (last_rows, carried, table, adst))
                nt_, nsm_, n16_ = [x[:, ts, :] for x in nt], [x[:, ts] for x in nsm], [x[:, ts, :, :] for x in n16]
                tri_, tri2_ = (x[:, :, ts, :] for x in (tri, tri2))
                dve.wait_ge(s[f"last_in{k}"], 16 * PAIRS)
                dve.wait_ge(s["carry_in"], 32)
                ec = void[:, ts].rearrange("p (t a) -> p t a", a=1).broadcast_to([P, PAIRS, HEADS])
                link(V.tensor_tensor(nt_[0], last[:, :, 0:HEADS], ec, ALU.add))
                link(V.tensor_tensor(nt_[1], nt_[0], before[:, :, 0:HEADS], ALU.max))
                link(V.tensor_tensor(nt_[1], nt_[1], own_rows[:, :, HE:ROW], ALU.max))
                V.tensor_tensor(nt_[2], nt_[1], own_dst, ALU.add)
                V.tensor_tensor(tri_[:, 0], nt_[0], own_dst, ALU.add)
                V.tensor_tensor(tri_[:, 1], before[:, :, 0:HEADS], own_dst, ALU.add)
                link(V.tensor_tensor(tri_[:, 2], own_rows[:, :, HE:ROW], own_dst, ALU.add))
                V.scalar_tensor_tensor(out=nt_[2], in0=nt_[2], scalar=SLOPE, in1=nt_[2], op0=ALU.mult, op1=ALU.max)
                link(V.scalar_tensor_tensor(out=tri_, in0=tri_, scalar=SLOPE, in1=tri_, op0=ALU.mult, op1=ALU.max))
                V.tensor_tensor(tri_.rearrange("p a t h -> p a (t h)"), tri_.rearrange("p a t h -> p a (t h)"),
                                nt_[2].rearrange("p (a t) h -> p a (t h)", a=1).broadcast_to([P, 3, NH4 // 2]), ALU.subtract) \
                 .then_inc(s["node_diff"], 1)
                dve.wait_ge(s["node_w"], k + 1)

                def spread(x):
                    return x.rearrange("p t (h a) -> p t h a", a=1).broadcast_to([P, PAIRS, HEADS, EXP])

                V.tensor_tensor(nt_[0], last[:, :, HEADS:2 * HEADS], tri2_[:, 0], ALU.mult)
                V.tensor_tensor(nt_[1], before[:, :, HEADS:2 * HEADS], tri2_[:, 1], ALU.mult)
                V.tensor_tensor(n16_[0], last[:, :, 2 * HEADS:ST].rearrange("p t (h e) -> p t h e", h=HEADS), spread(tri2_[:, 0]), ALU.mult)
                V.tensor_tensor(n16_[1], before[:, :, 2 * HEADS:ST].rearrange("p t (h e) -> p t h e", h=HEADS), spread(tri2_[:, 1]), ALU.mult)
                link(V.tensor_tensor(n16_[2], own_rows[:, :, 0:HE].rearrange("p t (h e) -> p t h e", h=HEADS), spread(tri2_[:, 2]), ALU.mult))
                V.tensor_tensor(nt_[0], nt_[0], nt_[1], ALU.add)
                link(V.tensor_tensor(n16_[0], n16_[0], n16_[1], ALU.add))
                V.tensor_tensor(nt_[0], nt_[0], tri2_[:, 2], ALU.add)
                link(V.tensor_tensor(n16_[0], n16_[0], n16_[2], ALU.add))
                link(V.tensor_scalar(nt_[0], nt_[0], 1e-16, None, ALU.add))
                link(V.reciprocal(nt_[1], nt_[0]))
                link(V.tensor_tensor(n16_[0], n16_[0], spread(nt_[1]), ALU.mult))
                flat = [x.rearrange("p t h e -> p t (h e)") for x in n16_]

                def per_row(n):
                    return rowc[:, n:n + 1, :].broadcast_to([P, PAIRS, HE])

                def per_node(x):
                    return x.rearrange("p (t a) -> p t a", a=1).broadcast_to([P, PAIRS, HE])

                link(V.tensor_tensor(flat[0], flat[0], per_row(2), ALU.add))
                link(V.tensor_reduce(nsm_[0], flat[0], AX.X, ALU.add))
                link(V.tensor_scalar(nsm_[0], nsm_[0], 1.0 / HE, None, ALU.mult))
                link(V.tensor_tensor(flat[0], flat[0], per_node(nsm_[0]), ALU.subtract))
                link(V.tensor_tensor(flat[1], flat[0], flat[0], ALU.mult))
                V.tensor_reduce(nsm_[0], flat[1], AX.X, ALU.add).then_inc(s["node_var"], 1)
                dve.wait_ge(s["node_std"], k + 1)
                link(V.reciprocal(nsm_[2], nsm_[1]))
                link(V.tensor_tensor(flat[0], flat[0], per_node(nsm_[2]), ALU.mult))
                link(V.tensor_tensor(flat[0], flat[0], per_row(3), ALU.mult))
                link(V.tensor_tensor(flat[0], flat[0], per_row(4), ALU.add))
                link(V.tensor_reduce(nt_[3], n16_[0].rearrange("p t h e -> p t e h"), AX.X, ALU.add))
                link(V.tensor_scalar(nt_[3], nt_[3], 1.0 / HEADS, None, ALU.mult))
                link(V.memset(nt_[6], 0.0))
                for a in range(EXP):
                    for b in range(a + 1, EXP):
                        link(V.tensor_tensor(nsm_[3], nt_[3][:, :, b], nt_[3][:, :, a], ALU.is_gt))
                        V.tensor_tensor(nt_[6][:, :, a], nt_[6][:, :, a], nsm_[3], ALU.add)
                        link(V.tensor_scalar(nsm_[4], nsm_[3], -1.0, 1.0, ALU.mult, ALU.add))
                        link(V.tensor_tensor(nt_[6][:, :, b], nt_[6][:, :, b], nsm_[4], ALU.add))
                V.tensor_scalar(nt_[6], nt_[6], 2.0, None, ALU.is_lt)
                link(V.tensor_reduce(nsm_[5], nt_[3], AX.X, ALU.max))

                def per_four(x):
                    return x.rearrange("p (t a) -> p t a", a=1).broadcast_to([P, PAIRS, EXP])

                V.tensor_tensor(nt_[4], nt_[3], per_four(nsm_[5]), ALU.subtract).then_inc(s["top_ready"], 1)
                dve.wait_ge(s["top_exp"], k + 1)
                link(V.tensor_tensor(nt_[5], nt_[5], nt_[6], ALU.mult))
                link(V.tensor_reduce(nsm_[6], nt_[5], AX.X, ALU.add))
                link(V.reciprocal(nsm_[7], nsm_[6]))
                link(V.tensor_tensor(nt_[5], nt_[5], per_four(nsm_[7]), ALU.mult))
                link(V.tensor_copy(gates[:, :, k * PAIRS // 2:(k + 1) * PAIRS // 2, :].rearrange("p e a h -> p (a h) e"), nt_[5]))

            def finish(c):
                dve.wait_ge(s["out_ps"], c + 1)
                cs = slice(c * CH, (c + 1) * CH)
                V.tensor_tensor(x_sb[:, cs], x_sb[:, cs], psum[c % 2][:, :], ALU.add).then_inc(s["final"], 1)

            for c in range(NCH):
                if c % (NCH // 2) == 0:
                    nodes(c // (NCH // 2))
                if c == 0:
                    dve.wait_ge(s["ex_ready"], 4 * NCH)
                for e in range(EXP):
                    x = experts[:, 4 * c:4 * c + 4, e, :].rearrange("p a (h n) -> p a h n", h=2)
                    g = gates[:, e, 4 * c:4 * c + 4, :].rearrange("p a (h n) -> p a h n", n=1).broadcast_to([P, 4, 2, C])
                    ins = V.tensor_tensor(x, x, g, ALU.mult)
                ins.then_inc(s["gated"], 1)
                if c >= 1:
                    finish(c - 1)
            finish(NCH - 1)
    return nc


def kernel(**inputs):
    import numpy as np
    import concourse.bacc as bacc
    from concourse.bass_utils import run_bass_kernel_spmd

    nc = bacc.Bacc("TRN2", target_bir_lowering=False, num_devices=1)
    arrays, args = {}, {}
    for name, value in inputs.items():
        a = np.asarray(value)
        if name == "L0_conv_pad_fill":
            a = a.reshape(1).view(np.int64)
            short = "pad"
        else:
            short = name.replace("L0_conv_", "").replace("L0_ffn_", "")
        a = np.ascontiguousarray(a)
        arrays["in_" + short] = a
        args[short] = nc.dram_tensor("in_" + short, a.shape, mybir.dt.from_np(a.dtype), kind="ExternalInput").ap()
    out = nc.dram_tensor("out", (B, C, SIDE, SIDE), F32, kind="ExternalOutput").ap()
    build(nc, args, out)
    return run_bass_kernel_spmd(nc, [arrays], core_ids=[0]).results[0]["out"]
```
